# Optimizing a Trainium2 kernel written in Bass

```python
import numpy as np
import jax
import jax.numpy as jnp

def _softmax(x, axis=-1):
    return jax.nn.softmax(x, axis=axis)

def _gelu(x):
    return jax.nn.gelu(x, approximate=True)

def _silu(x):
    return jax.nn.silu(x)

def _sigmoid(x):
    return jax.nn.sigmoid(x)

def _layernorm(x, axis=-1, eps=1e-05):
    m = jnp.mean(x, axis=axis, keepdims=True)
    v = jnp.var(x, axis=axis, keepdims=True)
    return (x - m) / jnp.sqrt(v + eps)

def _scatter_add(tgt, idx, src, axis=0):
    return tgt.at[idx].add(src)

def _segment_sum(src, seg, n):
    return jax.ops.segment_sum(src, seg, n)
kernel_name = 'mk_seq_preln_d4_jaxref_r8_3803b1'

def setup_inputs(seed: int=0):
    np.random.seed(seed)
    _w = jnp.asarray

    def _L0_attn_setup():
        import jax, jax.numpy as jnp
        import numpy as np
        import math
        D_MODEL = 512
        NUM_HEADS = 32
        NUM_KV_HEADS = 8
        HEAD_DIM = D_MODEL // NUM_HEADS
        GROUP = NUM_HEADS // NUM_KV_HEADS
        SEQ_LEN = 256
        BATCH = 2
        ROPE_THETA = 10000.0

        def apply_rope(x, start_pos=0):
            b, h, s, hd = x.shape
            inv_freq = 1.0 / ROPE_THETA ** (jnp.arange(0, hd, 2, dtype=jnp.float32) / hd)
            pos = jnp.arange(start_pos, start_pos + s, dtype=jnp.float32)
            ang = pos[:, None] * inv_freq[None, :]
            cos = jnp.cos(ang).astype(x.dtype)
            sin = jnp.sin(ang).astype(x.dtype)
            xr = x[..., 0::2]
            xi = x[..., 1::2]
            out_r = xr * cos - xi * sin
            out_i = xr * sin + xi * cos
            return jnp.stack([out_r, out_i], axis=-1).reshape(b, h, s, hd)
        key = jax.random.key(seed)
        ks = jax.random.split(key, 5)
        qkv_dim = HEAD_DIM * (NUM_HEADS + 2 * NUM_KV_HEADS)
        scale = 1.0 / math.sqrt(D_MODEL)
        return {'x': jax.random.normal(ks[0], (BATCH, SEQ_LEN, D_MODEL), jnp.float32), 'w_qkv': jax.random.normal(ks[1], (qkv_dim, D_MODEL), jnp.float32) * scale, 'b_qkv': jax.random.normal(ks[2], (qkv_dim,), jnp.float32) * 0.01, 'w_o': jax.random.normal(ks[3], (D_MODEL, D_MODEL), jnp.float32) * scale, 'b_o': jax.random.normal(ks[4], (D_MODEL,), jnp.float32) * 0.01}
    _L0_attn_in = _L0_attn_setup()

    def _L0_ffn_setup():
        import jax, jax.numpy as jnp
        import numpy as np
        IMAGE_START_POS = 34
        Q_START = IMAGE_START_POS + 72 + 1
        Q_END = -1
        LORA_ALPHA = 32
        LORA_RANK = 16
        SCALING = LORA_ALPHA / LORA_RANK
        key = jax.random.key(seed)
        ks = jax.random.split(key, 7)
        B_, S, D, O, E, R = (4, 256, 512, 512, 8, LORA_RANK)
        s = 0.02
        return {'x': jax.random.normal(ks[0], (B_, S, D), jnp.float32), 'W': jax.random.normal(ks[1], (O, D), jnp.float32) * s, 'b': jax.random.normal(ks[2], (O,), jnp.float32) * s, 'A': jax.random.normal(ks[3], (E, R, D), jnp.float32) * s, 'B': jax.random.normal(ks[4], (E, O, R), jnp.float32) * s, 'router_W': jax.random.normal(ks[5], (E, D), jnp.float32) * s, 'router_b': jax.random.normal(ks[6], (E,), jnp.float32) * s}
    _L0_ffn_in = _L0_ffn_setup()

    def _L1_attn_setup():
        import jax, jax.numpy as jnp
        import numpy as np
        B, N, HID = (1, 256, 512)
        H, KVH, D, W = (32, 8, 128, 64)
        THETA = 10000.0
        GATE_NORM = 16.0

        def rope(x, pos):
            half = jnp.arange(D // 2, dtype=jnp.float32)
            inv = 1.0 / THETA ** (2.0 * half / D)
            fr = pos[:, None].astype(jnp.float32) * inv[None, :]
            emb = jnp.concatenate([fr, fr], axis=-1)
            cos, sin = (jnp.cos(emb)[None, None], jnp.sin(emb)[None, None])
            x1, x2 = jnp.split(x, 2, axis=-1)
            rot = jnp.concatenate([-x2, x1], axis=-1)
            return x * cos + rot * sin

        def gla_scan(q, k, v, g):
            qt, kt, vt, gt = (jnp.moveaxis(t, 2, 0) for t in (q, k, v, g))
            b, h = (q.shape[0], q.shape[1])
            S0 = jnp.zeros((b, h, D, D), jnp.float32)

            def step(S, x):
                q_t, k_t, v_t, g_t = x
                S = S * jnp.exp(g_t)[..., None] + k_t[..., None] * v_t[..., None, :]
                return (S, jnp.einsum('bhk,bhkv->bhv', q_t, S))
            _, o = jax.lax.scan(step, S0, (qt, kt, vt, gt))
            return jnp.moveaxis(o, 0, 2)

        def sliding_window_attn(q, k, v):
            b, h, n, d = q.shape
            nb = n // W
            qb = q.reshape(b, h, nb, W, d)

            def two_blocks(x):
                xb = x.reshape(b, h, nb, W, d)
                prev = jnp.concatenate([jnp.zeros_like(xb[:, :, :1]), xb[:, :, :-1]], axis=2)
                return jnp.concatenate([prev, xb], axis=3)
            kb, vb = (two_blocks(k), two_blocks(v))
            scores = jnp.einsum('bhnqd,bhnkd->bhnqk', qb, kb) / jnp.sqrt(jnp.float32(d))
            a = jnp.arange(W)[:, None]
            c = jnp.arange(2 * W)[None, :]
            rel = a + W - c
            base = (rel >= 0) & (rel <= W)
            blk = jnp.arange(nb)[:, None, None]
            keypos = (blk - 1) * W + c[None]
            mask = base[None] & (keypos >= 0)
            scores = jnp.where(mask[None, None], scores, -jnp.inf)
            p = jax.nn.softmax(scores, axis=-1)
            ob = jnp.einsum('bhnqk,bhnkd->bhnqd', p, vb)
            return ob.reshape(b, h, n, d)
        key = jax.random.key(seed)
        ks = jax.random.split(key, 5)
        s = 0.02
        return {'hidden_states': jax.random.normal(ks[0], (B, N, HID), jnp.float32), 'Wq': jax.random.normal(ks[1], (HID, H * D), jnp.float32) * s, 'Wk': jax.random.normal(ks[2], (HID, KVH * D), jnp.float32) * s, 'Wv': jax.random.normal(ks[3], (HID, KVH * D), jnp.float32) * s, 'Wo': jax.random.normal(ks[4], (H * D, HID), jnp.float32) * s}
    _L1_attn_in = _L1_attn_setup()

    def _L1_ffn_setup():
        import jax, jax.numpy as jnp
        import numpy as np
        D_MODEL = 512
        D_HIDDEN = 1376
        RANK = 16
        BATCH, SEQ = (2, 256)

        def _matmul_lora(x, w, a, b, scale=1.0):
            out = jnp.einsum('bsd,hd->bsh', x, w)
            out = out + jnp.einsum('bsr,hr->bsh', jnp.einsum('bsd,rd->bsr', x, a), b) * scale
            return out
        key = jax.random.key(seed)
        ks = jax.random.split(key, 10)
        s = 0.02
        return {'x': jax.random.normal(ks[0], (BATCH, SEQ, D_MODEL), jnp.float32), 'gate_w': jax.random.normal(ks[1], (D_HIDDEN, D_MODEL), jnp.float32) * s, 'up_w': jax.random.normal(ks[2], (D_HIDDEN, D_MODEL), jnp.float32) * s, 'down_w': jax.random.normal(ks[3], (D_MODEL, D_HIDDEN), jnp.float32) * s, 'gate_a': jax.random.normal(ks[4], (RANK, D_MODEL), jnp.float32) * s, 'gate_b': jax.random.normal(ks[5], (D_HIDDEN, RANK), jnp.float32) * s, 'up_a': jax.random.normal(ks[6], (RANK, D_MODEL), jnp.float32) * s, 'up_b': jax.random.normal(ks[7], (D_HIDDEN, RANK), jnp.float32) * s, 'down_a': jax.random.normal(ks[8], (RANK, D_HIDDEN), jnp.float32) * s, 'down_b': jax.random.normal(ks[9], (D_MODEL, RANK), jnp.float32) * s}
    _L1_ffn_in = _L1_ffn_setup()

    def _L2_attn_setup():
        import jax, jax.numpy as jnp
        import numpy as np
        HIDDEN = 512
        NUM_HEADS = 32
        HEAD_DIM = HIDDEN // NUM_HEADS
        B, S = (2, 128)

        def _alibi_slopes(n):
            start = 2.0 ** (-2.0 ** (-(np.log2(n) - 3)))
            return np.array([start ** (i + 1) for i in range(n)], dtype=np.float32)
        key = jax.random.key(seed)
        k1, k2, k3, k4 = jax.random.split(key, 4)
        hidden_states = jax.random.normal(k1, (B, S, HIDDEN), jnp.float32)
        Wq = jax.random.normal(k2, (HIDDEN, HIDDEN), jnp.float32) * 0.02
        Wkv = jax.random.normal(k3, (HIDDEN, 2 * HEAD_DIM), jnp.float32) * 0.02
        Wo = jax.random.normal(k4, (HIDDEN, HIDDEN), jnp.float32) * 0.02
        return {'hidden_states': hidden_states, 'Wq': Wq, 'Wkv': Wkv, 'Wo': Wo}
    _L2_attn_in = _L2_attn_setup()

    def _L2_ffn_setup():
        import jax, jax.numpy as jnp
        import numpy as np
        NUM_EXPERTS = 4
        HIDDEN = 512
        RANK = 8
        ALPHA = 8.0
        SCALE = ALPHA / RANK
        key = jax.random.key(seed)
        ks = jax.random.split(key, 6)
        B, T, H, E, R = (4, 512, HIDDEN, NUM_EXPERTS, RANK)
        x = jax.random.normal(ks[0], (B, T, H), dtype=jnp.float32)
        W_up = jax.random.normal(ks[1], (H, H), dtype=jnp.float32) / np.sqrt(H)
        gate_w = jax.random.normal(ks[2], (E, H), dtype=jnp.float32) / np.sqrt(H)
        expert_bias = jnp.zeros((E,), dtype=jnp.float32)
        lora_A = jax.random.normal(ks[3], (E, R, H), dtype=jnp.float32) / np.sqrt(H)
        lora_B = jax.random.normal(ks[4], (E, H, R), dtype=jnp.float32) * 0.01
        return {'x': x, 'W_up': W_up, 'gate_w': gate_w, 'expert_bias': expert_bias, 'lora_A': lora_A, 'lora_B': lora_B}
    _L2_ffn_in = _L2_ffn_setup()

    def _L3_attn_setup():
        import jax, jax.numpy as jnp
        import numpy as np
        NUM_HEADS = 32
        NUM_KV_HEADS = 8
        HEAD_DIM = 128
        ROPE_THETA = 10000.0

        def _rope_cos_sin(seq_len, head_dim, dtype):
            inv_freq = 1.0 / ROPE_THETA ** (jnp.arange(0, head_dim, 2, dtype=jnp.float32) / head_dim)
            t = jnp.arange(seq_len, dtype=jnp.float32)
            freqs = jnp.outer(t, inv_freq)
            emb = jnp.concatenate([freqs, freqs], axis=-1)
            return (jnp.cos(emb).astype(dtype), jnp.sin(emb).astype(dtype))

        def _rotate_half(x):
            h = x.shape[-1] // 2
            return jnp.concatenate([-x[..., h:], x[..., :h]], axis=-1)

        def _apply_rope(x, cos, sin):
            return x * cos[None, None] + _rotate_half(x) * sin[None, None]
        key = jax.random.key(seed)
        ks = jax.random.split(key, 5)
        B, S, H = (1, 256, 512)
        return {'hidden_states': jax.random.normal(ks[0], (B, S, H), dtype=jnp.float32), 'Wq': jax.random.normal(ks[1], (H, NUM_HEADS * HEAD_DIM), dtype=jnp.float32) * 0.02, 'Wk': jax.random.normal(ks[2], (H, NUM_KV_HEADS * HEAD_DIM), dtype=jnp.float32) * 0.02, 'Wv': jax.random.normal(ks[3], (H, NUM_KV_HEADS * HEAD_DIM), dtype=jnp.float32) * 0.02, 'Wo': jax.random.normal(ks[4], (NUM_HEADS * HEAD_DIM, H), dtype=jnp.float32) * 0.02}
    _L3_attn_in = _L3_attn_setup()

    def _L3_ffn_setup():
        import jax, jax.numpy as jnp
        import numpy as np
        NUM_EXPERTS = 8
        TOP_K = 2
        RANK = 16
        LORA_ALPHA = 32
        SCALING = LORA_ALPHA / RANK
        key = jax.random.key(seed)
        ks = jax.random.split(key, 6)
        B, S, D_IN, D_OUT = (4, 256, 512, 512)
        x = jax.random.normal(ks[0], (B, S, D_IN), dtype=jnp.float32)
        W_base = jax.random.normal(ks[1], (D_OUT, D_IN), dtype=jnp.float32) * 0.02
        b_base = jax.random.normal(ks[2], (D_OUT,), dtype=jnp.float32) * 0.02
        W_router = jax.random.normal(ks[3], (NUM_EXPERTS, D_IN), dtype=jnp.float32) * 0.02
        A = jax.random.normal(ks[4], (NUM_EXPERTS, RANK, D_IN), dtype=jnp.float32) * 0.02
        Bm = jax.random.normal(ks[5], (D_OUT, RANK), dtype=jnp.float32) * 0.02
        Bm = jnp.broadcast_to(Bm, (NUM_EXPERTS, D_OUT, RANK)) * jnp.arange(1, NUM_EXPERTS + 1, dtype=jnp.float32)[:, None, None] * 0.2
        return {'x': x, 'W_base': W_base, 'b_base': b_base, 'W_router': W_router, 'A': A, 'B': Bm}
    _L3_ffn_in = _L3_ffn_setup()
    _d = {'L0_attn_x': _L0_attn_in['x'], 'L0_attn_w_qkv': _L0_attn_in['w_qkv'], 'L0_attn_b_qkv': _L0_attn_in['b_qkv'], 'L0_attn_w_o': _L0_attn_in['w_o'], 'L0_attn_b_o': _L0_attn_in['b_o'], 'L0_ffn_W': _L0_ffn_in['W'], 'L0_ffn_b': _L0_ffn_in['b'], 'L0_ffn_A': _L0_ffn_in['A'], 'L0_ffn_B': _L0_ffn_in['B'], 'L0_ffn_router_W': _L0_ffn_in['router_W'], 'L0_ffn_router_b': _L0_ffn_in['router_b'], 'L1_attn_Wq': _L1_attn_in['Wq'], 'L1_attn_Wk': _L1_attn_in['Wk'], 'L1_attn_Wv': _L1_attn_in['Wv'], 'L1_attn_Wo': _L1_attn_in['Wo'], 'L1_ffn_gate_w': _L1_ffn_in['gate_w'], 'L1_ffn_up_w': _L1_ffn_in['up_w'], 'L1_ffn_down_w': _L1_ffn_in['down_w'], 'L1_ffn_gate_a': _L1_ffn_in['gate_a'], 'L1_ffn_gate_b': _L1_ffn_in['gate_b'], 'L1_ffn_up_a': _L1_ffn_in['up_a'], 'L1_ffn_up_b': _L1_ffn_in['up_b'], 'L1_ffn_down_a': _L1_ffn_in['down_a'], 'L1_ffn_down_b': _L1_ffn_in['down_b'], 'L2_attn_Wq': _L2_attn_in['Wq'], 'L2_attn_Wkv': _L2_attn_in['Wkv'], 'L2_attn_Wo': _L2_attn_in['Wo'], 'L2_ffn_W_up': _L2_ffn_in['W_up'], 'L2_ffn_gate_w': _L2_ffn_in['gate_w'], 'L2_ffn_expert_bias': _L2_ffn_in['expert_bias'], 'L2_ffn_lora_A': _L2_ffn_in['lora_A'], 'L2_ffn_lora_B': _L2_ffn_in['lora_B'], 'L3_attn_Wq': _L3_attn_in['Wq'], 'L3_attn_Wk': _L3_attn_in['Wk'], 'L3_attn_Wv': _L3_attn_in['Wv'], 'L3_attn_Wo': _L3_attn_in['Wo'], 'L3_ffn_W_base': _L3_ffn_in['W_base'], 'L3_ffn_b_base': _L3_ffn_in['b_base'], 'L3_ffn_W_router': _L3_ffn_in['W_router'], 'L3_ffn_A': _L3_ffn_in['A'], 'L3_ffn_B': _L3_ffn_in['B']}
    _x0 = _d['L0_attn_x']
    _d['L0_attn_x'] = jax.random.normal(jax.random.fold_in(jax.random.key(seed), 1), (4, 256, 512), dtype=_x0.dtype)
    del _x0
    return _d

def reference(L0_attn_x, L0_attn_w_qkv, L0_attn_b_qkv, L0_attn_w_o, L0_attn_b_o, L0_ffn_W, L0_ffn_b, L0_ffn_A, L0_ffn_B, L0_ffn_router_W, L0_ffn_router_b, L1_attn_Wq, L1_attn_Wk, L1_attn_Wv, L1_attn_Wo, L1_ffn_gate_w, L1_ffn_up_w, L1_ffn_down_w, L1_ffn_gate_a, L1_ffn_gate_b, L1_ffn_up_a, L1_ffn_up_b, L1_ffn_down_a, L1_ffn_down_b, L2_attn_Wq, L2_attn_Wkv, L2_attn_Wo, L2_ffn_W_up, L2_ffn_gate_w, L2_ffn_expert_bias, L2_ffn_lora_A, L2_ffn_lora_B, L3_attn_Wq, L3_attn_Wk, L3_attn_Wv, L3_attn_Wo, L3_ffn_W_base, L3_ffn_b_base, L3_ffn_W_router, L3_ffn_A, L3_ffn_B):

    def _L0_attn_ref(x, w_qkv, b_qkv, w_o, b_o):
        import jax, jax.numpy as jnp
        import numpy as np
        import math
        D_MODEL = 512
        NUM_HEADS = 32
        NUM_KV_HEADS = 8
        HEAD_DIM = D_MODEL // NUM_HEADS
        GROUP = NUM_HEADS // NUM_KV_HEADS
        SEQ_LEN = 256
        BATCH = 2
        ROPE_THETA = 10000.0

        def apply_rope(x, start_pos=0):
            b, h, s, hd = x.shape
            inv_freq = 1.0 / ROPE_THETA ** (jnp.arange(0, hd, 2, dtype=jnp.float32) / hd)
            pos = jnp.arange(start_pos, start_pos + s, dtype=jnp.float32)
            ang = pos[:, None] * inv_freq[None, :]
            cos = jnp.cos(ang).astype(x.dtype)
            sin = jnp.sin(ang).astype(x.dtype)
            xr = x[..., 0::2]
            xi = x[..., 1::2]
            out_r = xr * cos - xi * sin
            out_i = xr * sin + xi * cos
            return jnp.stack([out_r, out_i], axis=-1).reshape(b, h, s, hd)
        bs, seq_len, d_model = x.shape
        qkv = x @ w_qkv.T + b_qkv
        q_dim = NUM_HEADS * HEAD_DIM
        kv_dim = NUM_KV_HEADS * HEAD_DIM
        q, k, v = jnp.split(qkv, [q_dim, q_dim + kv_dim], axis=-1)
        q = q.reshape(bs, seq_len, NUM_HEADS, HEAD_DIM).transpose(0, 2, 1, 3)
        k = k.reshape(bs, seq_len, NUM_KV_HEADS, HEAD_DIM).transpose(0, 2, 1, 3)
        v = v.reshape(bs, seq_len, NUM_KV_HEADS, HEAD_DIM).transpose(0, 2, 1, 3)
        q = apply_rope(q, 0)
        k = apply_rope(k, 0)
        k = jnp.repeat(k, GROUP, axis=1)
        v = jnp.repeat(v, GROUP, axis=1)
        scores = jnp.einsum('bhqd,bhkd->bhqk', q, k) / math.sqrt(HEAD_DIM)
        causal = jnp.tril(jnp.ones((seq_len, seq_len), dtype=bool))
        scores = jnp.where(causal[None, None, :, :], scores, jnp.float32(-1e+20))
        attn = jax.nn.softmax(scores, axis=-1)
        out = jnp.einsum('bhqk,bhkd->bhqd', attn, v)
        out = out.transpose(0, 2, 1, 3).reshape(bs, seq_len, d_model)
        return out @ w_o.T + b_o

    def _L0_ffn_ref(x, W, b, A, B, router_W, router_b):
        import jax, jax.numpy as jnp
        import numpy as np
        IMAGE_START_POS = 34
        Q_START = IMAGE_START_POS + 72 + 1
        Q_END = -1
        LORA_ALPHA = 32
        LORA_RANK = 16
        SCALING = LORA_ALPHA / LORA_RANK
        x_q = x[:, Q_START:Q_END, :]
        q = x_q.mean(axis=1)
        logits = q @ router_W.T + router_b
        routing = jax.nn.softmax(logits, axis=-1)
        base = x @ W.T + b
        t = jnp.einsum('bsd,erd->bser', x, A)
        lora = jnp.einsum('bser,eor,be->bso', t, B, routing) * SCALING
        return base + lora

    def _L1_attn_ref(hidden_states, Wq, Wk, Wv, Wo):
        import jax, jax.numpy as jnp
        import numpy as np
        B, N, HID = (1, 256, 512)
        H, KVH, D, W = (32, 8, 128, 64)
        THETA = 10000.0
        GATE_NORM = 16.0

        def rope(x, pos):
            half = jnp.arange(D // 2, dtype=jnp.float32)
            inv = 1.0 / THETA ** (2.0 * half / D)
            fr = pos[:, None].astype(jnp.float32) * inv[None, :]
            emb = jnp.concatenate([fr, fr], axis=-1)
            cos, sin = (jnp.cos(emb)[None, None], jnp.sin(emb)[None, None])
            x1, x2 = jnp.split(x, 2, axis=-1)
            rot = jnp.concatenate([-x2, x1], axis=-1)
            return x * cos + rot * sin

        def gla_scan(q, k, v, g):
            qt, kt, vt, gt = (jnp.moveaxis(t, 2, 0) for t in (q, k, v, g))
            b, h = (q.shape[0], q.shape[1])
            S0 = jnp.zeros((b, h, D, D), jnp.float32)

            def step(S, x):
                q_t, k_t, v_t, g_t = x
                S = S * jnp.exp(g_t)[..., None] + k_t[..., None] * v_t[..., None, :]
                return (S, jnp.einsum('bhk,bhkv->bhv', q_t, S))
            _, o = jax.lax.scan(step, S0, (qt, kt, vt, gt))
            return jnp.moveaxis(o, 0, 2)

        def sliding_window_attn(q, k, v):
            b, h, n, d = q.shape
            nb = n // W
            qb = q.reshape(b, h, nb, W, d)

            def two_blocks(x):
                xb = x.reshape(b, h, nb, W, d)
                prev = jnp.concatenate([jnp.zeros_like(xb[:, :, :1]), xb[:, :, :-1]], axis=2)
                return jnp.concatenate([prev, xb], axis=3)
            kb, vb = (two_blocks(k), two_blocks(v))
            scores = jnp.einsum('bhnqd,bhnkd->bhnqk', qb, kb) / jnp.sqrt(jnp.float32(d))
            a = jnp.arange(W)[:, None]
            c = jnp.arange(2 * W)[None, :]
            rel = a + W - c
            base = (rel >= 0) & (rel <= W)
            blk = jnp.arange(nb)[:, None, None]
            keypos = (blk - 1) * W + c[None]
            mask = base[None] & (keypos >= 0)
            scores = jnp.where(mask[None, None], scores, -jnp.inf)
            p = jax.nn.softmax(scores, axis=-1)
            ob = jnp.einsum('bhnqk,bhnkd->bhnqd', p, vb)
            return ob.reshape(b, h, n, d)
        b, n, _ = hidden_states.shape
        grp = H // KVH
        q = hidden_states @ Wq
        k = hidden_states @ Wk
        v = hidden_states @ Wv
        g = k
        q = q.reshape(b, n, H, D).transpose(0, 2, 1, 3)
        k = k.reshape(b, n, KVH, D).transpose(0, 2, 1, 3)
        v = v.reshape(b, n, KVH, D).transpose(0, 2, 1, 3)
        g = g.reshape(b, n, KVH, D).transpose(0, 2, 1, 3)
        k = jnp.repeat(k, grp, axis=1)
        v = jnp.repeat(v, grp, axis=1)
        g = jnp.repeat(g, grp, axis=1)
        sq, sk, sv = (q, k, v)
        qs = jax.nn.softmax(q.astype(jnp.float32), axis=-1)
        ks_ = jax.nn.softmax(k.astype(jnp.float32), axis=-1)
        gs = jax.nn.log_sigmoid(g.astype(jnp.float32)) / GATE_NORM
        o_lin = gla_scan(qs, ks_, v.astype(jnp.float32), gs)
        pos = jnp.arange(n)
        sq = rope(sq, pos)
        sk = rope(sk, pos)
        y = sliding_window_attn(sq, sk, sv)
        o_ = 0.5 * y + 0.5 * o_lin
        o_ = o_.astype(jnp.bfloat16).astype(jnp.float32)
        o = o_.transpose(0, 2, 1, 3).reshape(b, n, H * D) @ Wo
        return o

    def _L1_ffn_ref(x, gate_w, up_w, down_w, gate_a, gate_b, up_a, up_b, down_a, down_b):
        import jax, jax.numpy as jnp
        import numpy as np
        D_MODEL = 512
        D_HIDDEN = 1376
        RANK = 16
        BATCH, SEQ = (2, 256)

        def _matmul_lora(x, w, a, b, scale=1.0):
            out = jnp.einsum('bsd,hd->bsh', x, w)
            out = out + jnp.einsum('bsr,hr->bsh', jnp.einsum('bsd,rd->bsr', x, a), b) * scale
            return out
        gate = _matmul_lora(x, gate_w, gate_a, gate_b)
        up = _matmul_lora(x, up_w, up_a, up_b)
        hidden = jax.nn.silu(gate) * up
        out = _matmul_lora(hidden, down_w, down_a, down_b)
        return out

    def _L2_attn_ref(hidden_states, Wq, Wkv, Wo):
        import jax, jax.numpy as jnp
        import numpy as np
        HIDDEN = 512
        NUM_HEADS = 32
        HEAD_DIM = HIDDEN // NUM_HEADS
        B, S = (2, 128)

        def _alibi_slopes(n):
            start = 2.0 ** (-2.0 ** (-(np.log2(n) - 3)))
            return np.array([start ** (i + 1) for i in range(n)], dtype=np.float32)
        b, s, h = hidden_states.shape
        scale = HEAD_DIM ** (-0.5)
        q = (hidden_states @ Wq).reshape(b, s, NUM_HEADS, HEAD_DIM)
        kv = hidden_states @ Wkv
        k, v = (kv[..., :HEAD_DIM], kv[..., HEAD_DIM:])
        scores = jnp.einsum('bqhd,bkd->bhqk', q, k) * scale
        pos = jnp.arange(s)
        slopes = jnp.asarray(_alibi_slopes(NUM_HEADS))
        bias = slopes[:, None, None] * (pos[None, None, :] - pos[None, :, None]).astype(jnp.float32)
        causal = pos[None, :] <= pos[:, None]
        scores = jnp.where(causal[None, None], scores + bias[None], -jnp.inf)
        attn = jax.nn.softmax(scores, axis=-1)
        out = jnp.einsum('bhqk,bkd->bqhd', attn, v).reshape(b, s, h)
        return out @ Wo

    def _L2_ffn_ref(x, W_up, gate_w, expert_bias, lora_A, lora_B):
        import jax, jax.numpy as jnp
        import numpy as np
        NUM_EXPERTS = 4
        HIDDEN = 512
        RANK = 8
        ALPHA = 8.0
        SCALE = ALPHA / RANK
        B, T, H = x.shape
        E = gate_w.shape[0]
        x_flat = x.reshape(-1, H)
        logits = x_flat @ gate_w.T + expert_bias
        top1 = jnp.argmax(logits, axis=-1)
        one_hot = jax.nn.one_hot(top1, E, dtype=x_flat.dtype)
        base_out = jnp.einsum('bth,oh->bto', x, W_up)
        z = jnp.einsum('nh,erh->ner', x_flat, lora_A)
        d = jnp.einsum('ner,ehr->neh', z, lora_B) * SCALE
        delta = jnp.einsum('neh,ne->nh', d, one_hot)
        return base_out + delta.reshape(B, T, H)

    def _L3_attn_ref(hidden_states, Wq, Wk, Wv, Wo):
        import jax, jax.numpy as jnp
        import numpy as np
        NUM_HEADS = 32
        NUM_KV_HEADS = 8
        HEAD_DIM = 128
        ROPE_THETA = 10000.0

        def _rope_cos_sin(seq_len, head_dim, dtype):
            inv_freq = 1.0 / ROPE_THETA ** (jnp.arange(0, head_dim, 2, dtype=jnp.float32) / head_dim)
            t = jnp.arange(seq_len, dtype=jnp.float32)
            freqs = jnp.outer(t, inv_freq)
            emb = jnp.concatenate([freqs, freqs], axis=-1)
            return (jnp.cos(emb).astype(dtype), jnp.sin(emb).astype(dtype))

        def _rotate_half(x):
            h = x.shape[-1] // 2
            return jnp.concatenate([-x[..., h:], x[..., :h]], axis=-1)

        def _apply_rope(x, cos, sin):
            return x * cos[None, None] + _rotate_half(x) * sin[None, None]
        B, S, H = hidden_states.shape
        nh, nkv, hd = (NUM_HEADS, NUM_KV_HEADS, HEAD_DIM)
        groups = nh // nkv
        q = (hidden_states @ Wq).reshape(B, S, nh, hd).transpose(0, 2, 1, 3)
        k = (hidden_states @ Wk).reshape(B, S, nkv, hd).transpose(0, 2, 1, 3)
        v = (hidden_states @ Wv).reshape(B, S, nkv, hd).transpose(0, 2, 1, 3)
        cos, sin = _rope_cos_sin(S, hd, q.dtype)
        q = _apply_rope(q, cos, sin)
        k = _apply_rope(k, cos, sin)
        k = jnp.repeat(k, groups, axis=1)
        v = jnp.repeat(v, groups, axis=1)
        scale = 1.0 / jnp.sqrt(jnp.asarray(hd, dtype=q.dtype))
        logits = jnp.einsum('bhqd,bhkd->bhqk', q, k) * scale
        causal = jnp.tril(jnp.ones((S, S), dtype=bool))
        neg = jnp.asarray(jnp.finfo(logits.dtype).min, dtype=logits.dtype)
        logits = jnp.where(causal[None, None], logits, neg)
        attn = jax.nn.softmax(logits.astype(jnp.float32), axis=-1).astype(q.dtype)
        out = jnp.einsum('bhqk,bhkd->bhqd', attn, v)
        out = out.transpose(0, 2, 1, 3).reshape(B, S, nh * hd)
        return out @ Wo

    def _L3_ffn_ref(x, W_base, b_base, W_router, A, B):
        import jax, jax.numpy as jnp
        import numpy as np
        NUM_EXPERTS = 8
        TOP_K = 2
        RANK = 16
        LORA_ALPHA = 32
        SCALING = LORA_ALPHA / RANK
        bs, seq, d_in = x.shape
        T = bs * seq
        xf = x.reshape(T, d_in)
        base = xf @ W_base.T + b_base
        logits = xf @ W_router.T
        rw, sel = jax.lax.top_k(logits, TOP_K)
        rw = jax.nn.softmax(rw, axis=-1)
        onehot = jax.nn.one_hot(sel, NUM_EXPERTS, dtype=rw.dtype)
        w = jnp.einsum('tk,tke->te', rw, onehot)
        h = jnp.einsum('td,erd->ter', xf, A)
        lora = jnp.einsum('ter,te,eor->to', h, w, B) * SCALING
        return (base + lora).reshape(bs, seq, -1)
    x = L0_attn_x
    x = x + _L0_attn_ref(_layernorm(x, axis=-1), L0_attn_w_qkv, L0_attn_b_qkv, L0_attn_w_o, L0_attn_b_o)
    x = x + _L0_ffn_ref(_layernorm(x, axis=-1), L0_ffn_W, L0_ffn_b, L0_ffn_A, L0_ffn_B, L0_ffn_router_W, L0_ffn_router_b)
    x = x + _L1_attn_ref(_layernorm(x, axis=-1), L1_attn_Wq, L1_attn_Wk, L1_attn_Wv, L1_attn_Wo)
    x = x + _L1_ffn_ref(_layernorm(x, axis=-1), L1_ffn_gate_w, L1_ffn_up_w, L1_ffn_down_w, L1_ffn_gate_a, L1_ffn_gate_b, L1_ffn_up_a, L1_ffn_up_b, L1_ffn_down_a, L1_ffn_down_b)
    x = x + _L2_attn_ref(_layernorm(x, axis=-1), L2_attn_Wq, L2_attn_Wkv, L2_attn_Wo)
    x = x + _L2_ffn_ref(_layernorm(x, axis=-1), L2_ffn_W_up, L2_ffn_gate_w, L2_ffn_expert_bias, L2_ffn_lora_A, L2_ffn_lora_B)
    x = x + _L3_attn_ref(_layernorm(x, axis=-1), L3_attn_Wq, L3_attn_Wk, L3_attn_Wv, L3_attn_Wo)
    x = x + _L3_ffn_ref(_layernorm(x, axis=-1), L3_ffn_W_base, L3_ffn_b_base, L3_ffn_W_router, L3_ffn_A, L3_ffn_B)
    return x

_drawn_inputs = setup_inputs


def setup_inputs(seed=0):
    import zlib

    import numpy as np

    out = dict(_drawn_inputs(seed))
    spreads = {'L2_ffn_expert_bias': (0.0, 2.0)}
    factors = {'L0_attn_b_qkv': 5.283,
     'L0_attn_b_o': 6.21,
     'L0_ffn_b': 3.609,
     'L0_ffn_A': 3.416,
     'L0_ffn_B': 3.418,
     'L0_ffn_router_W': 8.0,
     'L0_ffn_router_b': 8.0,
     'L1_attn_Wq': 8.0,
     'L1_attn_Wk': 8.0,
     'L1_ffn_gate_a': 8.0,
     'L1_ffn_gate_b': 8.0,
     'L1_ffn_up_a': 8.0,
     'L1_ffn_up_b': 8.0,
     'L1_ffn_down_a': 8.0,
     'L1_ffn_down_b': 8.0,
     'L2_attn_Wq': 61.616,
     'L2_ffn_gate_w': 5.066,
     'L2_ffn_lora_A': 4.464,
     'L2_ffn_lora_B': 4.414,
     'L3_attn_Wq': 7.847,
     'L3_attn_Wk': 7.814,
     'L3_ffn_b_base': 43.762,
     'L3_ffn_W_router': 22.896,
     'L2_attn_Wkv': 7.003,
     'L2_attn_Wo': 7.97,
     'L3_ffn_A': 8.0,
     'L3_ffn_B': 8.0}
    for name, (base, spread) in spreads.items():
        noise = np.random.default_rng([zlib.crc32(name.encode()), seed]).standard_normal(out[name].shape)
        drawn = base * np.exp(spread * noise) if base else spread * noise
        out[name] = jnp.asarray(drawn.astype(out[name].dtype))
    for name, factor in factors.items():
        out[name] = (out[name] * factor).astype(out[name].dtype)
    return out
```

```python
from contextlib import ExitStack

import concourse.bass as bass
import concourse.mybir as mybir
import numpy as np

F32 = mybir.dt.float32
BF16 = mybir.dt.bfloat16
U32 = mybir.dt.uint32
ALU = mybir.AluOpType
ACT = mybir.ActivationFunctionType
AX = mybir.AxisListType

P = 128
D = 512
C = D // P
B, S = 4, 256
TPS = S // P
NT = B * TPS
EPS = 1e-5
BIG = 1e30
HEADS, KV_HEADS = 32, 8
WINDOW = 64
MEAN_FROM, MEAN_TO = 34 + 72 + 1, S - 1
GROUP = HEADS // KV_HEADS
SCORE_COLS = P + S
SPAN = [slice(0, P), slice(P, P + S)]


class Core:

    def __init__(self, nc, ctx, dram):
        self.nc, self.dram = nc, dram
        self.X = ctx.enter_context(nc.sbuf_tensor("X", [P, NT, D], F32))
        self.ident = ctx.enter_context(nc.sbuf_tensor("ident", [P, P], F32))
        self.one = ctx.enter_context(nc.sbuf_tensor("one", [P, 1], F32))
        self.eps = ctx.enter_context(nc.sbuf_tensor("eps", [P, 1], F32))
        self.mask = ctx.enter_context(nc.sbuf_tensor("mask", [P, SCORE_COLS], F32))
        self.carrier = ctx.enter_context(nc.semaphore("carrier"))
        self.loaded = ctx.enter_context(nc.semaphore("constants_loaded"))

    def carry_wait(self, eng):
        eng.sem_inc(self.carrier, 1)


class Layer:

    def __init__(self, core, ctx, name):
        self.core, self.ctx, self.name, self.nc = core, ctx, name, core.nc
        self.sems = []
        ctx.callback(self.close)

    def close(self):
        self.nc.clear_and_free_semaphores(self.sems)
        self.nc.all_engine_barrier()

    def sb(self, name, shape, dtype=F32):
        return self.ctx.enter_context(self.nc.sbuf_tensor(f"{self.name}_{name}", shape, dtype))

    def bank(self, name, shape=(P, 512), dtype=F32):
        return self.ctx.enter_context(self.nc.psum_tensor(f"{self.name}_{name}", list(shape), dtype))

    def sem(self, name):
        self.sems.append(self.nc.alloc_semaphore(f"{self.name}_{name}"))
        return self.sems[-1]


class Ring:

    def __init__(self, layer, name, per):
        assert per % 2 == 0
        self.banks = [layer.bank(f"{name}{k}") for k in range(2)]
        self.filled = [layer.sem(f"{name}{k}_filled") for k in range(2)]
        self.emptied = [layer.sem(f"{name}{k}_emptied") for k in range(2)]
        self.per = per // 2

    def wait_free(self, pe, i, n):
        pe.wait_ge(self.emptied[n % 2], 1 + i * self.per + n // 2)

    def wait_empty(self, eng, i, n):
        eng.wait_ge(self.emptied[n % 2], 1 + i * self.per + n // 2 + 1)

    def open(self, pe):
        for k in self.emptied:
            pe.sem_inc(k, 1)

    def wait_full(self, eng, i, n):
        eng.wait_ge(self.filled[n % 2], i * self.per + n // 2 + 1)


class LayerNorm:

    def __init__(self, layer, ring):
        self.core, self.nc, self.ring = layer.core, layer.nc, ring
        self.xn = layer.sb("xn", [P, TPS, D])
        self.xT = layer.sb("xT", [P, C, S])
        self.stats = layer.sb("stats", [P, TPS, 6])
        self.moments = layer.sb("moments", [P, TPS, 2])
        self.std = layer.sb("std", [P, TPS])
        self.rstd = layer.sb("rstd", [P, TPS])
        self.stats_ready = layer.sem("stats_ready")
        self.moments_ready = layer.sem("moments_ready")
        self.std_ready = layer.sem("std_ready")
        self.rstd_ready = layer.sem("rstd_ready")
        self.xn_ready = layer.sem("xn_ready")
        self.xT_ready = layer.sem("xT_ready")

    def vector(self, dve, b):
        nc, X = self.nc, self.core.X
        for t in range(TPS):
            nc.vector.bn_stats(self.stats[:, t, :], X[:, TPS * b + t, :]).then_inc(self.stats_ready, 1)
        for t in range(TPS):
            dve.wait_ge(self.stats_ready, TPS * b + t + 1)
            self.core.carry_wait(dve)
            nc.vector.bn_aggr(self.moments[:, t, :], self.stats[:, t, :]).then_inc(self.moments_ready, 1)
        for t in range(TPS):
            dve.wait_ge(self.std_ready, TPS * b + t + 1)
            nc.vector.reciprocal(self.rstd[:, t:t + 1], self.std[:, t:t + 1]).then_inc(self.rstd_ready, 1)
            dve.wait_ge(self.rstd_ready, TPS * b + t + 1)
            nc.vector.tensor_scalar(self.xn[:, t, :], X[:, TPS * b + t, :], self.moments[:, t, 0:1],
                                    self.rstd[:, t:t + 1], ALU.subtract, ALU.mult).then_inc(self.xn_ready, 1)

    def scalar(self, act, b):
        nc = self.nc
        for t in range(TPS):
            act.wait_ge(self.moments_ready, TPS * b + t + 1)
            nc.scalar.activation(self.std[:, t:t + 1], self.moments[:, t, 1:2], ACT.Sqrt,
                                 bias=self.core.eps[:, 0:1]).then_inc(self.std_ready, 1)

    def scalar_xT(self, act, b, xT=None):
        nc, xT = self.nc, self.xT if xT is None else xT
        for t in range(TPS):
            self.ring.wait_full(act, b, t)
            nc.scalar.copy(xT[:, :, t * P:(t + 1) * P],
                           self.ring.banks[t].rearrange("p (c n) -> p c n", c=C))\
                .then_inc(self.ring.emptied[t], 1)

    def tensor(self, pe, b):
        nc = self.nc
        for t in range(TPS):
            pe.wait_ge(self.xn_ready, TPS * b + t + 1)
            self.ring.wait_free(pe, b, t)
            for c in range(C):
                last = nc.tensor.transpose(self.ring.banks[t][:, c * P:(c + 1) * P],
                                           self.xn[:, t, c * P:(c + 1) * P], self.core.ident[:, :])
            last.then_inc(self.ring.filled[t], 1)

    def wait_xT(self, eng, b, t):
        self.ring.wait_empty(eng, b, t)


def load_constants(core):
    nc, dram = core.nc, core.dram
    loaded = core.loaded
    with ExitStack() as ctx:
        block = ctx.enter_context(nc.Block())

        @block.sync
        def _(sp):
            sp.dma_start(core.ident[:, :], dram["ident"]).then_inc(loaded, 16)
            sp.dma_start(core.mask[:, :], dram["mask"]).then_inc(loaded, 16)
            sp.dma_start(core.eps[:, :], dram["eps"]).then_inc(loaded, 16)
            sp.dma_start(core.one[:, :], dram["one"]).then_inc(loaded, 16)
            xv = dram["x"].rearrange("b (t p) d -> p (b t) d", p=P)
            sp.dma_start(core.X[:, :, :], xv).then_inc(loaded, 16)
            sp.wait_ge(loaded, 80)


def store_result(core):
    nc = core.nc
    with ExitStack() as ctx:
        stored = ctx.enter_context(nc.semaphore("stored"))
        block = ctx.enter_context(nc.Block())

        @block.sync
        def _(sp):
            ov = core.dram["out"].rearrange("b (t p) d -> p (b t) d", p=P)
            sp.dma_start(ov, core.X[:, :, :]).then_inc(stored, 16)
            sp.wait_ge(stored, 16)


def narrow_attention(core, name, rope):
    nc, dram, X, ident = core.nc, core.dram, core.X, core.ident
    HD = 16
    SLOT = 32
    SLOTS = P // SLOT
    QG = HEADS // SLOTS
    KG = KV_HEADS if rope else 1
    ROWS = HD if rope else HD + 2
    KV = KG * HD
    QKV = HEADS * HD + 2 * KV
    PIECES = [(0, 512), (512, QKV - 512)]
    QU, KU = QG * P // 512, max(1, KG * P // 512)
    KB = KG // KU
    LN_USES = TPS
    HEAD0 = LN_USES + TPS * (QU + KU)
    OUT0 = HEAD0 + HEADS
    T_USES = OUT0 + TPS
    A_USES = TPS * 2 + TPS

    with ExitStack() as ctx:
        L = Layer(core, ctx, name)
        turned = Ring(L, "turned", T_USES)
        summed = Ring(L, "summed", A_USES)
        ln = LayerNorm(L, turned)
        scores = [L.bank(f"scores{k}") for k in range(2)]
        heads_out = [L.bank(f"heads_out{t}") for t in range(TPS)]

        w_qkv = L.sb("w_qkv", [P, C, QKV])
        w_o = L.sb("w_o", [P, C, D])
        q_pad = L.sb("q_pad", [P, TPS, HEADS, SLOT])
        k_pad = L.sb("k_pad", [P, TPS, KG, SLOTS, SLOT])
        v = L.sb("v", [P, TPS, KG, HD])
        qT = L.sb("qT", [P, QG, S])
        kT = L.sb("kT", [P, KG, S])
        masked = L.sb("masked", [P, 2, SCORE_COLS])
        neg_max = L.sb("neg_max", [P, TPS, HEADS])
        total = L.sb("total", [P, TPS, HEADS])
        r_total = L.sb("r_total", [P, TPS, HEADS])
        probs = L.sb("probs", [P, 2, SCORE_COLS])
        probsT = L.sb("probsT", [P, 2, SCORE_COLS])
        out = L.sb("out", [P, TPS, HEADS, HD])
        outT = L.sb("outT", [P, C, S])
        if rope:
            b_qkv = L.sb("b_qkv", [P, QKV])
            b_o = L.sb("b_o", [P, D])
            qkv = L.sb("qkv", [P, TPS, QKV])
            straight = L.sb("straight", [P, TPS, (HEADS + KG) * HD])
            crossed = L.sb("crossed", [P, TPS, (HEADS + KG) * HD])
            cos = L.sb("cos", [P, TPS, (HEADS + KG) * HD])
            sin = L.sb("sin", [P, TPS, (HEADS + KG) * HD])

        weights_loaded = L.sem("weights_loaded")
        padded = L.sem("padded")
        qkv_ready = L.sem("qkv_ready")
        turned_parts_ready = L.sem("rope_parts_ready")
        q_pad_ready = L.sem("q_pad_ready")
        kv_ready = L.sem("kv_ready")
        scores_filled = L.sem("scores_filled")
        masked_ready = L.sem("masked_ready")
        probs_ready = L.sem("probs_ready")
        pv_done = L.sem("pv_done")
        r_total_ready = L.sem("r_total_ready")
        out_ready = L.sem("out_ready")
        x_written = L.sem("x_written")
        bias_added = L.sem("bias_added")
        block = ctx.enter_context(nc.Block())

        @block.sync
        def _(sp):
            sp.dma_start(w_qkv[:, :, :], dram[f"{name}_w_qkv"].rearrange("(c p) n -> p c n", p=P))\
                .then_inc(weights_loaded, 16)
            sp.dma_start(w_o[:, :, :], dram[f"{name}_w_o"].rearrange("(c p) n -> p c n", p=P))\
                .then_inc(weights_loaded, 16)
            if rope:
                sp.dma_start(b_qkv[:, :], dram[f"{name}_b_qkv"].partition_broadcast(P)).then_inc(weights_loaded, 16)
                sp.dma_start(b_o[:, :], dram[f"{name}_b_o"].partition_broadcast(P)).then_inc(weights_loaded, 16)
                sp.dma_start(cos[:, :, :], dram[f"{name}_cos"]).then_inc(weights_loaded, 16)
                sp.dma_start(sin[:, :, :], dram[f"{name}_sin"]).then_inc(weights_loaded, 16)
            sp.dma_start(q_pad[:, :, :, :], dram[f"{name}_q_pad"]).then_inc(padded, 16)
            sp.dma_start(k_pad[:, :, :, :, :], dram[f"{name}_k_pad"]).then_inc(padded, 16)

        loads = 16 * (6 if rope else 2)

        @block.vector
        def _(dve):
            dve.wait_ge(padded, 32)
            if rope:
                dve.wait_ge(weights_loaded, loads)
            with dve.Fori(0, B) as b:
                ln.vector(dve, b)
                for t in range(TPS):
                    if rope:
                        for j, (at, n) in enumerate(PIECES):
                            summed.wait_full(dve, b, 2 * t + j)
                            nc.vector.tensor_tensor(qkv[:, t, at:at + n], summed.banks[j][:, 0:n],
                                                    b_qkv[:, at:at + n], ALU.add)\
                                .then_inc(summed.emptied[j], 1)
                        NR = (HEADS + KG) * HD
                        summed.wait_empty(dve, b, 2 * t)
                        summed.wait_empty(dve, b, 2 * t + 1)
                        nc.vector.tensor_tensor(straight[:, t, :], qkv[:, t, 0:NR], cos[:, t, :], ALU.mult)\
                            .then_inc(turned_parts_ready, 1)
                        src = qkv[:, t, 0:NR].rearrange("p (n two) -> p n two", two=2)
                        dst = crossed[:, t, :].rearrange("p (n two) -> p n two", two=2)
                        sn = sin[:, t, :].rearrange("p (n two) -> p n two", two=2)
                        for e in range(2):
                            nc.vector.tensor_tensor(dst[:, :, e], src[:, :, 1 - e], sn[:, :, e], ALU.mult)\
                                .then_inc(turned_parts_ready, 1)
                        dve.wait_ge(turned_parts_ready, 3 * (TPS * b + t + 1))
                        QN = HEADS * HD
                        nc.vector.tensor_tensor(
                            q_pad[:, t, :, 0:HD], straight[:, t, 0:QN].rearrange("p (h d) -> p h d", d=HD),
                            crossed[:, t, 0:QN].rearrange("p (h d) -> p h d", d=HD), ALU.add)\
                            .then_inc(q_pad_ready, 1)
                        for s in range(SLOTS):
                            nc.vector.tensor_tensor(
                                k_pad[:, t, :, s, 0:HD],
                                straight[:, t, QN:NR].rearrange("p (h d) -> p h d", d=HD),
                                crossed[:, t, QN:NR].rearrange("p (h d) -> p h d", d=HD), ALU.add)\
                                .then_inc(kv_ready, 1)
                        nc.vector.tensor_copy(v[:, t, :, :],
                                              qkv[:, t, NR:QKV].rearrange("p (h d) -> p h d", d=HD))\
                            .then_inc(kv_ready, 1)
                    else:
                        summed.wait_full(dve, b, 2 * t)
                        nc.vector.tensor_scalar(
                            q_pad[:, t, :, 0:HD], summed.banks[0].rearrange("p (h d) -> p h d", d=HD),
                            -float(HD) ** -0.5, None, ALU.mult).then_inc(summed.emptied[0], 1)
                        summed.wait_full(dve, b, 2 * t + 1)
                        for s in range(SLOTS):
                            nc.vector.tensor_copy(k_pad[:, t, 0, s, 0:HD], summed.banks[1][:, 0:HD])\
                                .then_inc(kv_ready, 1)
                        nc.vector.tensor_copy(v[:, t, 0, :], summed.banks[1][:, HD:2 * HD])\
                            .then_inc(summed.emptied[1], 1)

                def mask_scores(h):
                    k = h % 2
                    dve.wait_ge(scores_filled, HEADS * b + h + 1)
                    if h >= 2:
                        dve.wait_ge(probs_ready, TPS * (HEADS * b + h - 1))
                    core.carry_wait(dve)
                    for t in range(TPS):
                        nc.vector.tensor_tensor_reduce(masked[:, k, SPAN[t]], scores[k][:, SPAN[t]],
                                                       core.mask[:, SPAN[t]], 1.0, 3e38, ALU.add, ALU.min,
                                                       neg_max[:, t, h:h + 1]).then_inc(masked_ready, 1)

                def empty_probsT(h):
                    n = HEAD0 + h
                    turned.wait_full(dve, b, n)
                    if h >= 2:
                        dve.wait_ge(pv_done, HEADS * b + h - 1)
                    nc.vector.tensor_copy(probsT[:, h % 2, :], turned.banks[n % 2][:, 0:SCORE_COLS])\
                        .then_inc(turned.emptied[n % 2], 1)

                mask_scores(0)
                for h in range(HEADS):
                    if h + 1 < HEADS:
                        mask_scores(h + 1)
                    if h % 2 == 0:
                        empty_probsT(h)
                dve.wait_ge(probs_ready, TPS * HEADS * (b + 1))
                for t in range(TPS):
                    nc.vector.reciprocal(r_total[:, t, :], total[:, t, :]).then_inc(r_total_ready, 1)
                dve.wait_ge(pv_done, HEADS * (b + 1))
                for t in range(TPS):
                    dve.wait_ge(r_total_ready, TPS * b + t + 1)
                    nc.vector.tensor_tensor(out[:, t, :, :],
                                            heads_out[t].rearrange("p (h d) -> p h d", d=HD),
                                            r_total[:, t, :].unsqueeze(2).to_broadcast([P, HEADS, HD]),
                                            ALU.mult).then_inc(out_ready, 1)
                if rope:
                    dve.wait_ge(bias_added, TPS * (b + 1))
                for t in range(TPS):
                    n = 2 * TPS + t
                    summed.wait_full(dve, b, n)
                    nc.vector.tensor_tensor(X[:, TPS * b + t, :], X[:, TPS * b + t, :],
                                            summed.banks[n % 2][:, :], ALU.add)\
                        .then_inc(summed.emptied[n % 2], 1)

        @block.gpsimd
        def _(pool):
            if rope:
                pool.wait_ge(weights_loaded, loads)
                with pool.Fori(0, B) as b:
                    for t in range(TPS):
                        pool.wait_ge(ln.xn_ready, TPS * b + t + 1)
                        nc.gpsimd.tensor_tensor(X[:, TPS * b + t, :], X[:, TPS * b + t, :], b_o[:, :], ALU.add)\
                            .then_inc(bias_added, 1)

        @block.scalar
        def _(act):
            with act.Fori(0, B) as b:
                ln.scalar(act, b)
                ln.scalar_xT(act, b)
                for t in range(TPS):
                    for j in range(QU + KU):
                        n = LN_USES + t * (QU + KU) + j
                        turned.wait_full(act, b, n)
                        src = turned.banks[n % 2]
                        if j < QU:
                            nc.scalar.copy(qT[:, 4 * j:4 * j + 4, t * P:(t + 1) * P],
                                           src.rearrange("p (g n) -> p g n", g=4))\
                                .then_inc(turned.emptied[n % 2], 1)
                        else:
                            u = j - QU
                            nc.scalar.copy(kT[:, KB * u:KB * (u + 1), t * P:(t + 1) * P],
                                           src[:, 0:KB * P].rearrange("p (g n) -> p g n", g=KB))\
                                .then_inc(turned.emptied[n % 2], 1)

                def exponentials(h):
                    k = h % 2
                    for t in range(TPS):
                        act.wait_ge(masked_ready, TPS * (HEADS * b + h) + t + 1)
                        if t == 0 and h >= 2:
                            turned.wait_full(act, b, HEAD0 + h - 2)
                        nc.scalar.activation(probs[:, k, SPAN[t]], masked[:, k, SPAN[t]], ACT.Exp,
                                             bias=neg_max[:, t, h:h + 1], scale=-1.0,
                                             accum_out=total[:, t, h:h + 1]).then_inc(probs_ready, 1)

                exponentials(0)
                for h in range(HEADS):
                    if h + 1 < HEADS:
                        exponentials(h + 1)
                    if h % 2 == 1:
                        n = HEAD0 + h
                        turned.wait_full(act, b, n)
                        if h >= 2:
                            act.wait_ge(pv_done, HEADS * b + h - 1)
                        nc.scalar.copy(probsT[:, h % 2, :], turned.banks[n % 2][:, 0:SCORE_COLS])\
                            .then_inc(turned.emptied[n % 2], 1)
                for t in range(TPS):
                    n = OUT0 + t
                    turned.wait_full(act, b, n)
                    nc.scalar.copy(outT[:, :, t * P:(t + 1) * P],
                                   turned.banks[n % 2].rearrange("p (c n) -> p c n", c=C))\
                        .then_inc(turned.emptied[n % 2], 1)

        @block.tensor
        def _(pe):
            pe.wait_ge(weights_loaded, loads)
            pe.wait_ge(padded, 32)
            turned.open(pe)
            summed.open(pe)
            with pe.Fori(0, B) as b:
                ln.tensor(pe, b)
                for t in range(TPS):
                    ln.wait_xT(pe, b, t)
                    for j, (at, n) in enumerate(PIECES):
                        use = 2 * t + j
                        summed.wait_free(pe, b, use)
                        for c in range(C):
                            last = nc.tensor.matmul(summed.banks[use % 2][:, 0:n],
                                                    ln.xT[:, c, t * P:(t + 1) * P], w_qkv[:, c, at:at + n],
                                                    start=(c == 0), stop=(c == C - 1))
                        last.then_inc(summed.filled[use % 2], 1)
                for t in range(TPS):
                    for j in range(QU + KU):
                        n = LN_USES + t * (QU + KU) + j
                        if j == 0:
                            if rope:
                                pe.wait_ge(q_pad_ready, TPS * b + t + 1)
                            else:
                                summed.wait_empty(pe, b, 2 * t)
                        if j == QU:
                            if rope:
                                pe.wait_ge(kv_ready, (SLOTS + 1) * (TPS * b + t + 1))
                            else:
                                pe.wait_ge(kv_ready, SLOTS * (TPS * b + t + 1))
                        turned.wait_free(pe, b, n)
                        for g in range(4 if j < QU else KB):
                            if j < QU:
                                src = q_pad[:, t, SLOTS * (4 * j + g):SLOTS * (4 * j + g + 1), :]
                            else:
                                src = k_pad[:, t, KB * (j - QU) + g, :, :]
                            last = nc.tensor.transpose(turned.banks[n % 2][:, g * P:(g + 1) * P],
                                                       src.rearrange("p s d -> p (s d)"), ident[:, :])
                        last.then_inc(turned.filled[n % 2], 1)
                for k in range(2):
                    turned.wait_empty(pe, b, HEAD0 - 1 - k)

                def score(h):
                    g, s = divmod(h, SLOTS)
                    rows = slice(SLOT * s, SLOT * s + ROWS)
                    kg = g if rope else 0
                    if h >= 2:
                        pe.wait_ge(masked_ready, TPS * (HEADS * b + h - 1))
                    for t in range(TPS):
                        last = nc.tensor.matmul(scores[h % 2][:, SPAN[t]], qT[rows, g, t * P:(t + 1) * P],
                                                kT[rows, kg, 0:(t + 1) * P], start=True, stop=True)
                    last.then_inc(scores_filled, 1)

                def turn_probs(h):
                    n = HEAD0 + h
                    pe.wait_ge(probs_ready, TPS * (HEADS * b + h + 1))
                    turned.wait_free(pe, b, n)
                    for j in range(SCORE_COLS // P):
                        last = nc.tensor.transpose(turned.banks[n % 2][:, j * P:(j + 1) * P],
                                                   probs[:, h % 2, j * P:(j + 1) * P], ident[:, :])
                    last.then_inc(turned.filled[n % 2], 1)

                def weigh_values(h):
                    n = HEAD0 + h
                    kg = h // GROUP if rope else 0
                    turned.wait_empty(pe, b, n)
                    pT = probsT[:, h % 2, :]
                    cols = slice(HD * h, HD * (h + 1))
                    nc.tensor.matmul(heads_out[0][:, cols], pT[:, 0:P], v[:, 0, kg, :], start=True, stop=True)
                    nc.tensor.matmul(heads_out[1][:, cols], pT[:, P:2 * P], v[:, 0, kg, :], start=True, stop=False)
                    nc.tensor.matmul(heads_out[1][:, cols], pT[:, 2 * P:3 * P], v[:, 1, kg, :],
                                     start=False, stop=True).then_inc(pv_done, 1)

                if not rope:
                    summed.wait_empty(pe, b, 2 * TPS - 1)
                score(0)
                score(1)
                for h in range(HEADS):
                    turn_probs(h)
                    if h + 2 < HEADS:
                        score(h + 2)
                    if h >= 1:
                        weigh_values(h - 1)
                weigh_values(HEADS - 1)
                for t in range(TPS):
                    n = OUT0 + t
                    pe.wait_ge(out_ready, TPS * b + t + 1)
                    turned.wait_free(pe, b, n)
                    for c in range(C):
                        last = nc.tensor.transpose(
                            turned.banks[n % 2][:, c * P:(c + 1) * P],
                            out[:, t, :, :].rearrange("p h d -> p (h d)")[:, c * P:(c + 1) * P], ident[:, :])
                    last.then_inc(turned.filled[n % 2], 1)
                for t in range(TPS):
                    n, use = OUT0 + t, 2 * TPS + t
                    turned.wait_empty(pe, b, n)
                    summed.wait_free(pe, b, use)
                    for c in range(C):
                        last = nc.tensor.matmul(summed.banks[use % 2][:, :], outT[:, c, t * P:(t + 1) * P],
                                                w_o[:, c, :], start=(c == 0), stop=(c == C - 1))
                    last.then_inc(summed.filled[use % 2], 1)


class Bank:

    def __init__(self, layer, name, lead, body, last, rounds):
        self.tile = layer.bank(name)
        self.filled = layer.sem(f"{name}_filled")
        self.emptied = layer.sem(f"{name}_emptied")
        self.order = {"lead": lead, "body": body, "last": last}
        self.start = {"lead": lambda r: 0, "body": lambda r: len(lead) + len(body) * r,
                      "last": lambda r: len(lead) + len(body) * rounds}

    def before(self, step, use):
        phase, r = step
        return self.start[phase](r) + self.order[phase].index(use)

    def wait_free(self, pe, step, use):
        pe.wait_ge(self.emptied, 1 + self.before(step, use))

    def open(self, pe):
        pe.sem_inc(self.emptied, 1)

    def wait_full(self, eng, step, use):
        eng.wait_ge(self.filled, self.before(step, use) + 1)

    def wait_empty(self, eng, step, use):
        eng.wait_ge(self.emptied, 1 + self.before(step, use) + 1)


def normalise_all(core, name, xT_all):
    with ExitStack() as ctx:
        L = Layer(core, ctx, f"{name}_norm")
        turned = Ring(L, "turned", TPS)
        ln = LayerNorm(L, turned)
        block = ctx.enter_context(core.nc.Block())

        @block.vector
        def _(dve):
            with dve.Fori(0, B) as b:
                ln.vector(dve, b)

        @block.scalar
        def _(act):
            with act.Fori(0, B) as b:
                ln.scalar(act, b)
                ln.scalar_xT(act, b, xT_all[:, b, :, :])

        @block.tensor
        def _(pe):
            turned.open(pe)
            with pe.Fori(0, B) as b:
                ln.tensor(pe, b)


def wide_attention(core, name, linear):
    nc, dram, X, ident = core.nc, core.dram, core.X, core.ident
    HD = 128
    UNITS = KV_HEADS * B
    QN = GROUP * HD
    RN = QN + HD
    QKV = RN + HD
    BLK = 32
    NB = S // BLK
    BPT = P // BLK
    ROUNDS = UNITS - 1

    with ExitStack() as ctx:
        xT_all = ctx.enter_context(nc.sbuf_tensor(f"{name}_xT_all", [P, B, C, S], F32))
        normalise_all(core, name, xT_all)
        L = Layer(core, ctx, name)
        lin = linear
        summed = [Bank(L, "summed0", ["q0", "kv"], ["q0", "kv", "wo1"], ["wo1"], ROUNDS),
                  Bank(L, "summed1", ["q1"], ["q1", "wo0"], ["wo0"], ROUNDS)]
        if lin:
            turned = [Bank(L, "turned0", ["q0", "k", "qs0"], ["P0", "P2", "q0", "k", "qs0"], ["P0", "P2"], ROUNDS),
                      Bank(L, "turned1", ["kk", "q1", "qs1"], ["P1", "P3", "kk", "q1", "qs1"], ["P1", "P3"], ROUNDS)]
            scores = [Bank(L, "scores0", [], ["S0", "S2", "G0", "G2"], ["S0", "S2", "G0", "G2"], ROUNDS),
                      Bank(L, "scores1", [], ["S1", "S3", "G1"], ["S1", "S3", "G1"], ROUNDS)]
        else:
            turned = [Bank(L, "turned0", ["q0", "k"], ["P0", "P2", "q0", "k"], ["P0", "P2"], ROUNDS),
                      Bank(L, "turned1", ["q1"], ["P1", "P3", "q1"], ["P1", "P3"], ROUNDS)]
            scores = [Bank(L, "scores0", [], ["S0", "S2"], ["S0", "S2"], ROUNDS),
                      Bank(L, "scores1", [], ["S1", "S3"], ["S1", "S3"], ROUNDS)]
        heads = [L.bank(f"heads{t}") for t in range(TPS)]

        w_in = L.sb("w_in", [P, 2, C, QKV])
        w_o = L.sb("w_o", [P, 2, GROUP, D])
        xT = L.sb("xT", [P, C, S])
        cos = L.sb("cos", [P, TPS, RN])
        sin = L.sb("sin", [P, TPS, RN])
        qkv = L.sb("qkv", [P, TPS, QKV])
        straight = L.sb("straight", [P, TPS, RN])
        crossed = L.sb("crossed", [P, TPS, RN])
        v = L.sb("v", [P, TPS, HD])
        qT = L.sb("qT", [P, TPS, GROUP, P])
        kT = L.sb("kT", [P, S])
        masked = L.sb("masked", [P, 2, SCORE_COLS])
        neg_max = L.sb("neg_max", [P, GROUP, TPS])
        total = L.sb("total", [P, GROUP, TPS])
        r_total = L.sb("r_total", [P, GROUP, TPS])
        probs = L.sb("probs", [P, 2, SCORE_COLS])
        probsT = L.sb("probsT", [P, 2, SCORE_COLS])
        outT = L.sb("outT", [P, TPS, GROUP, P])
        if lin:
            mask = L.sb("mask", [P, SCORE_COLS])
            half_mask = L.sb("half_mask", [P, BPT, GROUP * BLK])
            out_bf = L.sb("out_bf", [P, TPS, GROUP, P], BF16)
            neg_kq_max = L.sb("neg_kq_max", [P, TPS, GROUP + 1])
            kq_total = L.sb("kq_total", [P, TPS, GROUP + 1])
            r_kq_total = L.sb("r_kq_total", [P, TPS, GROUP])
            log_k_total = L.sb("log_k_total", [P, TPS])
            kq_exp = L.sb("kq_exp", [P, TPS, RN])
            qs = L.sb("qs", [P, TPS, QN])
            log_ks = L.sb("log_ks", [P, TPS, HD])
            kk = L.sb("kk", [P, 2, S])
            min_k = L.sb("min_k", [P, S])
            neg_abs_k = L.sb("neg_abs_k", [P, S])
            exp_abs_k = L.sb("exp_abs_k", [P, S])
            soft = L.sb("soft", [P, S])
            G = L.sb("G", [P, S])
            R = L.sb("R", [P, NB])
            key_log = L.sb("key_log", [P, S])
            decay_log = L.sb("decay_log", [P, S])
            decay = L.sb("decay", [P, S])
            qf = L.sb("qf", [P, GROUP, S])
            kf = [L.sb(f"kf{n}", [P, BPT, P]) for n in range(3)]
            A = [L.sb(f"A{n}", [P, BPT, GROUP * BLK]) for n in range(3)]
        else:
            mask = core.mask

        weights_loaded = L.sem("weights_loaded")
        heads_emptied = L.sem("heads_emptied")
        tables_loaded = L.sem("tables_loaded")
        xT_ready = L.sem("xT_ready")
        v_ready = L.sem("v_ready")
        rope_parts = L.sem("rope_parts")
        rope_ready = L.sem("rope_ready")
        exp_ready = L.sem("exp_ready")
        r_total_ready = L.sem("r_total_ready")
        probs_ready = L.sem("probs_ready")
        probs_scaled = L.sem("probs_scaled")
        masked_ready = L.sem("masked_ready")
        pv_done = L.sem("pv_done")
        out_f32 = L.sem("out_f32")
        if lin:
            zeroed = L.sem("zeroed")
            max_ready = L.sem("kq_max_ready")
            kq_exp_ready = L.sem("kq_exp_ready")
            log_total_ready = L.sem("log_total_ready")
            r_kq_ready = L.sem("r_kq_ready")
            log_ks_ready = L.sem("log_ks_ready")
            qs_ready = L.sem("qs_ready")
            min_ready = L.sem("min_ready")
            abs_ready = L.sem("abs_ready")
            exp_abs_ready = L.sem("exp_abs_ready")
            soft_ready = L.sem("soft_ready")
            G_ready = L.sem("G_ready")
            R_ready = L.sem("R_ready")
            decay_log_ready = L.sem("decay_log_ready")
            decay_ready = L.sem("decay_ready")
            kf_ready = L.sem("kf_ready")
            linear_kept = [L.sem(f"linear_kept{k}") for k in range(2)]
            linear_done = L.sem("linear_done")
        block = ctx.enter_context(nc.Block())

        def wait_heads(eng, u):
            if lin:
                eng.wait_ge(linear_done, u + 1)
            else:
                eng.wait_ge(pv_done, GROUP * (u + 1))

        def wait_projected(eng, u):
            summed[0].wait_full(eng, ("body", u), "wo1")

        @block.sync
        def _(sp):
            sp.dma_start(cos[:, :, :], dram["wide_cos"]).then_inc(tables_loaded, 16)
            sp.dma_start(sin[:, :, :], dram["wide_sin"]).then_inc(tables_loaded, 16)
            if lin:
                sp.dma_start(mask[:, :], dram["window_mask"]).then_inc(tables_loaded, 16)
                sp.dma_start(half_mask[:, :, :], dram["half_mask"]).then_inc(tables_loaded, 16)

            def load(g):
                k = g % 2
                sp.dma_start(w_in[:, k, :, :], dram[f"{name}_w_in"][g, :, :].rearrange("(c p) n -> p c n", p=P))\
                    .then_inc(weights_loaded, 16)
                sp.dma_start(w_o[:, k, :, :], dram[f"{name}_w_o"][g, :, :].rearrange("(h p) n -> p h n", p=P))\
                    .then_inc(weights_loaded, 16)

            load(0)
            with sp.Fori(1, KV_HEADS) as g:
                sp.wait_ge(weights_loaded, 32 * g)
                wait_projected(sp, B * (g - 1) - 1)
                load(g)

        tables = 16 * (4 if lin else 2)

        @block.gpsimd
        def _(pool):
            if lin:
                for n in (0, 2):
                    nc.gpsimd.memset(kf[n][:, :, :], 0.0).then_inc(zeroed, 1)

            def copy_xT(u, b):
                nc.gpsimd.tensor_copy(xT[:, :, :], xT_all[:, b, :, :]).then_inc(xT_ready, 1)

            def copy_v(step, u):
                summed[0].wait_empty(pool, step, "kv")
                core.carry_wait(pool)
                nc.gpsimd.tensor_copy(v[:, :, :], qkv[:, :, RN:QKV]).then_inc(v_ready, 1)

            def round_out(u):
                for t in range(TPS):
                    pool.wait_ge(heads_emptied, 1 + TPS * u + t + 1)
                    if t == 0:
                        wait_projected(pool, u - 1)
                    core.carry_wait(pool)
                    nc.gpsimd.tensor_copy(outT[:, t, :, :], out_bf[:, t, :, :]).then_inc(out_f32, 1)

            if lin:
                pool.sem_inc(out_f32, 1)
            copy_xT(0, 0)
            copy_v(("lead", 0), 0)
            summed[0].wait_full(pool, ("lead", 0), "kv")
            copy_xT(1, 1)
            with pool.Fori(0, ROUNDS) as u:
                summed[0].wait_full(pool, ("body", u), "kv")
                core.carry_wait(pool)
                copy_xT(u + 2, (u + 2) % B)
                wait_heads(pool, u)
                copy_v(("body", u), u + 1)
                if lin:
                    round_out(u)
            if lin:
                round_out(ROUNDS)

        @block.vector
        def _(dve):
            dve.wait_ge(tables_loaded, tables)

            def rope(w):
                for t in range(TPS):
                    nc.vector.tensor_tensor(straight[:, t, :], qkv[:, t, 0:RN], cos[:, t, :], ALU.mult)\
                        .then_inc(rope_parts, 1)
                    src = qkv[:, t, 0:RN].rearrange("p (h e d) -> p h e d", e=2, d=HD // 2)
                    dst = crossed[:, t, :].rearrange("p (h e d) -> p h e d", e=2, d=HD // 2)
                    sn = sin[:, t, :].rearrange("p (h e d) -> p h e d", e=2, d=HD // 2)
                    for e in range(2):
                        nc.vector.tensor_tensor(dst[:, :, e, :], src[:, :, 1 - e, :], sn[:, :, e, :], ALU.mult)\
                            .then_inc(rope_parts, 1)
                for t in range(TPS):
                    dve.wait_ge(rope_parts, 3 * (TPS * w + t + 1))
                    nc.vector.tensor_tensor(straight[:, t, :], straight[:, t, :], crossed[:, t, :], ALU.add)\
                        .then_inc(rope_ready, 1)

            def prepare(step, w):
                summed[0].wait_empty(dve, step, "q0")
                summed[1].wait_empty(dve, step, "q1")
                summed[0].wait_empty(dve, step, "kv")
                if lin:
                    for t in range(TPS):
                        nc.vector.tensor_reduce(neg_kq_max[:, t, :],
                                                qkv[:, t, 0:RN].rearrange("p (h d) -> p h d", d=HD),
                                                AX.X, ALU.max, negate=True).then_inc(max_ready, 1)
                rope(w)
                if lin:
                    for t in range(TPS):
                        dve.wait_ge(log_total_ready, w + 1)
                        nc.vector.tensor_scalar(log_ks[:, t, :], qkv[:, t, QN:RN], neg_kq_max[:, t, GROUP:GROUP + 1],
                                                log_k_total[:, t:t + 1], ALU.add, ALU.subtract)\
                            .then_inc(log_ks_ready, 1)
                    dve.wait_ge(kq_exp_ready, TPS * (GROUP + 1) * (w + 1))
                    nc.vector.reciprocal(r_kq_total[:, :, :], kq_total[:, :, 0:GROUP]).then_inc(r_kq_ready, 1)
                    dve.wait_ge(r_kq_ready, w + 1)
                    for t in range(TPS):
                        nc.vector.tensor_tensor(qs[:, t, :].rearrange("p (h d) -> p h d", d=HD),
                                                kq_exp[:, t, 0:QN].rearrange("p (h d) -> p h d", d=HD),
                                                r_kq_total[:, t, :].unsqueeze(2).to_broadcast([P, GROUP, HD]),
                                                ALU.mult).then_inc(qs_ready, 1)

            def decays(step, w):
                turned[1].wait_empty(dve, step, "kk")
                k, log_k = kk[:, 0, :], kk[:, 1, :]
                nc.vector.tensor_scalar(min_k[:, :], k, 0.0, None, ALU.min).then_inc(min_ready, 1)
                dve.wait_ge(min_ready, w + 1)
                nc.vector.scalar_tensor_tensor(neg_abs_k[:, :], min_k[:, :], 2.0, k, ALU.mult, ALU.subtract)\
                    .then_inc(abs_ready, 1)
                dve.wait_ge(soft_ready, w + 1)
                nc.vector.tensor_tensor_scan(G[:, :], min_k[:, :], soft[:, :], 0.0, ALU.add, ALU.subtract)\
                    .then_inc(G_ready, 1)
                dve.wait_ge(G_ready, w + 1)
                nc.vector.tensor_scalar(R[:, :], G[:, BLK // 2 - 1:S:BLK], 1.0 / 16, None, ALU.mult)\
                    .then_inc(R_ready, 1)
                nc.vector.scalar_tensor_tensor(key_log[:, :], G[:, :], -1.0 / 16, log_k, ALU.mult, ALU.add)\
                    .then_inc(R_ready, 1)
                nc.vector.tensor_tensor(decay_log[:, :].rearrange("p (n s) -> p n s", s=BLK),
                                        G[:, :].rearrange("p (n s) -> p n s", s=BLK),
                                        G[:, BLK // 2 - 1:S:BLK].unsqueeze(2).to_broadcast([P, NB, BLK]),
                                        ALU.subtract).then_inc(decay_log_ready, 1)

            def decayed_queries(step, w):
                dve.wait_ge(decay_ready, w + 1)
                for t in range(TPS):
                    turned[t].wait_full(dve, step, f"qs{t}")
                    nc.vector.tensor_tensor(qf[:, :, t * P:(t + 1) * P],
                                            turned[t].tile.rearrange("p (h n) -> p h n", h=GROUP),
                                            decay[:, t * P:(t + 1) * P].unsqueeze(1).to_broadcast([P, GROUP, P]),
                                            ALU.mult).then_inc(turned[t].emptied, 1)

            def mask_scores(step, u, h):
                k = h % 2
                scores[k].wait_full(dve, step, f"S{h}")
                core.carry_wait(dve)
                if h >= 2:
                    dve.wait_ge(exp_ready, TPS * (GROUP * u + h - 1))
                    core.carry_wait(dve)
                for t in range(TPS):
                    ins = nc.vector.tensor_tensor_reduce(masked[:, k, SPAN[t]], scores[k].tile[:, SPAN[t]],
                                                         mask[:, SPAN[t]], 1.0, 3e38, ALU.add, ALU.min,
                                                         neg_max[:, h, t:t + 1])
                    ins.then_inc(masked_ready, 1)

            def scale_probs(u, h):
                k = h % 2
                dve.wait_ge(exp_ready, TPS * (GROUP * u + h + 1))
                nc.vector.reciprocal(r_total[:, h, :], total[:, h, :]).then_inc(r_total_ready, 1)
                dve.wait_ge(r_total_ready, GROUP * u + h + 1)
                for t in range(TPS):
                    nc.vector.tensor_scalar(probs[:, k, SPAN[t]], probs[:, k, SPAN[t]], r_total[:, h, t:t + 1],
                                            0.5 if lin else 1.0, ALU.mult, ALU.mult).then_inc(probs_scaled, 1)

            def keep_linear(step, n):
                k = scores[n % 2]
                k.wait_full(dve, step, f"G{n}")
                nc.vector.tensor_tensor(A[n][:, :, :], k.tile.rearrange("p (i m) -> p i m", i=BPT),
                                        half_mask[:, :, :], ALU.mult).then_inc(linear_kept[0], 1)

            def attend(step, u):
                mask_scores(step, u, 0)
                mask_scores(step, u, 1)
                for h in range(GROUP):
                    scale_probs(u, h)
                    if h + 2 < GROUP:
                        mask_scores(step, u, h + 2)
                if lin:
                    keep_linear(step, 0)
                    keep_linear(step, 2)

            def add_out(step, b):
                for t in range(TPS):
                    k = summed[1 - t]
                    k.wait_full(dve, step, f"wo{t}")
                    nc.vector.tensor_tensor(X[:, TPS * b + t, :], X[:, TPS * b + t, :], k.tile[:, :], ALU.add)\
                        .then_inc(k.emptied, 1)

            prepare(("lead", 0), 0)
            if lin:
                decays(("lead", 0), 0)
                decayed_queries(("lead", 0), 0)
            with dve.Fori(0, ROUNDS) as u:
                attend(("body", u), u)
                prepare(("body", u), u + 1)
                add_out(("body", u), u % B)
                if lin:
                    decays(("body", u), u + 1)
                    decayed_queries(("body", u), u + 1)
            attend(("last", 0), ROUNDS)
            add_out(("last", 0), ROUNDS % B)

        @block.scalar
        def _(act):
            def take_q(step, w, t):
                k = summed[t]
                k.wait_full(act, step, f"q{t}")
                if w is not None:
                    act.wait_ge(rope_ready, TPS * w)
                    if lin:
                        act.wait_ge(kq_exp_ready, TPS * (GROUP + 1) * w)
                nc.scalar.copy(qkv[:, t, 0:QN], k.tile[:, :]).then_inc(k.emptied, 1)

            def take_kv(step, w):
                summed[0].wait_full(act, step, "kv")
                if w is not None:
                    act.wait_ge(v_ready, w)
                    if lin:
                        act.wait_ge(log_ks_ready, TPS * w)
                nc.scalar.copy(qkv[:, :, QN:QKV], summed[0].tile.rearrange("p (t n) -> p t n", t=TPS))\
                    .then_inc(summed[0].emptied, 1)

            def softmax_qk(w):
                for t in range(TPS):
                    act.wait_ge(max_ready, TPS * w + t + 1)
                    for h in reversed(range(GROUP + 1)):
                        cols = slice(HD * h, HD * (h + 1))
                        nc.scalar.activation(kq_exp[:, t, cols], qkv[:, t, cols], ACT.Exp,
                                             bias=neg_kq_max[:, t, h:h + 1], accum_out=kq_total[:, t, h:h + 1])\
                            .then_inc(kq_exp_ready, 1)
                act.wait_ge(kq_exp_ready, TPS * (GROUP + 1) * (w + 1))
                nc.scalar.activation(log_k_total[:, :], kq_total[:, :, GROUP], ACT.Ln).then_inc(log_total_ready, 1)

            def turn_in(step, w):
                if lin:
                    turned[1].wait_full(act, step, "kk")
                    nc.scalar.copy(kk[:, :, :], turned[1].tile.rearrange("p (a n) -> p a n", a=2))\
                        .then_inc(turned[1].emptied, 1)
                    act.wait_ge(abs_ready, w + 1)
                    nc.scalar.activation(exp_abs_k[:, :], neg_abs_k[:, :], ACT.Exp).then_inc(exp_abs_ready, 1)
                    act.wait_ge(exp_abs_ready, w + 1)
                    nc.scalar.activation(soft[:, :], exp_abs_k[:, :], ACT.Ln, bias=core.one[:, 0:1])\
                        .then_inc(soft_ready, 1)
                for t in range(TPS):
                    turned[t].wait_full(act, step, f"q{t}")
                    nc.scalar.copy(qT[:, t, :, :], turned[t].tile.rearrange("p (h n) -> p h n", h=GROUP))\
                        .then_inc(turned[t].emptied, 1)
                turned[0].wait_full(act, step, "k")
                nc.scalar.copy(kT[:, :], turned[0].tile[:, 0:S]).then_inc(turned[0].emptied, 1)
                if lin:
                    act.wait_ge(decay_log_ready, w + 1)
                    nc.scalar.activation(decay[:, :], decay_log[:, :], ACT.Exp, scale=1.0 / 16)\
                        .then_inc(decay_ready, 1)
                    act.wait_ge(R_ready, 2 * (w + 1))
                    act.wait_ge(zeroed, 2)
                    for n, (block0, key0) in enumerate(((0, 0), (BPT, 0), (BPT, P))):
                        for i in range(BPT):
                            cols = P if n == 1 else BLK * (i + 1)
                            nc.scalar.activation(kf[n][:, i, 0:cols], key_log[:, key0:key0 + cols], ACT.Exp,
                                                 bias=R[:, block0 + i:block0 + i + 1]).then_inc(kf_ready, 1)

            def exponentials(u, h):
                k = h % 2
                for t in range(TPS):
                    act.wait_ge(masked_ready, TPS * (GROUP * u + h) + t + 1)
                    nc.scalar.activation(probs[:, k, SPAN[t]], masked[:, k, SPAN[t]], ACT.Exp,
                                         bias=neg_max[:, h, t:t + 1], scale=-1.0,
                                         accum_out=total[:, h, t:t + 1]).then_inc(exp_ready, 1)

            def take_probsT(step, u, h):
                k = h % 2
                turned[k].wait_full(act, step, f"P{h}")
                if h >= 2:
                    act.wait_ge(pv_done, GROUP * u + h - 1)
                nc.scalar.copy(probsT[:, k, :], turned[k].tile[:, 0:SCORE_COLS]).then_inc(turned[k].emptied, 1)

            def take_out(u):
                wait_heads(act, u)
                if lin:
                    act.wait_ge(out_f32, 1 + TPS * u)
                else:
                    wait_projected(act, u - 1)
                for t in range(TPS):
                    nc.scalar.copy((out_bf if lin else outT)[:, t, :, :],
                                   heads[t].rearrange("p (h n) -> p h n", h=GROUP)).then_inc(heads_emptied, 1)

            def attend(step, u, more):
                exponentials(u, 0)
                exponentials(u, 1)
                if more:
                    take_q(step, u + 1, 0)
                take_probsT(step, u, 0)
                exponentials(u, 2)
                if more:
                    take_q(step, u + 1, 1)
                take_probsT(step, u, 1)
                exponentials(u, 3)
                if more:
                    take_kv(step, u + 1)
                take_probsT(step, u, 2)
                take_probsT(step, u, 3)
                if lin:
                    scores[1].wait_full(act, step, "G1")
                    nc.scalar.mul(A[1][:, :, :], scores[1].tile.rearrange("p (i m) -> p i m", i=BPT), 0.5)\
                        .then_inc(linear_kept[1], 1)
                take_out(u)
                if more and lin:
                    softmax_qk(u + 1)
                if more:
                    turn_in(step, u + 1)

            lead = ("lead", 0)
            take_q(lead, None, 0)
            take_q(lead, None, 1)
            take_kv(lead, None)
            if lin:
                softmax_qk(0)
            turn_in(lead, 0)
            with act.Fori(0, ROUNDS) as u:
                attend(("body", u), u, True)
            attend(("last", 0), ROUNDS, False)

        @block.tensor
        def _(pe):
            def weights(w):
                return w // B % 2

            def project_q(step, w, g2, t):
                k = summed[t]
                if t == 0:
                    pe.wait_ge(xT_ready, w + 1)
                    pe.wait_ge(weights_loaded, 32 * (w // B + 1))
                k.wait_free(pe, step, f"q{t}")
                for c in range(C):
                    last = nc.tensor.matmul(k.tile[:, :], xT[:, c, t * P:(t + 1) * P], w_in[:, g2, c, 0:QN],
                                            start=(c == 0), stop=(c == C - 1))
                last.then_inc(k.filled, 1)

            def project_kv(step, w, g2):
                k = summed[0]
                k.wait_free(pe, step, "kv")
                for t in range(TPS):
                    for c in range(C):
                        last = nc.tensor.matmul(k.tile[:, t * 2 * HD:(t + 1) * 2 * HD],
                                                xT[:, c, t * P:(t + 1) * P], w_in[:, g2, c, QN:QKV],
                                                start=(c == 0), stop=(c == C - 1))
                last.then_inc(k.filled, 1)

            def turn_in(step, w):
                if lin:
                    turned[1].wait_free(pe, step, "kk")
                    pe.wait_ge(log_ks_ready, TPS * (w + 1))
                    for a in range(2):
                        for t in range(TPS):
                            src = qkv[:, t, QN:RN] if a == 0 else log_ks[:, t, :]
                            last = nc.tensor.transpose(turned[1].tile[:, a * S + t * P:a * S + (t + 1) * P],
                                                       src, ident[:, :])
                    last.then_inc(turned[1].filled, 1)
                for t in range(TPS):
                    pe.wait_ge(rope_ready, TPS * w + t + 1)
                    turned[t].wait_free(pe, step, f"q{t}")
                    for h in range(GROUP):
                        last = nc.tensor.transpose(turned[t].tile[:, h * P:(h + 1) * P],
                                                   straight[:, t, h * HD:(h + 1) * HD], ident[:, :])
                    last.then_inc(turned[t].filled, 1)
                turned[0].wait_free(pe, step, "k")
                for t in range(TPS):
                    last = nc.tensor.transpose(turned[0].tile[:, t * P:(t + 1) * P], straight[:, t, QN:RN],
                                               ident[:, :])
                last.then_inc(turned[0].filled, 1)
                if lin:
                    for t in range(TPS):
                        pe.wait_ge(qs_ready, TPS * w + t + 1)
                        turned[t].wait_free(pe, step, f"qs{t}")
                        for h in range(GROUP):
                            last = nc.tensor.transpose(turned[t].tile[:, h * P:(h + 1) * P],
                                                       qs[:, t, h * HD:(h + 1) * HD], ident[:, :])
                        last.then_inc(turned[t].filled, 1)

            def score(step, u, h):
                k = scores[h % 2]
                if h >= 2:
                    pe.wait_ge(masked_ready, TPS * (GROUP * u + h - 1))
                for t in range(TPS):
                    last = nc.tensor.matmul(k.tile[:, SPAN[t]], qT[:, t, h, :], kT[:, 0:(t + 1) * P],
                                            start=True, stop=True)
                last.then_inc(k.filled, 1)

            def turn_probs(step, u, h):
                k = turned[h % 2]
                pe.wait_ge(probs_scaled, TPS * (GROUP * u + h + 1))
                k.wait_free(pe, step, f"P{h}")
                for j in range(SCORE_COLS // P):
                    last = nc.tensor.transpose(k.tile[:, j * P:(j + 1) * P], probs[:, h % 2, j * P:(j + 1) * P],
                                               ident[:, :])
                last.then_inc(k.filled, 1)

            def weigh(step, u, h):
                turned[h % 2].wait_empty(pe, step, f"P{h}")
                pT = probsT[:, h % 2, :]
                if h == 0:
                    pe.wait_ge(v_ready, u + 1)
                    pe.wait_ge(heads_emptied, 1 + TPS * u)
                cols = slice(h * P, (h + 1) * P)
                end = not lin
                nc.tensor.matmul(heads[0][:, cols], v[:, 0, :], pT[:, 0:P], start=(h == 0), stop=end,
                                 skip_group_check=True)
                nc.tensor.matmul(heads[1][:, cols], v[:, 0, :], pT[:, P:2 * P], start=(h == 0), stop=False,
                                 skip_group_check=True)
                nc.tensor.matmul(heads[1][:, cols], v[:, 1, :], pT[:, 2 * P:3 * P], start=False, stop=end,
                                 skip_group_check=True).then_inc(pv_done, 1)

            def linear_scores(step, u, n):
                k = scores[n % 2]
                if n == 0:
                    pe.wait_ge(kf_ready, 3 * BPT * (u + 1))
                    pe.wait_ge(masked_ready, TPS * (GROUP * u + 3))
                elif n == 1:
                    pe.wait_ge(masked_ready, TPS * (GROUP * u + 4))
                else:
                    pe.wait_ge(linear_kept[0], 2 * u + 1)
                block0 = 0 if n == 0 else BPT
                for i in range(BPT):
                    at = BLK * (block0 + i)
                    last = nc.tensor.matmul(k.tile[:, i * P:(i + 1) * P], kf[n][:, i, :], qf[:, :, at:at + BLK],
                                            start=True, stop=True)
                last.then_inc(k.filled, 1)

            def linear_values(u, n):
                pe.wait_ge(linear_kept[n % 2], {0: 2 * u + 1, 1: u + 1, 2: 2 * u + 2}[n])
                out = heads[0 if n == 0 else 1].rearrange("p (h n) -> p h n", h=GROUP)
                for i in range(BPT):
                    last = nc.tensor.matmul(out[:, :, BLK * i:BLK * (i + 1)], v[:, n // 2, :],
                                            A[n][:, i, :].rearrange("p (h s) -> p h s", h=GROUP),
                                            start=False, stop=(n != 1), skip_group_check=True)
                if n == 2:
                    last.then_inc(linear_done, 1)

            def project_out(step, u, g2):
                for t in range(TPS):
                    k = summed[1 - t]
                    if lin:
                        pe.wait_ge(out_f32, 1 + TPS * u + t + 1)
                    else:
                        pe.wait_ge(heads_emptied, 1 + TPS * u + t + 1)
                    k.wait_free(pe, step, f"wo{t}")
                    for h in range(GROUP):
                        last = nc.tensor.matmul(k.tile[:, :], outT[:, t, h, :], w_o[:, g2, h, :],
                                                start=(h == 0), stop=(h == GROUP - 1))
                    last.then_inc(k.filled, 1)

            def attend(step, u, more):
                g2 = weights(u + 1) if more else None
                arrived = ("body", u - 1)
                turned[0].wait_empty(pe, arrived, "q0")
                turned[1].wait_empty(pe, arrived, "q1")
                turned[0].wait_empty(pe, arrived, "k")
                score(step, u, 0)
                score(step, u, 1)
                if more:
                    project_q(step, u + 1, g2, 0)
                turn_probs(step, u, 0)
                score(step, u, 2)
                if more:
                    project_q(step, u + 1, g2, 1)
                turn_probs(step, u, 1)
                weigh(step, u, 0)
                score(step, u, 3)
                if more:
                    project_kv(step, u + 1, g2)
                turn_probs(step, u, 2)
                weigh(step, u, 1)
                if lin:
                    turned[0].wait_empty(pe, arrived, "qs0")
                    turned[1].wait_empty(pe, arrived, "qs1")
                    linear_scores(step, u, 0)
                    linear_scores(step, u, 1)
                turn_probs(step, u, 3)
                weigh(step, u, 2)
                if lin:
                    linear_scores(step, u, 2)
                weigh(step, u, 3)
                if lin:
                    linear_values(u, 0)
                    linear_values(u, 1)
                    linear_values(u, 2)
                project_out(step, u, weights(u))
                if more:
                    turn_in(step, u + 1)

            for k in summed + turned:
                k.open(pe)
            pe.sem_inc(heads_emptied, 1)
            lead = ("lead", 0)
            project_q(lead, 0, 0, 0)
            project_q(lead, 0, 0, 1)
            project_kv(lead, 0, 0)
            turn_in(lead, 0)
            with pe.Fori(0, ROUNDS) as u:
                attend(("body", u), u, True)
            attend(("last", 0), ROUNDS, False)


def routed_ffn(core, name, experts, rank, mode):
    nc, dram, X, ident = core.nc, core.dram, core.X, core.ident
    E, ER = experts, experts * rank
    RC = E + ER
    bias = mode != "top1"
    logit_bias = mode != "top2"
    T_USES = 2 * TPS
    R_USES = 2 * TPS if mode == "sequence" else TPS

    with ExitStack() as ctx:
        L = Layer(core, ctx, name)
        turned = Ring(L, "turned", T_USES)
        routed = Ring(L, "routed", R_USES)
        summed = Ring(L, "summed", TPS)
        ln = LayerNorm(L, turned)
        w = L.sb("w", [P, C, D])
        w_ra = L.sb("w_ra", [P, C, RC])
        w_b = L.sb("w_b", [ER, D])
        if bias:
            b_out = L.sb("b_out", [P, D])
        if logit_bias:
            b_logit = L.sb("b_logit", [P, E])
        if mode == "sequence":
            mean_rows = L.sb("mean_rows", [P, TPS, P])
        KEYS = max(8, E)
        logits = L.sb("logits", [P, TPS, KEYS])
        za = L.sb("za", [P, TPS, ER])
        top = L.sb("top", [P, TPS, 8])
        top_at = L.sb("top_at", [P, TPS, 8], U32)
        top_atf = L.sb("top_atf", [P, TPS, 8])
        iota = L.sb("iota", [P, E])
        expd = L.sb("expd", [P, TPS, 8])
        total = L.sb("total", [P, TPS])
        r_total = L.sb("r_total", [P, TPS])
        p2 = L.sb("p2", [P, TPS])
        weight = L.sb("weight", [P, TPS, E])
        weight2 = L.sb("weight2", [P, TPS, E])
        zw = L.sb("zw", [P, TPS, ER])
        zwT = L.sb("zwT", [P, TPS, P])

        weights_loaded = L.sem("weights_loaded")
        logits_ready = L.sem("logits_ready")
        za_ready = L.sem("za_ready")
        step = L.sem("routing_step")
        expd_ready = L.sem("expd_ready")
        max_ready = L.sem("max_ready")
        zw_ready = L.sem("zw_ready")
        bias_added = L.sem("bias_added")
        n_loads = 4 + bias + logit_bias + (mode == "sequence")
        block = ctx.enter_context(nc.Block())

        @block.sync
        def _(sp):
            sp.dma_start(w[:, :, :], dram[f"{name}_w"].rearrange("(c p) n -> p c n", p=P)).then_inc(weights_loaded, 16)
            sp.dma_start(w_ra[:, :, 0:E], dram[f"{name}_router"].rearrange("(c p) n -> p c n", p=P),
                         allow_slow_non_contiguous=True).then_inc(weights_loaded, 16)
            sp.dma_start(w_ra[:, :, E:RC], dram[f"{name}_A"].rearrange("(c p) n -> p c n", p=P)).then_inc(weights_loaded, 16)
            sp.dma_start(w_b[:, :], dram[f"{name}_B"]).then_inc(weights_loaded, 16)
            if bias:
                sp.dma_start(b_out[:, :], dram[f"{name}_b"].partition_broadcast(P)).then_inc(weights_loaded, 16)
            if logit_bias:
                sp.dma_start(b_logit[:, :], dram[f"{name}_router_b"].partition_broadcast(P))\
                    .then_inc(weights_loaded, 16)
            if mode == "sequence":
                sp.dma_start(mean_rows[:, :, :], dram["mean_rows"]).then_inc(weights_loaded, 16)

        def apply_weights(dve, t):
            nc.vector.tensor_tensor(zw[:, t, :].rearrange("p (e r) -> p e r", e=E),
                                    za[:, t, :].rearrange("p (e r) -> p e r", e=E),
                                    weight[:, t, :].unsqueeze(2).to_broadcast([P, E, rank]),
                                    ALU.mult).then_inc(zw_ready, 1)

        @block.gpsimd
        def _(pool):
            if bias:
                pool.wait_ge(weights_loaded, 16 * n_loads)
                with pool.Fori(0, B) as b:
                    for t in range(TPS):
                        pool.wait_ge(ln.xn_ready, TPS * b + t + 1)
                        nc.gpsimd.tensor_tensor(X[:, TPS * b + t, :], X[:, TPS * b + t, :], b_out[:, :], ALU.add)\
                            .then_inc(bias_added, 1)

        @block.vector
        def _(dve):
            dve.wait_ge(weights_loaded, 16 * n_loads)
            if mode != "sequence":
                for e in range(E):
                    nc.vector.memset(iota[:, e:e + 1], float(e)).then_inc(step, 1)
                nc.vector.memset(logits[:, :, :], -3e38).then_inc(step, 1)
                base = E + 1
                dve.wait_ge(step, base)
            else:
                base = 0
            with dve.Fori(0, B) as b:
                count = [0]
                per = {"sequence": 6, "top1": 4 * TPS, "top2": 10 * TPS}[mode]

                def stepped(ins):
                    count[0] += 1
                    ins.then_inc(step, 1)
                    dve.wait_ge(step, base + b * per + count[0])

                ln.vector(dve, b)
                for t in range(TPS):
                    routed.wait_full(dve, b, t)
                    src = routed.banks[t]
                    if mode == "sequence":
                        nc.vector.tensor_copy(logits[:, t, 0:E], src[:, 0:E]).then_inc(logits_ready, 1)
                    elif mode == "top1":
                        nc.vector.tensor_tensor(logits[:, t, 0:E], src[:, 0:E], b_logit[:, :], ALU.add)\
                            .then_inc(logits_ready, 1)
                    else:
                        nc.vector.tensor_copy(logits[:, t, 0:E], src[:, 0:E]).then_inc(logits_ready, 1)
                    nc.vector.tensor_copy(za[:, t, :], src[:, E:RC]).then_inc(routed.emptied[t], 1)
                if mode == "sequence":
                    n = TPS
                    routed.wait_full(dve, b, n)
                    stepped(nc.vector.tensor_tensor(top[:, 0, 0:E], routed.banks[n % 2][:, 0:E],
                                                    b_logit[:, :], ALU.add))
                    nc.vector.tensor_reduce(total[:, 1:2], top[:, 0, 0:E], AX.X, ALU.max, negate=True)\
                        .then_inc(max_ready, 1)
                    dve.wait_ge(expd_ready, b + 1)
                    stepped(nc.vector.reciprocal(r_total[:, 0:1], total[:, 0:1]))
                    stepped(nc.vector.tensor_scalar(weight[:, 0, :], expd[:, 0, 0:E], r_total[:, 0:1], 2.0,
                                                    ALU.mult, ALU.mult))
                    stepped(nc.vector.tensor_scalar(weight[:, 1, :], expd[:, 0, 0:E], r_total[:, 0:1], 2.0,
                                                    ALU.mult, ALU.mult))
                    routed.wait_full(dve, b, n + 1)
                    nc.vector.tensor_copy(total[:, 1:2], routed.banks[(n + 1) % 2][:, 0:1])\
                        .then_inc(routed.emptied[(n + 1) % 2], 1)
                    nc.vector.tensor_copy(p2[:, 0:1], routed.banks[n % 2][:, 0:1])\
                        .then_inc(routed.emptied[n % 2], 1)
                    for t in range(TPS):
                        apply_weights(dve, t)
                else:
                    for t in range(TPS):
                        dve.wait_ge(logits_ready, TPS * b + t + 1)
                        core.carry_wait(dve)
                        stepped(nc.vector.max(top[:, t, :], logits[:, t, :]))
                        core.carry_wait(dve)
                        stepped(nc.vector.max_index(top_at[:, t, :], top[:, t, :], logits[:, t, :]))
                        stepped(nc.vector.tensor_copy(top_atf[:, t, :], top_at[:, t, :]))
                        if mode == "top1":
                            stepped(nc.vector.tensor_scalar(weight[:, t, :], iota[:, :], top_atf[:, t, 0:1],
                                                            None, ALU.is_equal))
                        else:
                            stepped(nc.vector.tensor_tensor(expd[:, t, 0:1], top[:, t, 1:2], top[:, t, 0:1],
                                                            ALU.subtract))
                            nc.vector.tensor_copy(expd[:, t, 2:3], expd[:, t, 0:1]).then_inc(max_ready, 1)
                            dve.wait_ge(expd_ready, TPS * b + t + 1)
                            stepped(nc.vector.tensor_scalar(total[:, t:t + 1], expd[:, t, 1:2], 1.0, None, ALU.add))
                            stepped(nc.vector.reciprocal(r_total[:, t:t + 1], total[:, t:t + 1]))
                            stepped(nc.vector.tensor_scalar(p2[:, t:t + 1], expd[:, t, 1:2], r_total[:, t:t + 1],
                                                            2.0, ALU.mult, ALU.mult))
                            stepped(nc.vector.tensor_scalar(weight[:, t, :], iota[:, :], top_atf[:, t, 0:1],
                                                            r_total[:, t:t + 1], ALU.is_equal, ALU.mult))
                            stepped(nc.vector.tensor_scalar(weight2[:, t, :], iota[:, :], top_atf[:, t, 1:2],
                                                            p2[:, t:t + 1], ALU.is_equal, ALU.mult))
                            stepped(nc.vector.scalar_tensor_tensor(weight[:, t, :], weight[:, t, :], 2.0,
                                                                   weight2[:, t, :], ALU.mult, ALU.add))
                        apply_weights(dve, t)
                assert count[0] <= per
                while count[0] < per:
                    stepped(nc.vector.memset(top_atf[:, 0, 7:8], 0.0))
                if bias:
                    dve.wait_ge(bias_added, TPS * (b + 1))
                for t in range(TPS):
                    summed.wait_full(dve, b, t)
                    nc.vector.tensor_tensor(X[:, TPS * b + t, :], X[:, TPS * b + t, :], summed.banks[t][:, :],
                                            ALU.add).then_inc(summed.emptied[t], 1)

        @block.scalar
        def _(act):
            with act.Fori(0, B) as b:
                ln.scalar(act, b)
                ln.scalar_xT(act, b)
                if mode == "sequence":
                    act.wait_ge(max_ready, b + 1)
                    nc.scalar.activation(expd[:, 0, 0:E], top[:, 0, 0:E], ACT.Exp, bias=total[:, 1:2],
                                         accum_out=total[:, 0:1]).then_inc(expd_ready, 1)
                elif mode == "top2":
                    for t in range(TPS):
                        act.wait_ge(max_ready, TPS * b + t + 1)
                        nc.scalar.activation(expd[:, t, 1:2], expd[:, t, 2:3], ACT.Exp).then_inc(expd_ready, 1)
                for t in range(TPS):
                    n = TPS + t
                    turned.wait_full(act, b, n)
                    nc.scalar.copy(zwT[0:ER, t, :], turned.banks[n % 2][0:ER, 0:P])\
                        .then_inc(turned.emptied[n % 2], 1)

        @block.tensor
        def _(pe):
            pe.wait_ge(weights_loaded, 16 * n_loads)
            for ring in (turned, routed, summed):
                ring.open(pe)
            with pe.Fori(0, B) as b:
                ln.tensor(pe, b)
                for t in range(TPS):
                    ln.wait_xT(pe, b, t)
                    routed.wait_free(pe, b, t)
                    for c in range(C):
                        last = nc.tensor.matmul(routed.banks[t][:, 0:RC], ln.xT[:, c, t * P:(t + 1) * P],
                                                w_ra[:, c, :], start=(c == 0), stop=(c == C - 1))
                    last.then_inc(routed.filled[t], 1)
                for t in range(TPS):
                    summed.wait_free(pe, b, t)
                    for c in range(C):
                        nc.tensor.matmul(summed.banks[t][:, :], ln.xT[:, c, t * P:(t + 1) * P], w[:, c, :],
                                         start=(c == 0), stop=False)
                if mode == "sequence":
                    pe.wait_ge(logits_ready, TPS * (b + 1))
                    for k in range(2):
                        n = TPS + k
                        routed.wait_free(pe, b, n)
                        for t in range(TPS):
                            last = nc.tensor.matmul(routed.banks[n % 2][:, 0:E], mean_rows[:, t, :],
                                                    logits[:, t, 0:E], start=(t == 0), stop=(t == TPS - 1))
                        last.then_inc(routed.filled[n % 2], 1)
                for t in range(TPS):
                    n = TPS + t
                    pe.wait_ge(zw_ready, TPS * b + t + 1)
                    turned.wait_free(pe, b, n)
                    nc.tensor.transpose(turned.banks[n % 2][0:ER, 0:P], zw[:, t, :], ident[:, :])\
                        .then_inc(turned.filled[n % 2], 1)
                for t in range(TPS):
                    n = TPS + t
                    turned.wait_empty(pe, b, n)
                    nc.tensor.matmul(summed.banks[t][:, :], zwT[0:ER, t, :], w_b[:, :], start=False, stop=True)\
                        .then_inc(summed.filled[t], 1)


def gated_ffn(core, name):
    nc, dram, X = core.nc, core.dram, core.X
    H, RANK = 1376, 16
    HT = -(-H // P)
    ROWS = [min(P, H - P * j) for j in range(HT)]
    LOW = 2 * RANK
    S_USES = 1 + HT

    with ExitStack() as ctx:
        L = Layer(core, ctx, name)
        turned = Ring(L, "turned", TPS)
        summed = Ring(L, "summed", S_USES)
        results = Ring(L, "results", TPS)
        low_bank = L.bank("low_bank")
        ln = LayerNorm(L, turned)
        w_gate = L.sb("w_gate", [P, C, H])
        w_up = L.sb("w_up", [P, C, H])
        w_down = L.sb("w_down", [P, HT, D])
        a_in = L.sb("a_in", [P, C, LOW])
        b_in = L.sb("b_in", [LOW, 2, H])
        a_down = L.sb("a_down", [P, HT, RANK])
        b_down = L.sb("b_down", [RANK, D])
        low_in = L.sb("low_in", [LOW, S])
        low_down = L.sb("low_down", [RANK, S])
        silu = L.sb("silu", [P, 2, S])
        hidden = L.sb("hidden", [P, HT, S])

        zeroed = L.sem("zeroed")
        in_loaded = L.sem("in_loaded")
        down_loaded = L.sem("down_loaded")
        silu_ready = L.sem("silu_ready")
        hidden_ready = L.sem("hidden_ready")
        low_filled = L.sem("low_filled")
        low_emptied = L.sem("low_emptied")
        block = ctx.enter_context(nc.Block())

        @block.sync
        def _(sp):
            sp.wait_ge(zeroed, 1)
            for a, at in (("gate_a", 0), ("up_a", RANK)):
                sp.dma_start(a_in[:, :, at:at + RANK], dram[f"{name}_{a}"].rearrange("(c p) n -> p c n", p=P),
                             allow_slow_non_contiguous=True).then_inc(in_loaded, 16)
            for k, b in enumerate(("gate_b", "up_b")):
                sp.dma_start(b_in[k * RANK:(k + 1) * RANK, k, :], dram[f"{name}_{b}"]).then_inc(in_loaded, 16)
            for w, k in ((w_gate, "gate_w"), (w_up, "up_w")):
                sp.dma_start(w[:, :, :], dram[f"{name}_{k}"].rearrange("(c p) n -> p c n", p=P)).then_inc(in_loaded, 16)
            full = P * (HT - 1)
            for w, k in ((w_down, "down_w"), (a_down, "down_a")):
                src = dram[f"{name}_{k}"]
                sp.dma_start(w[:, 0:HT - 1, :], src[0:full, :].rearrange("(j p) n -> p j n", p=P),
                             allow_slow_non_contiguous=True).then_inc(down_loaded, 16)
                sp.dma_start(w[0:H - full, HT - 1, :], src[full:H, :]).then_inc(down_loaded, 16)
            sp.dma_start(b_down[:, :], dram[f"{name}_down_b"]).then_inc(down_loaded, 16)

        @block.gpsimd
        def _(pool):
            nc.gpsimd.memset(b_in[:, :, :], 0.0).then_inc(zeroed, 1)

        @block.vector
        def _(dve):
            with dve.Fori(0, B) as b:
                ln.vector(dve, b)
                for j in range(HT):
                    use, rows = 1 + j, slice(0, ROWS[j])
                    dve.wait_ge(silu_ready, HT * b + j + 1)
                    nc.vector.tensor_tensor(hidden[rows, j, :], silu[rows, j % 2, :],
                                            summed.banks[use % 2][rows, S:2 * S], ALU.mult)\
                        .then_inc(summed.emptied[use % 2], 1)
                for t in range(TPS):
                    results.wait_full(dve, b, t)
                    nc.vector.tensor_tensor(X[:, TPS * b + t, :], X[:, TPS * b + t, :], results.banks[t][:, :],
                                            ALU.add).then_inc(results.emptied[t], 1)

        @block.scalar
        def _(act):
            with act.Fori(0, B) as b:
                ln.scalar(act, b)
                ln.scalar_xT(act, b)
                summed.wait_full(act, b, 0)
                nc.scalar.copy(low_in[:, :], summed.banks[0][0:LOW, 0:S]).then_inc(summed.emptied[0], 1)
                for j in range(HT):
                    use, rows = 1 + j, slice(0, ROWS[j])
                    summed.wait_full(act, b, use)
                    if j >= 2:
                        summed.wait_empty(act, b, use - 2)
                    nc.scalar.activation(silu[rows, j % 2, :], summed.banks[use % 2][rows, 0:S], ACT.Silu)\
                        .then_inc(silu_ready, 1)
                act.wait_ge(low_filled, b + 1)
                nc.scalar.copy(low_down[:, :], low_bank[0:RANK, 0:S]).then_inc(low_emptied, 1)

        @block.tensor
        def _(pe):
            for ring in (turned, summed, results):
                ring.open(pe)
            pe.wait_ge(in_loaded, 16 * 6)
            with pe.Fori(0, B) as b:
                ln.tensor(pe, b)
                for t in range(TPS):
                    ln.wait_xT(pe, b, t)
                summed.wait_free(pe, b, 0)
                for c in range(C):
                    last = nc.tensor.matmul(summed.banks[0][0:LOW, 0:S], a_in[:, c, :], ln.xT[:, c, :],
                                            start=(c == 0), stop=(c == C - 1))
                last.then_inc(summed.filled[0], 1)
                for j in range(HT):
                    use, rows = 1 + j, slice(0, ROWS[j])
                    cols = slice(P * j, P * j + ROWS[j])
                    bank = summed.banks[use % 2]
                    summed.wait_free(pe, b, use)
                    for k, (w, half) in enumerate(((w_gate, 0), (w_up, S))):
                        for c in range(C):
                            nc.tensor.matmul(bank[rows, half:half + S], w[:, c, cols], ln.xT[:, c, :],
                                             start=(c == 0), stop=False)
                        if j == 0 and half == 0:
                            summed.wait_empty(pe, b, 0)
                        last = nc.tensor.matmul(bank[rows, half:half + S], b_in[:, k, cols],
                                                low_in[:, :], start=False, stop=True)
                    last.then_inc(summed.filled[use % 2], 1)
                pe.wait_ge(down_loaded, 16 * 5)
                for j in range(HT):
                    if j in (HT - 2, HT - 1):
                        summed.wait_empty(pe, b, 1 + j)
                    elif j == 0:
                        summed.wait_empty(pe, b, 1 + HT - 3)
                        summed.wait_empty(pe, b, 1 + HT - 4)
                    last = nc.tensor.matmul(low_bank[0:RANK, 0:S], a_down[0:ROWS[j], j, :], hidden[0:ROWS[j], j, :],
                                            start=(j == 0), stop=(j == HT - 1))
                last.then_inc(low_filled, 1)
                for t in range(TPS):
                    results.wait_free(pe, b, t)
                    for j in range(HT):
                        nc.tensor.matmul(results.banks[t][:, :], hidden[0:ROWS[j], j, t * P:(t + 1) * P],
                                         w_down[0:ROWS[j], j, :], start=(j == 0), stop=False)
                    if t == 0:
                        pe.wait_ge(low_emptied, b + 1)
                    nc.tensor.matmul(results.banks[t][:, :], low_down[:, t * P:(t + 1) * P], b_down[:, :],
                                     start=False, stop=True).then_inc(results.filled[t], 1)


def build(nc, dram):
    with ExitStack() as ctx:
        core = Core(nc, ctx, dram)
        load_constants(core)
        narrow_attention(core, "L0_attn", rope=True)
        routed_ffn(core, "L0_ffn", 8, 16, "sequence")
        wide_attention(core, "L1_attn", linear=True)
        gated_ffn(core, "L1_ffn")
        narrow_attention(core, "L2_attn", rope=False)
        routed_ffn(core, "L2_ffn", 4, 8, "top1")
        wide_attention(core, "L3_attn", linear=False)
        routed_ffn(core, "L3_ffn", 8, 16, "top2")
        store_result(core)


def narrow_tables():
    HD = 16
    inv = (1.0 / 10000.0 ** (np.arange(0, HD, 2, dtype=np.float32) / HD)).astype(np.float32)
    ang = np.arange(S, dtype=np.float32)[:, None] * inv[None, :]
    cos, sin = np.cos(ang).astype(np.float32), np.sin(ang).astype(np.float32)
    c2 = np.repeat(cos, 2, axis=1)
    s2 = np.stack([-sin, sin], axis=-1).reshape(S, HD)
    scale = -np.float32(HD) ** -0.5
    out = []
    for t in (c2, s2):
        full = np.concatenate([np.tile(t * scale, (1, HEADS)), np.tile(t, (1, KV_HEADS))], axis=1)
        out.append(np.ascontiguousarray(full.reshape(TPS, P, -1).transpose(1, 0, 2)).astype(np.float32))
    return out


def wide_tables():
    HD = 128
    inv = (1.0 / 10000.0 ** (np.arange(0, HD, 2, dtype=np.float32) / HD)).astype(np.float32)
    ang = np.arange(S, dtype=np.float32)[:, None] * inv[None, :]
    cos, sin = np.cos(ang).astype(np.float32), np.sin(ang).astype(np.float32)
    scale = np.float32(-1.0 / np.sqrt(HD))
    out = []
    for t in (np.concatenate([cos, cos], axis=1), np.concatenate([-sin, sin], axis=1)):
        full = np.concatenate([np.tile(t * scale, (1, GROUP)), t], axis=1)
        out.append(np.ascontiguousarray(full.reshape(TPS, P, -1).transpose(1, 0, 2)).astype(np.float32))
    return out


def shape_constants():
    k = {"ident": np.eye(P, dtype=np.float32), "eps": np.full((P, 1), EPS, np.float32),
         "one": np.ones((P, 1), np.float32)}
    q, c = np.arange(P)[:, None], np.arange(P)[None, :]
    tri = np.where(c <= q, 0.0, BIG).astype(np.float32)
    k["mask"] = np.concatenate([tri, np.zeros((P, P), np.float32), tri], axis=1)
    k["wide_cos"], k["wide_sin"] = wide_tables()
    qt, kt = np.arange(S)[:, None], np.arange(S)[None, :]
    window = np.where((kt <= qt) & (qt - kt <= WINDOW), 0.0, BIG).astype(np.float32)
    k["window_mask"] = np.concatenate([window[:P, :P], window[P:, :]], axis=1)
    key, blk, query = np.arange(P)[:, None, None, None], np.arange(4)[:, None, None], np.arange(32)
    half = np.broadcast_to(np.where(key <= 32 * blk + query, 0.5, 0.0), (P, 4, GROUP, 32))
    k["half_mask"] = half.reshape(P, 4, GROUP * 32).astype(np.float32)
    tok = np.arange(S)
    rows = ((tok >= MEAN_FROM) & (tok < MEAN_TO)).astype(np.float32) / np.float32(MEAN_TO - MEAN_FROM)
    k["mean_rows"] = np.repeat(rows.reshape(TPS, P).T[:, :, None], P, axis=2).astype(np.float32)
    k["L0_attn_cos"], k["L0_attn_sin"] = narrow_tables()
    k["L0_attn_q_pad"] = np.zeros((P, TPS, HEADS, 32), np.float32)
    k["L0_attn_k_pad"] = np.zeros((P, TPS, KV_HEADS, 4, 32), np.float32)
    start = 2.0 ** (-2.0 ** (-(np.log2(HEADS) - 3)))
    slopes = np.array([start ** (i + 1) for i in range(HEADS)], dtype=np.float32)
    pos = np.arange(S, dtype=np.float32).reshape(TPS, P).T
    qp = np.zeros((P, TPS, HEADS, 32), np.float32)
    qp[:, :, :, 16] = -slopes
    qp[:, :, :, 17] = slopes * pos[:, :, None]
    kp = np.zeros((P, TPS, 1, 4, 32), np.float32)
    kp[:, :, :, :, 16] = pos[:, :, None, None]
    kp[:, :, :, :, 17] = 1.0
    k["L2_attn_q_pad"], k["L2_attn_k_pad"] = qp, kp
    return k


def by_group(*ws):
    return np.concatenate([w.reshape(D, KV_HEADS, -1).transpose(1, 0, 2) for w in ws], axis=2)


def layouts(i):
    a = {k: np.asarray(v) for k, v in i.items()}
    return {
        "x": a["L0_attn_x"],
        "L0_attn_w_qkv": a["L0_attn_w_qkv"].T, "L0_attn_b_qkv": a["L0_attn_b_qkv"],
        "L0_attn_w_o": a["L0_attn_w_o"].T, "L0_attn_b_o": a["L0_attn_b_o"],
        "L0_ffn_w": a["L0_ffn_W"].T, "L0_ffn_b": a["L0_ffn_b"], "L0_ffn_router": a["L0_ffn_router_W"].T,
        "L0_ffn_router_b": a["L0_ffn_router_b"], "L0_ffn_A": a["L0_ffn_A"].reshape(-1, D).T,
        "L0_ffn_B": a["L0_ffn_B"].transpose(0, 2, 1).reshape(-1, D),
        "L2_attn_w_qkv": np.concatenate([a["L2_attn_Wq"], a["L2_attn_Wkv"]], axis=1),
        "L2_attn_w_o": a["L2_attn_Wo"],
        "L2_ffn_w": a["L2_ffn_W_up"].T, "L2_ffn_router": a["L2_ffn_gate_w"].T,
        "L2_ffn_router_b": a["L2_ffn_expert_bias"], "L2_ffn_A": a["L2_ffn_lora_A"].reshape(-1, D).T,
        "L2_ffn_B": a["L2_ffn_lora_B"].transpose(0, 2, 1).reshape(-1, D),
        "L1_attn_w_in": by_group(a["L1_attn_Wq"], a["L1_attn_Wk"], a["L1_attn_Wv"]),
        "L1_attn_w_o": a["L1_attn_Wo"].reshape(KV_HEADS, -1, D),
        **{f"L1_ffn_{k}": a[f"L1_ffn_{k}"].T for k in ("gate_w", "up_w", "down_w", "gate_a", "gate_b", "up_a",
                                                       "up_b", "down_a", "down_b")},
        "L3_attn_w_in": by_group(a["L3_attn_Wq"], a["L3_attn_Wk"], a["L3_attn_Wv"]),
        "L3_attn_w_o": a["L3_attn_Wo"].reshape(KV_HEADS, -1, D),
        "L3_ffn_w": a["L3_ffn_W_base"].T, "L3_ffn_b": a["L3_ffn_b_base"],
        "L3_ffn_router": a["L3_ffn_W_router"].T, "L3_ffn_A": a["L3_ffn_A"].reshape(-1, D).T,
        "L3_ffn_B": a["L3_ffn_B"].transpose(0, 2, 1).reshape(-1, D),
    }


def kernel(**inputs):
    import concourse.bacc as bacc
    from concourse.bass_utils import run_bass_kernel_spmd

    nc = bacc.Bacc("TRN2", target_bir_lowering=False, num_devices=1)
    arrays, dram = {}, {}
    for name, a in {**layouts(inputs), **shape_constants()}.items():
        arrays[f"in_{name}"] = np.ascontiguousarray(a)
        dram[name] = nc.dram_tensor(f"in_{name}", a.shape, mybir.dt.from_np(a.dtype), kind="ExternalInput").ap()
    dram["out"] = nc.dram_tensor("out_x", (B, S, D), F32, kind="ExternalOutput").ap()
    build(nc, dram)
    r = run_bass_kernel_spmd(nc, [arrays], core_ids=[0])
    return r.results[0]["out_x"]
```

```python
from contextlib import ExitStack

import concourse.bass as bass
import concourse.mybir as mybir
import numpy as np

F32 = mybir.dt.float32
F32R = mybir.dt.float32r
BF16 = mybir.dt.bfloat16
U32 = mybir.dt.uint32
ALU = mybir.AluOpType
ACT = mybir.ActivationFunctionType
AX = mybir.AxisListType

P = 128
D = 512
C = D // P
B, S = 4, 256
TPS = S // P
NT = B * TPS
EPS = 1e-5
BIG = 1e30
HEADS, KV_HEADS = 32, 8
WINDOW = 64
MEAN_FROM, MEAN_TO = 34 + 72 + 1, S - 1
GROUP = HEADS // KV_HEADS
SCORE_COLS = P + S
SPAN = [slice(0, P), slice(P, P + S)]


class Core:

    def __init__(self, nc, ctx, dram):
        self.nc, self.dram = nc, dram
        self.X = ctx.enter_context(nc.sbuf_tensor("X", [P, NT, D], F32))
        self.ident = ctx.enter_context(nc.sbuf_tensor("ident", [P, P], F32))
        self.one = ctx.enter_context(nc.sbuf_tensor("one", [P, 1], F32))
        self.eps = ctx.enter_context(nc.sbuf_tensor("eps", [P, 1], F32))
        self.mask = ctx.enter_context(nc.sbuf_tensor("mask", [P, SCORE_COLS], F32))
        self.carrier = ctx.enter_context(nc.semaphore("carrier"))
        self.loaded = ctx.enter_context(nc.semaphore("constants_loaded"))

    def carry_wait(self, eng):
        eng.sem_inc(self.carrier, 1)


class Layer:

    def __init__(self, core, ctx, name):
        self.core, self.ctx, self.name, self.nc = core, ctx, name, core.nc
        self.sems = []
        ctx.callback(self.close)

    def close(self):
        self.nc.clear_and_free_semaphores(self.sems)
        self.nc.all_engine_barrier()

    def sb(self, name, shape, dtype=F32):
        return self.ctx.enter_context(self.nc.sbuf_tensor(f"{self.name}_{name}", shape, dtype))

    def bank(self, name, shape=(P, 512), dtype=F32):
        return self.ctx.enter_context(self.nc.psum_tensor(f"{self.name}_{name}", list(shape), dtype))

    def sem(self, name):
        self.sems.append(self.nc.alloc_semaphore(f"{self.name}_{name}"))
        return self.sems[-1]


def split_matmul(nc, out, left, right, start, stop):
    pairs = [(left[0], right[0]), (left[0], right[1])]
    if len(left) == 2:
        pairs.append((left[1], right[0]))
    for n, (a, b) in enumerate(pairs):
        last = nc.tensor.matmul(out, a, b, start=start and n == 0, stop=stop and n == len(pairs) - 1)
    return last


class Ring:

    def __init__(self, layer, name, per):
        assert per % 2 == 0
        self.banks = [layer.bank(f"{name}{k}") for k in range(2)]
        self.filled = [layer.sem(f"{name}{k}_filled") for k in range(2)]
        self.emptied = [layer.sem(f"{name}{k}_emptied") for k in range(2)]
        self.per = per // 2

    def wait_free(self, pe, i, n):
        pe.wait_ge(self.emptied[n % 2], 1 + i * self.per + n // 2)

    def wait_empty(self, eng, i, n):
        eng.wait_ge(self.emptied[n % 2], 1 + i * self.per + n // 2 + 1)

    def open(self, pe):
        for k in self.emptied:
            pe.sem_inc(k, 1)

    def wait_full(self, eng, i, n):
        eng.wait_ge(self.filled[n % 2], i * self.per + n // 2 + 1)


class LayerNorm:

    def __init__(self, layer, ring):
        self.core, self.nc, self.ring = layer.core, layer.nc, ring
        self.xn = layer.sb("xn", [P, TPS, D])
        self.xT = layer.sb("xT", [P, C, S])
        self.stats = layer.sb("stats", [P, TPS, 6])
        self.moments = layer.sb("moments", [P, TPS, 2])
        self.std = layer.sb("std", [P, TPS])
        self.rstd = layer.sb("rstd", [P, TPS])
        self.stats_ready = layer.sem("stats_ready")
        self.moments_ready = layer.sem("moments_ready")
        self.std_ready = layer.sem("std_ready")
        self.rstd_ready = layer.sem("rstd_ready")
        self.xn_ready = layer.sem("xn_ready")
        self.xT_ready = layer.sem("xT_ready")

    def vector(self, dve, b):
        nc, X = self.nc, self.core.X
        for t in range(TPS):
            nc.vector.bn_stats(self.stats[:, t, :], X[:, TPS * b + t, :]).then_inc(self.stats_ready, 1)
        for t in range(TPS):
            dve.wait_ge(self.stats_ready, TPS * b + t + 1)
            self.core.carry_wait(dve)
            nc.vector.bn_aggr(self.moments[:, t, :], self.stats[:, t, :]).then_inc(self.moments_ready, 1)
        for t in range(TPS):
            dve.wait_ge(self.std_ready, TPS * b + t + 1)
            nc.vector.reciprocal(self.rstd[:, t:t + 1], self.std[:, t:t + 1]).then_inc(self.rstd_ready, 1)
            dve.wait_ge(self.rstd_ready, TPS * b + t + 1)
            nc.vector.tensor_scalar(self.xn[:, t, :], X[:, TPS * b + t, :], self.moments[:, t, 0:1],
                                    self.rstd[:, t:t + 1], ALU.subtract, ALU.mult).then_inc(self.xn_ready, 1)

    def scalar(self, act, b):
        nc = self.nc
        for t in range(TPS):
            act.wait_ge(self.moments_ready, TPS * b + t + 1)
            nc.scalar.activation(self.std[:, t:t + 1], self.moments[:, t, 1:2], ACT.Sqrt,
                                 bias=self.core.eps[:, 0:1]).then_inc(self.std_ready, 1)

    def scalar_xT(self, act, b, xT=None):
        nc, xT = self.nc, self.xT if xT is None else xT
        for t in range(TPS):
            self.ring.wait_full(act, b, t)
            nc.scalar.copy(xT[:, :, t * P:(t + 1) * P],
                           self.ring.banks[t].rearrange("p (c n) -> p c n", c=C))\
                .then_inc(self.ring.emptied[t], 1)

    def tensor(self, pe, b):
        nc = self.nc
        for t in range(TPS):
            pe.wait_ge(self.xn_ready, TPS * b + t + 1)
            self.ring.wait_free(pe, b, t)
            for c in range(C):
                last = nc.tensor.transpose(self.ring.banks[t][:, c * P:(c + 1) * P],
                                           self.xn[:, t, c * P:(c + 1) * P], self.core.ident[:, :])
            last.then_inc(self.ring.filled[t], 1)

    def wait_xT(self, eng, b, t):
        self.ring.wait_empty(eng, b, t)


def load_constants(core):
    nc, dram = core.nc, core.dram
    loaded = core.loaded
    with ExitStack() as ctx:
        block = ctx.enter_context(nc.Block())

        @block.sync
        def _(sp):
            sp.dma_start(core.ident[:, :], dram["ident"]).then_inc(loaded, 16)
            sp.dma_start(core.mask[:, :], dram["mask"]).then_inc(loaded, 16)
            sp.dma_start(core.eps[:, :], dram["eps"]).then_inc(loaded, 16)
            sp.dma_start(core.one[:, :], dram["one"]).then_inc(loaded, 16)
            xv = dram["x"].rearrange("b (t p) d -> p (b t) d", p=P)
            sp.dma_start(core.X[:, :, :], xv).then_inc(loaded, 16)
            sp.wait_ge(loaded, 80)


def store_result(core):
    nc = core.nc
    with ExitStack() as ctx:
        stored = ctx.enter_context(nc.semaphore("stored"))
        block = ctx.enter_context(nc.Block())

        @block.sync
        def _(sp):
            ov = core.dram["out"].rearrange("b (t p) d -> p (b t) d", p=P)
            sp.dma_start(ov, core.X[:, :, :]).then_inc(stored, 16)
            sp.wait_ge(stored, 16)


def narrow_attention(core, name, rope):
    nc, dram, X, ident = core.nc, core.dram, core.X, core.ident
    HD = 16
    SLOT = 32
    SLOTS = P // SLOT
    QG = HEADS // SLOTS
    KG = KV_HEADS if rope else 1
    KV = KG * HD
    QKV = HEADS * HD + 2 * KV
    PIECES = [(0, 512), (512, QKV - 512)]
    QU, KU = QG * P // 512, max(1, KG * P // 512)
    KB = KG // KU
    LN_USES = TPS
    HEAD0 = LN_USES + TPS * (QU + KU)
    OUT0 = HEAD0 + HEADS
    T_USES = OUT0 + TPS
    A_USES = TPS * 2 + TPS

    with ExitStack() as ctx:
        L = Layer(core, ctx, name)
        turned = Ring(L, "turned", T_USES)
        summed = Ring(L, "summed", A_USES)
        ln = LayerNorm(L, turned)
        scores = [L.bank(f"scores{k}") for k in range(2)]
        heads_out = [L.bank(f"heads_out{t}") for t in range(TPS)]

        w_qkv = L.sb("w_qkv", [P, C, QKV])
        w_o = L.sb("w_o", [P, C, D])
        q_pad = L.sb("q_pad", [P, TPS, HEADS, SLOT])
        k_pad = L.sb("k_pad", [P, TPS, KG, SLOTS, SLOT])
        v = L.sb("v", [P, TPS, KG, HD])
        qT = L.sb("qT", [P, QG, S])
        kT = L.sb("kT", [P, SLOTS, KG, S])
        masked = L.sb("masked", [P, 2, SCORE_COLS])
        neg_max = L.sb("neg_max", [P, TPS, HEADS])
        total = L.sb("total", [P, TPS, HEADS])
        r_total = L.sb("r_total", [P, TPS, HEADS])
        probs = L.sb("probs", [P, 2, SCORE_COLS])
        probsT = L.sb("probsT", [P, 2, SCORE_COLS])
        out = L.sb("out", [P, TPS, HEADS, HD])
        outT = L.sb("outT", [P, C, S])
        if rope:
            b_qkv = L.sb("b_qkv", [P, QKV])
            b_o = L.sb("b_o", [P, D])
            qkv = L.sb("qkv", [P, TPS, QKV])
            straight = L.sb("straight", [P, TPS, (HEADS + KG) * HD])
            crossed = L.sb("crossed", [P, TPS, (HEADS + KG) * HD])
            cos = L.sb("cos", [P, TPS, (HEADS + KG) * HD])
            sin = L.sb("sin", [P, TPS, (HEADS + KG) * HD])

        weights_loaded = L.sem("weights_loaded")
        padded = L.sem("padded")
        zeroed = L.sem("zeroed")
        qkv_ready = L.sem("qkv_ready")
        turned_parts_ready = L.sem("rope_parts_ready")
        q_pad_ready = L.sem("q_pad_ready")
        kv_ready = L.sem("kv_ready")
        scores_filled = L.sem("scores_filled")
        masked_ready = L.sem("masked_ready")
        probs_ready = L.sem("probs_ready")
        pv_done = L.sem("pv_done")
        r_total_ready = L.sem("r_total_ready")
        out_ready = L.sem("out_ready")
        x_written = L.sem("x_written")
        bias_added = L.sem("bias_added")
        block = ctx.enter_context(nc.Block())

        @block.sync
        def _(sp):
            sp.dma_start(w_qkv[:, :, :], dram[f"{name}_w_qkv"].rearrange("(c p) n -> p c n", p=P))\
                .then_inc(weights_loaded, 16)
            sp.dma_start(w_o[:, :, :], dram[f"{name}_w_o"].rearrange("(c p) n -> p c n", p=P))\
                .then_inc(weights_loaded, 16)
            if rope:
                sp.dma_start(b_qkv[:, :], dram[f"{name}_b_qkv"].partition_broadcast(P)).then_inc(weights_loaded, 16)
                sp.dma_start(b_o[:, :], dram[f"{name}_b_o"].partition_broadcast(P)).then_inc(weights_loaded, 16)
                sp.dma_start(cos[:, :, :], dram[f"{name}_cos"]).then_inc(weights_loaded, 16)
                sp.dma_start(sin[:, :, :], dram[f"{name}_sin"]).then_inc(weights_loaded, 16)
            sp.dma_start(q_pad[:, :, :, :], dram[f"{name}_q_pad"]).then_inc(padded, 16)
            sp.dma_start(k_pad[:, :, :, :, :], dram[f"{name}_k_pad"]).then_inc(padded, 16)

        loads = 16 * (6 if rope else 2)

        @block.vector
        def _(dve):
            dve.wait_ge(padded, 32)
            if rope:
                dve.wait_ge(weights_loaded, loads)
            with dve.Fori(0, B) as b:
                ln.vector(dve, b)
                for t in range(TPS):
                    if rope:
                        for j, (at, n) in enumerate(PIECES):
                            summed.wait_full(dve, b, 2 * t + j)
                            nc.vector.tensor_tensor(qkv[:, t, at:at + n], summed.banks[j][:, 0:n],
                                                    b_qkv[:, at:at + n], ALU.add)\
                                .then_inc(summed.emptied[j], 1)
                        NR = (HEADS + KG) * HD
                        summed.wait_empty(dve, b, 2 * t)
                        summed.wait_empty(dve, b, 2 * t + 1)
                        nc.vector.tensor_tensor(straight[:, t, :], qkv[:, t, 0:NR], cos[:, t, :], ALU.mult)\
                            .then_inc(turned_parts_ready, 1)
                        src = qkv[:, t, 0:NR].rearrange("p (n two) -> p n two", two=2)
                        dst = crossed[:, t, :].rearrange("p (n two) -> p n two", two=2)
                        sn = sin[:, t, :].rearrange("p (n two) -> p n two", two=2)
                        for e in range(2):
                            nc.vector.tensor_tensor(dst[:, :, e], src[:, :, 1 - e], sn[:, :, e], ALU.mult)\
                                .then_inc(turned_parts_ready, 1)
                        dve.wait_ge(turned_parts_ready, 3 * (TPS * b + t + 1))
                        QN = HEADS * HD
                        nc.vector.tensor_tensor(
                            q_pad[:, t, :, 0:HD], straight[:, t, 0:QN].rearrange("p (h d) -> p h d", d=HD),
                            crossed[:, t, 0:QN].rearrange("p (h d) -> p h d", d=HD), ALU.add)\
                            .then_inc(q_pad_ready, 1)
                        for s in range(SLOTS):
                            nc.vector.tensor_tensor(
                                k_pad[:, t, :, s, 0:HD],
                                straight[:, t, QN:NR].rearrange("p (h d) -> p h d", d=HD),
                                crossed[:, t, QN:NR].rearrange("p (h d) -> p h d", d=HD), ALU.add)\
                                .then_inc(kv_ready, 1)
                        nc.vector.tensor_copy(v[:, t, :, :],
                                              qkv[:, t, NR:QKV].rearrange("p (h d) -> p h d", d=HD))\
                            .then_inc(kv_ready, 1)
                    else:
                        summed.wait_full(dve, b, 2 * t)
                        nc.vector.tensor_scalar(
                            q_pad[:, t, :, 0:HD], summed.banks[0].rearrange("p (h d) -> p h d", d=HD),
                            -float(HD) ** -0.5, None, ALU.mult).then_inc(summed.emptied[0], 1)
                        summed.wait_full(dve, b, 2 * t + 1)
                        for s in range(SLOTS):
                            nc.vector.tensor_copy(k_pad[:, t, 0, s, 0:HD], summed.banks[1][:, 0:HD])\
                                .then_inc(kv_ready, 1)
                        nc.vector.tensor_copy(v[:, t, 0, :], summed.banks[1][:, HD:2 * HD])\
                            .then_inc(summed.emptied[1], 1)

                def mask_scores(h):
                    k = h % 2
                    dve.wait_ge(scores_filled, HEADS * b + h + 1)
                    if h >= 2:
                        dve.wait_ge(probs_ready, TPS * (HEADS * b + h - 1))
                    core.carry_wait(dve)
                    for t in range(TPS):
                        nc.vector.tensor_tensor_reduce(masked[:, k, SPAN[t]], scores[k][:, SPAN[t]],
                                                       core.mask[:, SPAN[t]], 1.0, 3e38, ALU.add, ALU.min,
                                                       neg_max[:, t, h:h + 1]).then_inc(masked_ready, 1)

                def empty_probsT(h):
                    n = HEAD0 + h
                    turned.wait_full(dve, b, n)
                    if h >= 2:
                        dve.wait_ge(pv_done, HEADS * b + h - 1)
                    nc.vector.tensor_copy(probsT[:, h % 2, :], turned.banks[n % 2][:, 0:SCORE_COLS])\
                        .then_inc(turned.emptied[n % 2], 1)

                mask_scores(0)
                for h in range(HEADS):
                    if h + 1 < HEADS:
                        mask_scores(h + 1)
                    if h % 2 == 0:
                        empty_probsT(h)
                dve.wait_ge(probs_ready, TPS * HEADS * (b + 1))
                for t in range(TPS):
                    nc.vector.reciprocal(r_total[:, t, :], total[:, t, :]).then_inc(r_total_ready, 1)
                dve.wait_ge(pv_done, HEADS * (b + 1))
                for t in range(TPS):
                    dve.wait_ge(r_total_ready, TPS * b + t + 1)
                    nc.vector.tensor_tensor(out[:, t, :, :],
                                            heads_out[t].rearrange("p (h d) -> p h d", d=HD),
                                            r_total[:, t, :].unsqueeze(2).to_broadcast([P, HEADS, HD]),
                                            ALU.mult).then_inc(out_ready, 1)
                if rope:
                    dve.wait_ge(bias_added, TPS * (b + 1))
                for t in range(TPS):
                    n = 2 * TPS + t
                    summed.wait_full(dve, b, n)
                    nc.vector.tensor_tensor(X[:, TPS * b + t, :], X[:, TPS * b + t, :],
                                            summed.banks[n % 2][:, :], ALU.add)\
                        .then_inc(summed.emptied[n % 2], 1)

        @block.gpsimd
        def _(pool):
            nc.gpsimd.memset(kT[:, :, :, :], 0.0).then_inc(zeroed, 1)
            if rope:
                pool.wait_ge(weights_loaded, loads)
                with pool.Fori(0, B) as b:
                    for t in range(TPS):
                        pool.wait_ge(ln.xn_ready, TPS * b + t + 1)
                        nc.gpsimd.tensor_tensor(X[:, TPS * b + t, :], X[:, TPS * b + t, :], b_o[:, :], ALU.add)\
                            .then_inc(bias_added, 1)

        @block.scalar
        def _(act):
            act.wait_ge(zeroed, 1)
            with act.Fori(0, B) as b:
                ln.scalar(act, b)
                ln.scalar_xT(act, b)
                for t in range(TPS):
                    for j in range(QU + KU):
                        n = LN_USES + t * (QU + KU) + j
                        turned.wait_full(act, b, n)
                        src = turned.banks[n % 2]
                        if j < QU:
                            nc.scalar.copy(qT[:, 4 * j:4 * j + 4, t * P:(t + 1) * P],
                                           src.rearrange("p (g n) -> p g n", g=4))\
                                .then_inc(turned.emptied[n % 2], 1)
                        else:
                            u = j - QU
                            for s in range(SLOTS):
                                rows = slice(SLOT * s, SLOT * (s + 1))
                                last = nc.scalar.copy(kT[rows, s, KB * u:KB * (u + 1), t * P:(t + 1) * P],
                                                      src[rows, 0:KB * P].rearrange("p (g n) -> p g n", g=KB))
                            last.then_inc(turned.emptied[n % 2], 1)

                def exponentials(h):
                    k = h % 2
                    for t in range(TPS):
                        act.wait_ge(masked_ready, TPS * (HEADS * b + h) + t + 1)
                        if t == 0 and h >= 2:
                            turned.wait_full(act, b, HEAD0 + h - 2)
                        nc.scalar.activation(probs[:, k, SPAN[t]], masked[:, k, SPAN[t]], ACT.Exp,
                                             bias=neg_max[:, t, h:h + 1], scale=-1.0,
                                             accum_out=total[:, t, h:h + 1]).then_inc(probs_ready, 1)

                exponentials(0)
                for h in range(HEADS):
                    if h + 1 < HEADS:
                        exponentials(h + 1)
                    if h % 2 == 1:
                        n = HEAD0 + h
                        turned.wait_full(act, b, n)
                        if h >= 2:
                            act.wait_ge(pv_done, HEADS * b + h - 1)
                        nc.scalar.copy(probsT[:, h % 2, :], turned.banks[n % 2][:, 0:SCORE_COLS])\
                            .then_inc(turned.emptied[n % 2], 1)
                for t in range(TPS):
                    n = OUT0 + t
                    turned.wait_full(act, b, n)
                    nc.scalar.copy(outT[:, :, t * P:(t + 1) * P],
                                   turned.banks[n % 2].rearrange("p (c n) -> p c n", c=C))\
                        .then_inc(turned.emptied[n % 2], 1)

        @block.tensor
        def _(pe):
            pe.wait_ge(weights_loaded, loads)
            pe.wait_ge(padded, 32)
            turned.open(pe)
            summed.open(pe)
            with pe.Fori(0, B) as b:
                ln.tensor(pe, b)
                for t in range(TPS):
                    ln.wait_xT(pe, b, t)
                    for j, (at, n) in enumerate(PIECES):
                        use = 2 * t + j
                        summed.wait_free(pe, b, use)
                        for c in range(C):
                            last = nc.tensor.matmul(summed.banks[use % 2][:, 0:n],
                                                    ln.xT[:, c, t * P:(t + 1) * P], w_qkv[:, c, at:at + n],
                                                    start=(c == 0), stop=(c == C - 1))
                        last.then_inc(summed.filled[use % 2], 1)
                for t in range(TPS):
                    for j in range(QU + KU):
                        n = LN_USES + t * (QU + KU) + j
                        if j == 0:
                            if rope:
                                pe.wait_ge(q_pad_ready, TPS * b + t + 1)
                            else:
                                summed.wait_empty(pe, b, 2 * t)
                        if j == QU:
                            if rope:
                                pe.wait_ge(kv_ready, (SLOTS + 1) * (TPS * b + t + 1))
                            else:
                                pe.wait_ge(kv_ready, SLOTS * (TPS * b + t + 1))
                        turned.wait_free(pe, b, n)
                        for g in range(4 if j < QU else KB):
                            if j < QU:
                                src = q_pad[:, t, SLOTS * (4 * j + g):SLOTS * (4 * j + g + 1), :]
                            else:
                                src = k_pad[:, t, KB * (j - QU) + g, :, :]
                            last = nc.tensor.transpose(turned.banks[n % 2][:, g * P:(g + 1) * P],
                                                       src.rearrange("p s d -> p (s d)"), ident[:, :])
                        last.then_inc(turned.filled[n % 2], 1)
                for k in range(2):
                    turned.wait_empty(pe, b, HEAD0 - 1 - k)

                def score(h):
                    g, s = divmod(h, SLOTS)
                    kg = g if rope else 0
                    if h >= 2:
                        pe.wait_ge(masked_ready, TPS * (HEADS * b + h - 1))
                    for t in range(TPS):
                        last = nc.tensor.matmul(scores[h % 2][:, SPAN[t]], qT[:, g, t * P:(t + 1) * P],
                                                kT[:, s, kg, 0:(t + 1) * P], start=True, stop=True)
                    last.then_inc(scores_filled, 1)

                def turn_probs(h):
                    n = HEAD0 + h
                    pe.wait_ge(probs_ready, TPS * (HEADS * b + h + 1))
                    turned.wait_free(pe, b, n)
                    for j in range(SCORE_COLS // P):
                        last = nc.tensor.transpose(turned.banks[n % 2][:, j * P:(j + 1) * P],
                                                   probs[:, h % 2, j * P:(j + 1) * P], ident[:, :])
                    last.then_inc(turned.filled[n % 2], 1)

                def weigh_values(h):
                    n = HEAD0 + h
                    kg = h // GROUP if rope else 0
                    turned.wait_empty(pe, b, n)
                    pT = probsT[:, h % 2, :]
                    cols = slice(HD * h, HD * (h + 1))
                    nc.tensor.matmul(heads_out[0][:, cols], pT[:, 0:P], v[:, 0, kg, :], start=True, stop=True)
                    nc.tensor.matmul(heads_out[1][:, cols], pT[:, P:2 * P], v[:, 0, kg, :], start=True, stop=False)
                    nc.tensor.matmul(heads_out[1][:, cols], pT[:, 2 * P:3 * P], v[:, 1, kg, :],
                                     start=False, stop=True).then_inc(pv_done, 1)

                if not rope:
                    summed.wait_empty(pe, b, 2 * TPS - 1)
                score(0)
                score(1)
                for h in range(HEADS):
                    turn_probs(h)
                    if h + 2 < HEADS:
                        score(h + 2)
                    if h >= 1:
                        weigh_values(h - 1)
                weigh_values(HEADS - 1)
                for t in range(TPS):
                    n = OUT0 + t
                    pe.wait_ge(out_ready, TPS * b + t + 1)
                    turned.wait_free(pe, b, n)
                    for c in range(C):
                        last = nc.tensor.transpose(
                            turned.banks[n % 2][:, c * P:(c + 1) * P],
                            out[:, t, :, :].rearrange("p h d -> p (h d)")[:, c * P:(c + 1) * P], ident[:, :])
                    last.then_inc(turned.filled[n % 2], 1)
                for t in range(TPS):
                    n, use = OUT0 + t, 2 * TPS + t
                    turned.wait_empty(pe, b, n)
                    summed.wait_free(pe, b, use)
                    for c in range(C):
                        last = nc.tensor.matmul(summed.banks[use % 2][:, :], outT[:, c, t * P:(t + 1) * P],
                                                w_o[:, c, :], start=(c == 0), stop=(c == C - 1))
                    last.then_inc(summed.filled[use % 2], 1)


class Bank:

    def __init__(self, layer, name, lead, first, body, last, rounds):
        self.tile = layer.bank(name)
        self.filled = layer.sem(f"{name}_filled")
        self.emptied = layer.sem(f"{name}_emptied")
        self.order = {"lead": lead, "first": first, "body": body, "last": last}
        head = len(lead) + len(first)
        self.start = {"lead": lambda r: 0, "first": lambda r: len(lead),
                      "body": lambda r: head + len(body) * (r - 1),
                      "last": lambda r: head + len(body) * (rounds - 1)}

    def before(self, step, use):
        phase, r = step
        return self.start[phase](r) + self.order[phase].index(use)

    def wait_free(self, pe, step, use):
        pe.wait_ge(self.emptied, 1 + self.before(step, use))

    def open(self, pe):
        pe.sem_inc(self.emptied, 1)

    def wait_full(self, eng, step, use):
        eng.wait_ge(self.filled, self.before(step, use) + 1)

    def wait_empty(self, eng, step, use):
        eng.wait_ge(self.emptied, 1 + self.before(step, use) + 1)


def normalise_all(core, name, xT_all):
    with ExitStack() as ctx:
        L = Layer(core, ctx, f"{name}_norm")
        turned = Ring(L, "turned", TPS)
        ln = LayerNorm(L, turned)
        block = ctx.enter_context(core.nc.Block())

        @block.vector
        def _(dve):
            with dve.Fori(0, B) as b:
                ln.vector(dve, b)

        @block.scalar
        def _(act):
            with act.Fori(0, B) as b:
                ln.scalar(act, b)
                ln.scalar_xT(act, b, xT_all[:, b, :, :])

        @block.tensor
        def _(pe):
            turned.open(pe)
            with pe.Fori(0, B) as b:
                ln.tensor(pe, b)


def wide_attention(core, name, linear):
    nc, dram, X, ident = core.nc, core.dram, core.X, core.ident
    HD = 128
    UNITS = KV_HEADS * B
    QN = GROUP * HD
    RN = QN + HD
    QKV = RN + HD
    BLK = 32
    NB = S // BLK
    BPT = P // BLK
    ROUNDS = UNITS - 1
    CHUNKS = KV_HEADS * C
    IN_AHEAD, OUT_AHEAD = 5, 3

    with ExitStack() as ctx:
        xT_all = ctx.enter_context(nc.sbuf_tensor(f"{name}_xT_all", [P, B, C, S], F32))
        normalise_all(core, name, xT_all)
        L = Layer(core, ctx, name)
        lin = linear
        summed = [Bank(L, "summed0", ["q0", "kv"], ["q0", "kv"], ["q0", "kv", "wo1"], ["wo1", "end_wo1"], ROUNDS),
                  Bank(L, "summed1", ["q1"], ["q1"], ["q1", "wo0"], ["wo0", "end_wo0"], ROUNDS)]
        if lin:
            t0, t1 = ["q0", "qs0"], ["kk", "q1", "qs1"]
            s0, s1 = ["S0", "S2", "G0", "G2"], ["S1", "S3", "G1"]
        else:
            t0, t1 = ["q0"], ["q1"]
            s0, s1 = ["S0", "S2"], ["S1", "S3"]
        turned = [Bank(L, f"turned{k}", t, p + t, p + t, p, ROUNDS)
                  for k, (p, t) in enumerate(((["P0", "P2"], t0), (["P1", "P3"], t1)))]
        scores = [Bank(L, f"scores{k}", x, n + x, n + x, n, ROUNDS) for k, (n, x) in enumerate(((s0, ["k"]), (s1, [])))]
        heads = [L.bank(f"heads{t}") for t in range(TPS)]

        raw_in = L.sb("raw_in", [P, 2, QKV])
        raw_out = L.sb("raw_out", [P, 2, D])
        w_in = [L.sb(f"w_in_{part}", [P, 2 * C, QKV], F32R) for part in ("high", "low")]
        w_out = [L.sb(f"w_out_{part}", [P, 2 * GROUP, D], F32R) for part in ("high", "low")]
        xT = [L.sb(f"xT_{part}", [P, C, S], F32R) for part in ("high", "low")]
        cos = L.sb("cos", [P, TPS, HD])
        sin = L.sb("sin", [P, TPS, HD])
        qkv = L.sb("qkv", [P, TPS, QKV])
        straight = L.sb("straight", [P, TPS, RN])
        crossed = L.sb("crossed", [P, RN])
        v = L.sb("v", [P, TPS, HD])
        qT = L.sb("qT", [P, TPS, GROUP, P])
        kT = L.sb("kT", [P, S])
        masked = L.sb("masked", [P, 2, SCORE_COLS])
        neg_max = L.sb("neg_max", [P, GROUP, TPS])
        total = L.sb("total", [P, GROUP, TPS])
        r_total = L.sb("r_total", [P, GROUP, TPS])
        probs = L.sb("probs", [P, 2, SCORE_COLS])
        probsT = L.sb("probsT", [P, 2, SCORE_COLS])
        outT = [L.sb(f"outT_{part}", [P, TPS, GROUP, P], F32R)
                for part in (("high",) if lin else ("high", "low"))]
        if lin:
            mask = L.sb("mask", [P, SCORE_COLS])
            half_mask = L.sb("half_mask", [P, BPT, GROUP * BLK])
            out_bf = L.sb("out_bf", [P, TPS, GROUP, P], BF16)
            neg_kq_max = L.sb("neg_kq_max", [P, TPS, GROUP + 1])
            kq_total = L.sb("kq_total", [P, TPS, GROUP + 1])
            r_kq_total = L.sb("r_kq_total", [P, TPS, GROUP + 1])
            r_half_k_total = L.sb("r_half_k_total", [P, TPS])
            kq_exp = L.sb("kq_exp", [P, TPS, RN])
            shifted_k = L.sb("shifted_k", [P, TPS, HD])
            kk = L.sb("kk", [P, 2, S])
            min_k = L.sb("min_k", [P, S])
            neg_abs_k = L.sb("neg_abs_k", [P, S])
            exp_abs_k = L.sb("exp_abs_k", [P, S])
            soft = L.sb("soft", [P, S])
            G = L.sb("G", [P, S])
            R = L.sb("R", [P, NB])
            key_log = L.sb("key_log", [P, S])
            decay_log = L.sb("decay_log", [P, S])
            decay = L.sb("decay", [P, S])
            qf = L.sb("qf", [P, GROUP, S])
            kf = [L.sb(f"kf{n}", [P, BPT, P]) for n in range(3)]
            A = [L.sb(f"A{n}", [P, BPT, GROUP * BLK]) for n in range(3)]
        else:
            mask = core.mask

        in_loaded = L.sem("in_loaded")
        out_loaded = L.sem("out_loaded")
        in_high_ready = L.sem("in_high_ready")
        out_high_ready = L.sem("out_high_ready")
        in_split = L.sem("in_split")
        out_split = L.sem("out_split")
        xT_high_ready = L.sem("xT_high_ready")
        heads_high_ready = L.sem("heads_high_ready")
        kT_ready = L.sem("kT_ready")
        heads_emptied = L.sem("heads_emptied")
        tables_loaded = L.sem("tables_loaded")
        xT_ready = L.sem("xT_ready")
        v_ready = L.sem("v_ready")
        rope_parts = L.sem("rope_parts")
        rope_ready = L.sem("rope_ready")
        exp_ready = L.sem("exp_ready")
        r_total_ready = L.sem("r_total_ready")
        probs_ready = L.sem("probs_ready")
        probs_scaled = L.sem("probs_scaled")
        masked_ready = L.sem("masked_ready")
        pv_done = L.sem("pv_done")
        out_f32 = L.sem("out_f32")
        if lin:
            zeroed = L.sem("zeroed")
            max_ready = L.sem("kq_max_ready")
            kq_exp_ready = L.sem("kq_exp_ready")
            r_kq_ready = L.sem("r_kq_ready")
            r_half_ready = L.sem("r_half_ready")
            shifted_ready = L.sem("shifted_ready")
            qs_ready = L.sem("qs_ready")
            min_ready = L.sem("min_ready")
            abs_ready = L.sem("abs_ready")
            exp_abs_ready = L.sem("exp_abs_ready")
            soft_ready = L.sem("soft_ready")
            G_ready = L.sem("G_ready")
            R_ready = L.sem("R_ready")
            decay_log_ready = L.sem("decay_log_ready")
            decay_ready = L.sem("decay_ready")
            kf_ready = L.sem("kf_ready")
            linear_kept = [L.sem(f"linear_kept{k}") for k in range(2)]
            linear_done = L.sem("linear_done")
        block = ctx.enter_context(nc.Block())

        def wait_heads(eng, u):
            if lin:
                eng.wait_ge(linear_done, u + 1)
            else:
                eng.wait_ge(pv_done, GROUP * (u + 1))

        def wait_projected(eng, step):
            summed[0].wait_full(eng, step, "wo1")

        @block.sync
        def _(sp):
            sp.dma_start(cos[:, :, :], dram["wide_cos"]).then_inc(tables_loaded, 16)
            sp.dma_start(sin[:, :, :], dram["wide_sin"]).then_inc(tables_loaded, 16)
            if lin:
                sp.dma_start(mask[:, :], dram["window_mask"]).then_inc(tables_loaded, 16)
                sp.dma_start(half_mask[:, :, :], dram["half_mask"]).then_inc(tables_loaded, 16)

            ins = dram[f"{name}_w_in"].rearrange("g (c p) n -> (g c) p n", p=P)
            outs = dram[f"{name}_w_o"].rearrange("g (h p) n -> (g h) p n", p=P)

            def load_in(p):
                if p >= 1:
                    sp.wait_ge(in_loaded, 16 * p)
                if p >= 2:
                    sp.wait_ge(in_split, p - 1)
                sp.dma_start(raw_in[:, p % 2, :], ins[p, :, :]).then_inc(in_loaded, 16)

            def load_out(p):
                if p >= 1:
                    sp.wait_ge(out_loaded, 16 * p)
                if p >= 2:
                    sp.wait_ge(out_split, p - 1)
                sp.dma_start(raw_out[:, p % 2, :], outs[p, :, :]).then_inc(out_loaded, 16)

            for p in range(IN_AHEAD):
                load_in(p)
            for p in range(OUT_AHEAD):
                load_out(p)
            with sp.Fori(0, ROUNDS) as u:
                sp.wait_ge(in_loaded, 16 * (u + IN_AHEAD))
                core.carry_wait(sp)
                sp.wait_ge(in_split, u + IN_AHEAD - 1)
                core.carry_wait(sp)
                sp.dma_start(raw_in[:, (u + IN_AHEAD) % 2, :], ins[(u + IN_AHEAD) % CHUNKS, :, :])\
                    .then_inc(in_loaded, 16)
                sp.wait_ge(out_loaded, 16 * (u + OUT_AHEAD))
                core.carry_wait(sp)
                sp.wait_ge(out_split, u + OUT_AHEAD - 1)
                core.carry_wait(sp)
                sp.dma_start(raw_out[:, (u + OUT_AHEAD) % 2, :], outs[(u + OUT_AHEAD) % CHUNKS, :, :])\
                    .then_inc(out_loaded, 16)

        tables = 16 * (4 if lin else 2)

        @block.gpsimd
        def _(pool):
            if lin:
                for n in (0, 2):
                    nc.gpsimd.memset(kf[n][:, :, :], 0.0).then_inc(zeroed, 1)

            def copy_v(step, u):
                summed[0].wait_empty(pool, step, "kv")
                core.carry_wait(pool)
                nc.gpsimd.tensor_copy(v[:, :, :], qkv[:, :, RN:QKV]).then_inc(v_ready, 1)

            def round_out(step, u):
                for t in range(TPS):
                    pool.wait_ge(heads_emptied, 1 + TPS * u + t + 1)
                    if t == 0 and step[0] != "first":
                        wait_projected(pool, step)
                    core.carry_wait(pool)
                    nc.gpsimd.tensor_copy(outT[0][:, t, :, :], out_bf[:, t, :, :]).then_inc(out_f32, 1)

            if lin:
                pool.sem_inc(out_f32, 1)
            copy_v(("lead", 0), 0)

            def advance(step, u):
                summed[0].wait_full(pool, step, "q0")
                pool.wait_ge(in_loaded, 16 * (u + IN_AHEAD + 1))
                pool.wait_ge(out_loaded, 16 * (u + OUT_AHEAD + 1))
                core.carry_wait(pool)
                p = u + IN_AHEAD
                nc.gpsimd.tensor_copy(w_in[0][:, p % (2 * C), :], raw_in[:, p % 2, :]).then_inc(in_high_ready, 1)
                p = u + OUT_AHEAD
                nc.gpsimd.tensor_copy(w_out[0][:, p % (2 * GROUP), :], raw_out[:, p % 2, :])\
                    .then_inc(out_high_ready, 1)
                wait_heads(pool, u)
                copy_v(step, u + 1)
                if lin:
                    round_out(step, u)

            advance(("first", 0), 0)
            with pool.Fori(1, ROUNDS) as u:
                advance(("body", u), u)
            if lin:
                round_out(("last", 0), ROUNDS)

        @block.vector
        def _(dve):
            dve.wait_ge(tables_loaded, tables)

            def rope(w):
                for t in range(TPS):
                    heads_of = qkv[:, t, 0:RN].rearrange("p (h d) -> p h d", d=HD)
                    nc.vector.tensor_tensor(straight[:, t, :].rearrange("p (h d) -> p h d", d=HD), heads_of,
                                            cos[:, t, :].unsqueeze(1).to_broadcast([P, GROUP + 1, HD]), ALU.mult)\
                        .then_inc(rope_parts, 1)
                    if t > 0:
                        dve.wait_ge(rope_ready, TPS * w + t)
                    src = qkv[:, t, 0:RN].rearrange("p (h e d) -> p h e d", e=2, d=HD // 2)
                    dst = crossed.rearrange("p (h e d) -> p h e d", e=2, d=HD // 2)
                    sn = sin[:, t, :].rearrange("p (e d) -> p e d", e=2)
                    for e in range(2):
                        nc.vector.tensor_tensor(dst[:, :, e, :], src[:, :, 1 - e, :],
                                                sn[:, e, :].unsqueeze(1).to_broadcast([P, GROUP + 1, HD // 2]),
                                                ALU.mult).then_inc(rope_parts, 1)
                    dve.wait_ge(rope_parts, 3 * (TPS * w + t + 1))
                    nc.vector.tensor_tensor(straight[:, t, :], straight[:, t, :], crossed[:, :], ALU.add)\
                        .then_inc(rope_ready, 1)

            def split_xT(w, b):
                dve.wait_ge(xT_high_ready, w + 1)
                nc.vector.tensor_tensor(xT[1][:, :, :], xT_all[:, b, :, :], xT[0].bitcast(F32)[:, :, :],
                                        ALU.subtract).then_inc(xT_ready, 1)

            def split_in(p):
                dve.wait_ge(in_high_ready, p + 1)
                k = p % (2 * C)
                nc.vector.tensor_tensor(w_in[1][:, k, :], raw_in[:, p % 2, :], w_in[0].bitcast(F32)[:, k, :],
                                        ALU.subtract).then_inc(in_split, 1)

            def split_out(p):
                dve.wait_ge(out_high_ready, p + 1)
                k = p % (2 * GROUP)
                nc.vector.tensor_tensor(w_out[1][:, k, :], raw_out[:, p % 2, :], w_out[0].bitcast(F32)[:, k, :],
                                        ALU.subtract).then_inc(out_split, 1)

            def split_heads(u):
                for t in range(TPS):
                    dve.wait_ge(heads_high_ready, TPS * u + t + 1)
                    nc.vector.tensor_tensor(outT[1][:, t, :, :], heads[t].rearrange("p (h n) -> p h n", h=GROUP),
                                            outT[0].bitcast(F32)[:, t, :, :], ALU.subtract)\
                        .then_inc(heads_emptied, 1)

            def prepare(step, w):
                summed[0].wait_empty(dve, step, "q0")
                summed[1].wait_empty(dve, step, "q1")
                summed[0].wait_empty(dve, step, "kv")
                if lin:
                    for t in range(TPS):
                        nc.vector.tensor_reduce(neg_kq_max[:, t, :],
                                                qkv[:, t, 0:RN].rearrange("p (h d) -> p h d", d=HD),
                                                AX.X, ALU.max, negate=True).then_inc(max_ready, 1)
                    for t in range(TPS):
                        dve.wait_ge(max_ready, TPS * w + t + 1)
                        nc.vector.tensor_scalar(shifted_k[:, t, :], qkv[:, t, QN:RN],
                                                neg_kq_max[:, t, GROUP:GROUP + 1], None, ALU.add)\
                            .then_inc(shifted_ready, 1)
                    if step[0] != "lead":
                        keep_linear(step, 2)
                rope(w)
                if lin:
                    turned[1].wait_empty(dve, step, "kk")
                    nc.vector.tensor_scalar(min_k[:, :], kk[:, 0, :], 0.0, None, ALU.min).then_inc(min_ready, 1)
                    dve.wait_ge(min_ready, w + 1)
                    nc.vector.scalar_tensor_tensor(neg_abs_k[:, :], min_k[:, :], 2.0, kk[:, 0, :], ALU.mult,
                                                   ALU.subtract).then_inc(abs_ready, 1)

            def normalise_q(step, w):
                dve.wait_ge(kq_exp_ready, TPS * (GROUP + 1) * (w + 1))
                if step[0] != "lead":
                    dve.wait_ge(linear_kept[0], 2 * w)
                    dve.wait_ge(linear_kept[1], w)
                nc.vector.reciprocal(r_kq_total[:, :, :], kq_total[:, :, :]).then_inc(r_kq_ready, 1)
                dve.wait_ge(r_kq_ready, w + 1)
                nc.vector.tensor_scalar(r_half_k_total[:, :], r_kq_total[:, :, GROUP], 0.5, None, ALU.mult)\
                    .then_inc(r_half_ready, 1)
                for t in range(TPS):
                    nc.vector.tensor_tensor(kq_exp[:, t, 0:QN].rearrange("p (h d) -> p h d", d=HD),
                                            kq_exp[:, t, 0:QN].rearrange("p (h d) -> p h d", d=HD),
                                            r_kq_total[:, t, 0:GROUP].unsqueeze(2).to_broadcast([P, GROUP, HD]),
                                            ALU.mult).then_inc(qs_ready, 1)

            def decays(step, w):
                if step[0] != "lead":
                    dve.wait_ge(kf_ready, 3 * BPT * w)
                dve.wait_ge(soft_ready, w + 1)
                nc.vector.tensor_tensor_scan(G[:, :], min_k[:, :], soft[:, :], 0.0, ALU.add, ALU.subtract)\
                    .then_inc(G_ready, 1)
                dve.wait_ge(G_ready, w + 1)
                nc.vector.tensor_scalar(R[:, :], G[:, BLK // 2 - 1:S:BLK], 1.0 / 16, None, ALU.mult)\
                    .then_inc(R_ready, 1)
                nc.vector.scalar_tensor_tensor(key_log[:, :], G[:, :], -1.0 / 16, kk[:, 1, :], ALU.mult, ALU.add)\
                    .then_inc(R_ready, 1)
                nc.vector.tensor_tensor(decay_log[:, :].rearrange("p (n s) -> p n s", s=BLK),
                                        G[:, :].rearrange("p (n s) -> p n s", s=BLK),
                                        G[:, BLK // 2 - 1:S:BLK].unsqueeze(2).to_broadcast([P, NB, BLK]),
                                        ALU.subtract).then_inc(decay_log_ready, 1)

            def decayed_queries(step, w):
                dve.wait_ge(decay_ready, w + 1)
                for t in range(TPS):
                    turned[t].wait_full(dve, step, f"qs{t}")
                    nc.vector.tensor_tensor(qf[:, :, t * P:(t + 1) * P],
                                            turned[t].tile.rearrange("p (h n) -> p h n", h=GROUP),
                                            decay[:, t * P:(t + 1) * P].unsqueeze(1).to_broadcast([P, GROUP, P]),
                                            ALU.mult).then_inc(turned[t].emptied, 1)

            def mask_scores(step, u, h):
                k = h % 2
                scores[k].wait_full(dve, step, f"S{h}")
                core.carry_wait(dve)
                if h >= 2:
                    dve.wait_ge(exp_ready, TPS * (GROUP * u + h - 1))
                    core.carry_wait(dve)
                for t in range(TPS):
                    ins = nc.vector.tensor_tensor_reduce(masked[:, k, SPAN[t]], scores[k].tile[:, SPAN[t]],
                                                         mask[:, SPAN[t]], 1.0, 3e38, ALU.add, ALU.min,
                                                         neg_max[:, h, t:t + 1])
                    ins.then_inc(masked_ready, 1)

            def scale_probs(u, h):
                k = h % 2
                dve.wait_ge(exp_ready, TPS * (GROUP * u + h + 1))
                nc.vector.reciprocal(r_total[:, h, :], total[:, h, :]).then_inc(r_total_ready, 1)
                dve.wait_ge(r_total_ready, GROUP * u + h + 1)
                for t in range(TPS):
                    nc.vector.tensor_scalar(probs[:, k, SPAN[t]], probs[:, k, SPAN[t]], r_total[:, h, t:t + 1],
                                            0.5 if lin else 1.0, ALU.mult, ALU.mult).then_inc(probs_scaled, 1)

            def keep_linear(step, n):
                k = scores[n % 2]
                k.wait_full(dve, step, f"G{n}")
                nc.vector.scalar_tensor_tensor(A[n][:, :, :], k.tile.rearrange("p (i m) -> p i m", i=BPT),
                                               r_kq_total[:, n // 2, GROUP:GROUP + 1], half_mask[:, :, :],
                                               ALU.mult, ALU.mult).then_inc(linear_kept[0], 1)

            def attend(step, u, more):
                mask_scores(step, u, 0)
                mask_scores(step, u, 1)
                if lin:
                    decayed_queries(("lead", 0) if step[0] == "first" else ("body", u - 1), u)
                elif step[0] != "first":
                    split_heads(u - 1)
                for h in range(GROUP):
                    scale_probs(u, h)
                    if h == 2 and more:
                        split_in(u + IN_AHEAD)
                        split_out(u + OUT_AHEAD)
                    if h + 2 < GROUP:
                        mask_scores(step, u, h + 2)
                if lin:
                    keep_linear(step, 0)

            def add_out(step, b, end=""):
                for t in range(TPS):
                    k = summed[1 - t]
                    k.wait_full(dve, step, f"{end}wo{t}")
                    nc.vector.tensor_tensor(X[:, TPS * b + t, :], X[:, TPS * b + t, :], k.tile[:, :], ALU.add)\
                        .then_inc(k.emptied, 1)

            def advance(step, u, more=True, out=True):
                attend(step, u, more)
                if more:
                    split_xT(u + 2, (u + 2) % B)
                    prepare(step, u + 1)
                elif lin:
                    keep_linear(step, 2)
                if lin and more:
                    normalise_q(step, u + 1)
                if out:
                    add_out(step, (u + B - 1) % B)
                if lin and more:
                    decays(step, u + 1)

            split_xT(0, 0)
            for p in range(IN_AHEAD):
                split_in(p)
                if p == C - 1:
                    split_xT(1, 1)
                    prepare(("lead", 0), 0)
            for p in range(OUT_AHEAD):
                split_out(p)
            if lin:
                normalise_q(("lead", 0), 0)
                decays(("lead", 0), 0)
            advance(("first", 0), 0, out=False)
            with dve.Fori(1, ROUNDS) as u:
                advance(("body", u), u)
            advance(("last", 0), ROUNDS, more=False)
            if not lin:
                split_heads(ROUNDS)
            add_out(("last", 0), ROUNDS % B, "end_")

        @block.scalar
        def _(act):
            def take_q(step, w, t):
                k = summed[t]
                k.wait_full(act, step, f"q{t}")
                if w is not None:
                    act.wait_ge(rope_ready, TPS * w)
                    if lin:
                        act.wait_ge(kq_exp_ready, TPS * (GROUP + 1) * w)
                nc.scalar.copy(qkv[:, t, 0:QN], k.tile[:, :]).then_inc(k.emptied, 1)

            def take_kv(step, w):
                summed[0].wait_full(act, step, "kv")
                if w is not None:
                    act.wait_ge(v_ready, w)
                    if lin:
                        act.wait_ge(shifted_ready, TPS * w)
                nc.scalar.copy(qkv[:, :, QN:QKV], summed[0].tile.rearrange("p (t n) -> p t n", t=TPS))\
                    .then_inc(summed[0].emptied, 1)

            def take_xT(w, b):
                nc.scalar.copy(xT[0][:, :, :], xT_all[:, b, :, :]).then_inc(xT_high_ready, 1)

            def high_in(p):
                act.wait_ge(in_loaded, 16 * (p + 1))
                nc.scalar.copy(w_in[0][:, p, :], raw_in[:, p % 2, :]).then_inc(in_high_ready, 1)

            def high_out(p):
                act.wait_ge(out_loaded, 16 * (p + 1))
                nc.scalar.copy(w_out[0][:, p, :], raw_out[:, p % 2, :]).then_inc(out_high_ready, 1)

            def softmax_qk(step, w):
                if step[0] != "lead":
                    before = ("lead", 0) if step[0] == "first" else ("body", w - 2)
                    turned[0].wait_full(act, before, "qs0")
                    turned[1].wait_full(act, before, "qs1")
                for t in range(TPS):
                    act.wait_ge(max_ready, TPS * w + t + 1)
                    for h in reversed(range(GROUP + 1)):
                        cols = slice(HD * h, HD * (h + 1))
                        nc.scalar.activation(kq_exp[:, t, cols], qkv[:, t, cols], ACT.Exp,
                                             bias=neg_kq_max[:, t, h:h + 1], accum_out=kq_total[:, t, h:h + 1])\
                            .then_inc(kq_exp_ready, 1)
                    if t == 0:
                        turned[1].wait_full(act, step, "kk")
                        nc.scalar.copy(kk[:, :, :], turned[1].tile.rearrange("p (a n) -> p a n", a=2))\
                            .then_inc(turned[1].emptied, 1)

            def turn_in(step, w):
                def take_q_turned(t):
                    turned[t].wait_full(act, step, f"q{t}")
                    nc.scalar.copy(qT[:, t, :, :], turned[t].tile.rearrange("p (h n) -> p h n", h=GROUP))\
                        .then_inc(turned[t].emptied, 1)

                take_q_turned(0)
                scores[0].wait_full(act, step, "k")
                nc.scalar.mul(kT[:, :], scores[0].tile[:, 0:S], -float(HD) ** -0.5).then_inc(kT_ready, 1)
                take_q_turned(1)
                if lin:
                    act.wait_ge(abs_ready, w + 1)
                    nc.scalar.activation(exp_abs_k[:, :], neg_abs_k[:, :], ACT.Exp).then_inc(exp_abs_ready, 1)
                    act.wait_ge(exp_abs_ready, w + 1)
                    nc.scalar.activation(soft[:, :], exp_abs_k[:, :], ACT.Ln, bias=core.one[:, 0:1])\
                        .then_inc(soft_ready, 1)
                if lin:
                    act.wait_ge(decay_log_ready, w + 1)
                    nc.scalar.activation(decay[:, :], decay_log[:, :], ACT.Exp, scale=1.0 / 16)\
                        .then_inc(decay_ready, 1)

            def decayed_keys(u, n):
                block0, key0 = ((0, 0), (BPT, 0), (BPT, P))[n]
                if n == 0:
                    act.wait_ge(R_ready, 2 * (u + 1))
                    act.wait_ge(zeroed, 2)
                for i in range(BPT):
                    cols = P if n == 1 else BLK * (i + 1)
                    nc.scalar.activation(kf[n][:, i, 0:cols], key_log[:, key0:key0 + cols], ACT.Exp,
                                         bias=R[:, block0 + i:block0 + i + 1]).then_inc(kf_ready, 1)

            def exponentials(u, h):
                k = h % 2
                for t in range(TPS):
                    act.wait_ge(masked_ready, TPS * (GROUP * u + h) + t + 1)
                    nc.scalar.activation(probs[:, k, SPAN[t]], masked[:, k, SPAN[t]], ACT.Exp,
                                         bias=neg_max[:, h, t:t + 1], scale=-1.0,
                                         accum_out=total[:, h, t:t + 1]).then_inc(exp_ready, 1)

            def take_probsT(step, u, h):
                k = h % 2
                turned[k].wait_full(act, step, f"P{h}")
                if h >= 2:
                    act.wait_ge(pv_done, GROUP * u + h - 1)
                nc.scalar.copy(probsT[:, k, :], turned[k].tile[:, 0:SCORE_COLS]).then_inc(turned[k].emptied, 1)

            def take_out(step, u):
                wait_heads(act, u)
                if lin:
                    act.wait_ge(out_f32, 1 + TPS * u)
                elif step[0] != "first":
                    wait_projected(act, step)
                for t in range(TPS):
                    nc.scalar.copy((out_bf if lin else outT[0])[:, t, :, :],
                                   heads[t].rearrange("p (h n) -> p h n", h=GROUP))\
                        .then_inc(heads_emptied if lin else heads_high_ready, 1)

            def attend(step, u, more):
                exponentials(u, 0)
                exponentials(u, 1)
                if more:
                    take_q(step, u + 1, 0)
                if lin:
                    decayed_keys(u, 0)
                if more:
                    take_q(step, u + 1, 1)
                take_probsT(step, u, 0)
                exponentials(u, 2)
                take_probsT(step, u, 1)
                exponentials(u, 3)
                if lin:
                    decayed_keys(u, 1)
                if more:
                    take_kv(step, u + 1)
                    take_xT(u + 2, (u + 2) % B)
                take_probsT(step, u, 2)
                if lin:
                    decayed_keys(u, 2)
                take_probsT(step, u, 3)
                if lin:
                    scores[1].wait_full(act, step, "G1")
                    act.wait_ge(r_half_ready, u + 1)
                    nc.scalar.mul(A[1][:, :, :], scores[1].tile.rearrange("p (i m) -> p i m", i=BPT),
                                  r_half_k_total[:, 0:1]).then_inc(linear_kept[1], 1)
                    if more:
                        softmax_qk(step, u + 1)
                    take_out(step, u)
                if more:
                    turn_in(step, u + 1)
                if not lin:
                    take_out(step, u)

            lead = ("lead", 0)
            take_xT(0, 0)
            for p in range(C):
                high_in(p)
            take_q(lead, None, 0)
            take_q(lead, None, 1)
            take_kv(lead, None)
            take_xT(1, 1)
            if lin:
                softmax_qk(lead, 0)
            for p in range(C, IN_AHEAD):
                high_in(p)
            for p in range(OUT_AHEAD):
                high_out(p)
            turn_in(lead, 0)
            attend(("first", 0), 0, True)
            with act.Fori(1, ROUNDS) as u:
                attend(("body", u), u, True)
            attend(("last", 0), ROUNDS, False)

        @block.tensor
        def _(pe):
            def weights(w):
                return w // B % 2 * C

            def project_q(step, w, g2, t):
                k = summed[t]
                if t == 0:
                    pe.wait_ge(xT_ready, w + 1)
                    pe.wait_ge(in_split, C * (w // B + 1))
                k.wait_free(pe, step, f"q{t}")
                for c in range(C):
                    last = split_matmul(nc, k.tile[:, :], [x[:, c, t * P:(t + 1) * P] for x in xT],
                                        [w_[:, g2 + c, 0:QN] for w_ in w_in], c == 0, c == C - 1)
                last.then_inc(k.filled, 1)

            def project_kv(step, w, g2):
                k = summed[0]
                k.wait_free(pe, step, "kv")
                for t in range(TPS):
                    for c in range(C):
                        last = split_matmul(nc, k.tile[:, t * 2 * HD:(t + 1) * 2 * HD],
                                            [x[:, c, t * P:(t + 1) * P] for x in xT],
                                            [w_[:, g2 + c, QN:QKV] for w_ in w_in], c == 0, c == C - 1)
                last.then_inc(k.filled, 1)

            def turn_kk(step, w):
                turned[1].wait_free(pe, step, "kk")
                pe.wait_ge(shifted_ready, TPS * (w + 1))
                for a in range(2):
                    for t in range(TPS):
                        src = qkv[:, t, QN:RN] if a == 0 else shifted_k[:, t, :]
                        last = nc.tensor.transpose(turned[1].tile[:, a * S + t * P:a * S + (t + 1) * P],
                                                   src, ident[:, :])
                last.then_inc(turned[1].filled, 1)

            def turn_in(step, w):
                for t in range(TPS):
                    pe.wait_ge(rope_ready, TPS * w + t + 1)
                    turned[t].wait_free(pe, step, f"q{t}")
                    for h in range(GROUP):
                        last = nc.tensor.transpose(turned[t].tile[:, h * P:(h + 1) * P],
                                                   straight[:, t, h * HD:(h + 1) * HD], ident[:, :])
                    last.then_inc(turned[t].filled, 1)
                    if t == 0:
                        pe.wait_ge(rope_ready, TPS * (w + 1))
                        if lin and step[0] != "lead":
                            pe.wait_ge(linear_kept[0], 2 * w)
                        for k in range(TPS):
                            last = nc.tensor.transpose(scores[0].tile[:, k * P:(k + 1) * P], straight[:, k, QN:RN],
                                                       ident[:, :])
                        last.then_inc(scores[0].filled, 1)
                if lin:
                    for t in range(TPS):
                        pe.wait_ge(qs_ready, TPS * w + t + 1)
                        turned[t].wait_free(pe, step, f"qs{t}")
                        for h in range(GROUP):
                            last = nc.tensor.transpose(turned[t].tile[:, h * P:(h + 1) * P],
                                                       kq_exp[:, t, h * HD:(h + 1) * HD], ident[:, :])
                        last.then_inc(turned[t].filled, 1)

            def score(step, u, h):
                k = scores[h % 2]
                if h >= 2:
                    pe.wait_ge(masked_ready, TPS * (GROUP * u + h - 1))
                for t in range(TPS):
                    last = nc.tensor.matmul(k.tile[:, SPAN[t]], qT[:, t, h, :], kT[:, 0:(t + 1) * P],
                                            start=True, stop=True)
                last.then_inc(k.filled, 1)

            def turn_probs(step, u, h):
                k = turned[h % 2]
                pe.wait_ge(probs_scaled, TPS * (GROUP * u + h + 1))
                k.wait_free(pe, step, f"P{h}")
                for j in range(SCORE_COLS // P):
                    last = nc.tensor.transpose(k.tile[:, j * P:(j + 1) * P], probs[:, h % 2, j * P:(j + 1) * P],
                                               ident[:, :])
                last.then_inc(k.filled, 1)

            def weigh(step, u, h):
                turned[h % 2].wait_empty(pe, step, f"P{h}")
                pT = probsT[:, h % 2, :]
                if h == 0:
                    pe.wait_ge(v_ready, u + 1)
                    pe.wait_ge(heads_emptied, 1 + TPS * u)
                cols = slice(h * P, (h + 1) * P)
                end = not lin
                nc.tensor.matmul(heads[0][:, cols], v[:, 0, :], pT[:, 0:P], start=(h == 0), stop=end,
                                 skip_group_check=True)
                nc.tensor.matmul(heads[1][:, cols], v[:, 0, :], pT[:, P:2 * P], start=(h == 0), stop=False,
                                 skip_group_check=True)
                nc.tensor.matmul(heads[1][:, cols], v[:, 1, :], pT[:, 2 * P:3 * P], start=False, stop=end,
                                 skip_group_check=True).then_inc(pv_done, 1)

            def linear_scores(step, u, n):
                k = scores[n % 2]
                pe.wait_ge(kf_ready, BPT * (3 * u + n + 1))
                if n == 0:
                    pe.wait_ge(masked_ready, TPS * (GROUP * u + 3))
                elif n == 1:
                    pe.wait_ge(masked_ready, TPS * (GROUP * u + 4))
                else:
                    pe.wait_ge(linear_kept[0], 2 * u + 1)
                block0 = 0 if n == 0 else BPT
                for i in range(BPT):
                    at = BLK * (block0 + i)
                    last = nc.tensor.matmul(k.tile[:, i * P:(i + 1) * P], kf[n][:, i, :], qf[:, :, at:at + BLK],
                                            start=True, stop=True)
                last.then_inc(k.filled, 1)

            def linear_values(u, n):
                pe.wait_ge(linear_kept[n % 2], {0: 2 * u + 1, 1: u + 1, 2: 2 * u + 2}[n])
                out = heads[0 if n == 0 else 1].rearrange("p (h n) -> p h n", h=GROUP)
                for i in range(BPT):
                    last = nc.tensor.matmul(out[:, :, BLK * i:BLK * (i + 1)], v[:, n // 2, :],
                                            A[n][:, i, :].rearrange("p (h s) -> p h s", h=GROUP),
                                            start=False, stop=(n != 1), skip_group_check=True)
                if n == 2:
                    last.then_inc(linear_done, 1)

            def project_out(step, u, tiles, end=""):
                pe.wait_ge(out_split, GROUP * (u // B + 1))
                for t in tiles:
                    k = summed[1 - t]
                    if lin:
                        pe.wait_ge(out_f32, 1 + TPS * u + t + 1)
                    else:
                        pe.wait_ge(heads_emptied, 1 + TPS * u + t + 1)
                    k.wait_free(pe, step, f"{end}wo{t}")
                    for h in range(GROUP):
                        last = split_matmul(nc, k.tile[:, :], [o[:, t, h, :] for o in outT],
                                            [w_[:, weights(u) + h, :] for w_ in w_out], h == 0, h == GROUP - 1)
                    last.then_inc(k.filled, 1)

            def attend(step, arrived, u, more=True, out=True):
                g2 = weights(u + 1) if more else None
                turned[0].wait_empty(pe, arrived, "q0")
                turned[1].wait_empty(pe, arrived, "q1")
                pe.wait_ge(kT_ready, u + 1)
                score(step, u, 0)
                score(step, u, 1)
                if more:
                    project_q(step, u + 1, g2, 0)
                score(step, u, 2)
                if more:
                    project_q(step, u + 1, g2, 1)
                score(step, u, 3)
                turn_probs(step, u, 0)
                turn_probs(step, u, 1)
                if more:
                    project_kv(step, u + 1, g2)
                weigh(step, u, 0)
                turn_probs(step, u, 2)
                weigh(step, u, 1)
                if lin:
                    turned[0].wait_empty(pe, arrived, "qs0")
                    turned[1].wait_empty(pe, arrived, "qs1")
                    linear_scores(step, u, 0)
                    linear_scores(step, u, 1)
                turn_probs(step, u, 3)
                if out and not lin:
                    project_out(step, u - 1, [0])
                weigh(step, u, 2)
                if out and not lin:
                    project_out(step, u - 1, [1])
                if lin:
                    linear_scores(step, u, 2)
                weigh(step, u, 3)
                if lin:
                    linear_values(u, 0)
                    linear_values(u, 1)
                    if more:
                        turn_kk(step, u + 1)
                    linear_values(u, 2)
                if out and lin:
                    project_out(step, u - 1, range(TPS))
                if more:
                    turn_in(step, u + 1)

            for k in summed + turned:
                k.open(pe)
            pe.sem_inc(heads_emptied, 1)
            lead = ("lead", 0)
            project_q(lead, 0, 0, 0)
            project_q(lead, 0, 0, 1)
            project_kv(lead, 0, 0)
            if lin:
                turn_kk(lead, 0)
            turn_in(lead, 0)
            attend(("first", 0), lead, 0, out=False)
            with pe.Fori(1, ROUNDS) as u:
                attend(("body", u), ("body", u - 1), u)
            attend(("last", 0), ("body", ROUNDS - 1), ROUNDS, more=False)
            project_out(("last", 0), ROUNDS, range(TPS), "end_")


def routed_ffn(core, name, experts, rank, mode):
    nc, dram, X, ident = core.nc, core.dram, core.X, core.ident
    E, ER = experts, experts * rank
    RC = E + ER
    bias = mode != "top1"
    logit_bias = mode != "top2"
    T_USES = 2 * TPS
    R_USES = 2 * TPS if mode == "sequence" else TPS

    with ExitStack() as ctx:
        L = Layer(core, ctx, name)
        turned = Ring(L, "turned", T_USES)
        routed = Ring(L, "routed", R_USES)
        summed = Ring(L, "summed", TPS)
        ln = LayerNorm(L, turned)
        w = L.sb("w", [P, C, D])
        w_ra = L.sb("w_ra", [P, C, RC])
        w_b = L.sb("w_b", [ER, D])
        if bias:
            b_out = L.sb("b_out", [P, D])
        if logit_bias:
            b_logit = L.sb("b_logit", [P, E])
        if mode == "sequence":
            mean_rows = L.sb("mean_rows", [P, TPS, P])
        KEYS = max(8, E)
        logits = L.sb("logits", [P, TPS, KEYS])
        za = L.sb("za", [P, TPS, ER])
        top = L.sb("top", [P, TPS, 8])
        top_at = L.sb("top_at", [P, TPS, 8], U32)
        top_atf = L.sb("top_atf", [P, TPS, 8])
        iota = L.sb("iota", [P, E])
        expd = L.sb("expd", [P, TPS, 8])
        total = L.sb("total", [P, TPS])
        r_total = L.sb("r_total", [P, TPS])
        p2 = L.sb("p2", [P, TPS])
        weight = L.sb("weight", [P, TPS, E])
        weight2 = L.sb("weight2", [P, TPS, E])
        zw = L.sb("zw", [P, TPS, ER])
        zwT = L.sb("zwT", [P, TPS, P])

        weights_loaded = L.sem("weights_loaded")
        logits_ready = L.sem("logits_ready")
        za_ready = L.sem("za_ready")
        step = L.sem("routing_step")
        expd_ready = L.sem("expd_ready")
        max_ready = L.sem("max_ready")
        zw_ready = L.sem("zw_ready")
        bias_added = L.sem("bias_added")
        n_loads = 4 + bias + logit_bias + (mode == "sequence")
        block = ctx.enter_context(nc.Block())

        @block.sync
        def _(sp):
            sp.dma_start(w[:, :, :], dram[f"{name}_w"].rearrange("(c p) n -> p c n", p=P)).then_inc(weights_loaded, 16)
            sp.dma_start(w_ra[:, :, 0:E], dram[f"{name}_router"].rearrange("(c p) n -> p c n", p=P),
                         allow_slow_non_contiguous=True).then_inc(weights_loaded, 16)
            sp.dma_start(w_ra[:, :, E:RC], dram[f"{name}_A"].rearrange("(c p) n -> p c n", p=P)).then_inc(weights_loaded, 16)
            sp.dma_start(w_b[:, :], dram[f"{name}_B"]).then_inc(weights_loaded, 16)
            if bias:
                sp.dma_start(b_out[:, :], dram[f"{name}_b"].partition_broadcast(P)).then_inc(weights_loaded, 16)
            if logit_bias:
                sp.dma_start(b_logit[:, :], dram[f"{name}_router_b"].partition_broadcast(P))\
                    .then_inc(weights_loaded, 16)
            if mode == "sequence":
                sp.dma_start(mean_rows[:, :, :], dram["mean_rows"]).then_inc(weights_loaded, 16)

        def apply_weights(dve, t):
            nc.vector.tensor_tensor(zw[:, t, :].rearrange("p (e r) -> p e r", e=E),
                                    za[:, t, :].rearrange("p (e r) -> p e r", e=E),
                                    weight[:, t, :].unsqueeze(2).to_broadcast([P, E, rank]),
                                    ALU.mult).then_inc(zw_ready, 1)

        @block.gpsimd
        def _(pool):
            if bias:
                pool.wait_ge(weights_loaded, 16 * n_loads)
                with pool.Fori(0, B) as b:
                    for t in range(TPS):
                        pool.wait_ge(ln.xn_ready, TPS * b + t + 1)
                        nc.gpsimd.tensor_tensor(X[:, TPS * b + t, :], X[:, TPS * b + t, :], b_out[:, :], ALU.add)\
                            .then_inc(bias_added, 1)

        @block.vector
        def _(dve):
            dve.wait_ge(weights_loaded, 16 * n_loads)
            if mode != "sequence":
                for e in range(E):
                    nc.vector.memset(iota[:, e:e + 1], float(e)).then_inc(step, 1)
                nc.vector.memset(logits[:, :, :], -3e38).then_inc(step, 1)
                base = E + 1
                dve.wait_ge(step, base)
            else:
                base = 0
            with dve.Fori(0, B) as b:
                count = [0]
                per = {"sequence": 6, "top1": 4 * TPS, "top2": 10 * TPS}[mode]

                def stepped(ins):
                    count[0] += 1
                    ins.then_inc(step, 1)
                    dve.wait_ge(step, base + b * per + count[0])

                ln.vector(dve, b)
                for t in range(TPS):
                    routed.wait_full(dve, b, t)
                    src = routed.banks[t]
                    if mode == "sequence":
                        nc.vector.tensor_copy(logits[:, t, 0:E], src[:, 0:E]).then_inc(logits_ready, 1)
                    elif mode == "top1":
                        nc.vector.tensor_tensor(logits[:, t, 0:E], src[:, 0:E], b_logit[:, :], ALU.add)\
                            .then_inc(logits_ready, 1)
                    else:
                        nc.vector.tensor_copy(logits[:, t, 0:E], src[:, 0:E]).then_inc(logits_ready, 1)
                    nc.vector.tensor_copy(za[:, t, :], src[:, E:RC]).then_inc(routed.emptied[t], 1)
                if mode == "sequence":
                    n = TPS
                    routed.wait_full(dve, b, n)
                    stepped(nc.vector.tensor_tensor(top[:, 0, 0:E], routed.banks[n % 2][:, 0:E],
                                                    b_logit[:, :], ALU.add))
                    nc.vector.tensor_reduce(total[:, 1:2], top[:, 0, 0:E], AX.X, ALU.max, negate=True)\
                        .then_inc(max_ready, 1)
                    dve.wait_ge(expd_ready, b + 1)
                    stepped(nc.vector.reciprocal(r_total[:, 0:1], total[:, 0:1]))
                    stepped(nc.vector.tensor_scalar(weight[:, 0, :], expd[:, 0, 0:E], r_total[:, 0:1], 2.0,
                                                    ALU.mult, ALU.mult))
                    stepped(nc.vector.tensor_scalar(weight[:, 1, :], expd[:, 0, 0:E], r_total[:, 0:1], 2.0,
                                                    ALU.mult, ALU.mult))
                    routed.wait_full(dve, b, n + 1)
                    nc.vector.tensor_copy(total[:, 1:2], routed.banks[(n + 1) % 2][:, 0:1])\
                        .then_inc(routed.emptied[(n + 1) % 2], 1)
                    nc.vector.tensor_copy(p2[:, 0:1], routed.banks[n % 2][:, 0:1])\
                        .then_inc(routed.emptied[n % 2], 1)
                    for t in range(TPS):
                        apply_weights(dve, t)
                else:
                    for t in range(TPS):
                        dve.wait_ge(logits_ready, TPS * b + t + 1)
                        core.carry_wait(dve)
                        stepped(nc.vector.max(top[:, t, :], logits[:, t, :]))
                        core.carry_wait(dve)
                        stepped(nc.vector.max_index(top_at[:, t, :], top[:, t, :], logits[:, t, :]))
                        stepped(nc.vector.tensor_copy(top_atf[:, t, :], top_at[:, t, :]))
                        if mode == "top1":
                            stepped(nc.vector.tensor_scalar(weight[:, t, :], iota[:, :], top_atf[:, t, 0:1],
                                                            None, ALU.is_equal))
                        else:
                            stepped(nc.vector.tensor_tensor(expd[:, t, 0:1], top[:, t, 1:2], top[:, t, 0:1],
                                                            ALU.subtract))
                            nc.vector.tensor_copy(expd[:, t, 2:3], expd[:, t, 0:1]).then_inc(max_ready, 1)
                            dve.wait_ge(expd_ready, TPS * b + t + 1)
                            stepped(nc.vector.tensor_scalar(total[:, t:t + 1], expd[:, t, 1:2], 1.0, None, ALU.add))
                            stepped(nc.vector.reciprocal(r_total[:, t:t + 1], total[:, t:t + 1]))
                            stepped(nc.vector.tensor_scalar(p2[:, t:t + 1], expd[:, t, 1:2], r_total[:, t:t + 1],
                                                            2.0, ALU.mult, ALU.mult))
                            stepped(nc.vector.tensor_scalar(weight[:, t, :], iota[:, :], top_atf[:, t, 0:1],
                                                            r_total[:, t:t + 1], ALU.is_equal, ALU.mult))
                            stepped(nc.vector.tensor_scalar(weight2[:, t, :], iota[:, :], top_atf[:, t, 1:2],
                                                            p2[:, t:t + 1], ALU.is_equal, ALU.mult))
                            stepped(nc.vector.scalar_tensor_tensor(weight[:, t, :], weight[:, t, :], 2.0,
                                                                   weight2[:, t, :], ALU.mult, ALU.add))
                        apply_weights(dve, t)
                assert count[0] <= per
                while count[0] < per:
                    stepped(nc.vector.memset(top_atf[:, 0, 7:8], 0.0))
                if bias:
                    dve.wait_ge(bias_added, TPS * (b + 1))
                for t in range(TPS):
                    summed.wait_full(dve, b, t)
                    nc.vector.tensor_tensor(X[:, TPS * b + t, :], X[:, TPS * b + t, :], summed.banks[t][:, :],
                                            ALU.add).then_inc(summed.emptied[t], 1)

        @block.scalar
        def _(act):
            with act.Fori(0, B) as b:
                ln.scalar(act, b)
                ln.scalar_xT(act, b)
                if mode == "sequence":
                    act.wait_ge(max_ready, b + 1)
                    nc.scalar.activation(expd[:, 0, 0:E], top[:, 0, 0:E], ACT.Exp, bias=total[:, 1:2],
                                         accum_out=total[:, 0:1]).then_inc(expd_ready, 1)
                elif mode == "top2":
                    for t in range(TPS):
                        act.wait_ge(max_ready, TPS * b + t + 1)
                        nc.scalar.activation(expd[:, t, 1:2], expd[:, t, 2:3], ACT.Exp).then_inc(expd_ready, 1)
                for t in range(TPS):
                    n = TPS + t
                    turned.wait_full(act, b, n)
                    nc.scalar.copy(zwT[0:ER, t, :], turned.banks[n % 2][0:ER, 0:P])\
                        .then_inc(turned.emptied[n % 2], 1)

        @block.tensor
        def _(pe):
            pe.wait_ge(weights_loaded, 16 * n_loads)
            for ring in (turned, routed, summed):
                ring.open(pe)
            with pe.Fori(0, B) as b:
                ln.tensor(pe, b)
                for t in range(TPS):
                    ln.wait_xT(pe, b, t)
                    routed.wait_free(pe, b, t)
                    for c in range(C):
                        last = nc.tensor.matmul(routed.banks[t][:, 0:RC], ln.xT[:, c, t * P:(t + 1) * P],
                                                w_ra[:, c, :], start=(c == 0), stop=(c == C - 1))
                    last.then_inc(routed.filled[t], 1)
                for t in range(TPS):
                    summed.wait_free(pe, b, t)
                    for c in range(C):
                        nc.tensor.matmul(summed.banks[t][:, :], ln.xT[:, c, t * P:(t + 1) * P], w[:, c, :],
                                         start=(c == 0), stop=False)
                if mode == "sequence":
                    pe.wait_ge(logits_ready, TPS * (b + 1))
                    for k in range(2):
                        n = TPS + k
                        routed.wait_free(pe, b, n)
                        for t in range(TPS):
                            last = nc.tensor.matmul(routed.banks[n % 2][:, 0:E], mean_rows[:, t, :],
                                                    logits[:, t, 0:E], start=(t == 0), stop=(t == TPS - 1))
                        last.then_inc(routed.filled[n % 2], 1)
                for t in range(TPS):
                    n = TPS + t
                    pe.wait_ge(zw_ready, TPS * b + t + 1)
                    turned.wait_free(pe, b, n)
                    nc.tensor.transpose(turned.banks[n % 2][0:ER, 0:P], zw[:, t, :], ident[:, :])\
                        .then_inc(turned.filled[n % 2], 1)
                for t in range(TPS):
                    n = TPS + t
                    turned.wait_empty(pe, b, n)
                    nc.tensor.matmul(summed.banks[t][:, :], zwT[0:ER, t, :], w_b[:, :], start=False, stop=True)\
                        .then_inc(summed.filled[t], 1)


def gated_ffn(core, name):
    nc, dram, X = core.nc, core.dram, core.X
    H, RANK = 1376, 16
    HT = -(-H // P)
    ROWS = [min(P, H - P * j) for j in range(HT)]
    LOW = 2 * RANK
    S_USES = 1 + HT

    with ExitStack() as ctx:
        L = Layer(core, ctx, name)
        turned = Ring(L, "turned", TPS)
        summed = Ring(L, "summed", S_USES)
        results = Ring(L, "results", TPS)
        low_bank = L.bank("low_bank")
        ln = LayerNorm(L, turned)
        w_gate = L.sb("w_gate", [P, C, H])
        w_up = L.sb("w_up", [P, C, H])
        w_down = L.sb("w_down", [P, HT, D])
        a_in = L.sb("a_in", [P, C, LOW])
        b_in = L.sb("b_in", [LOW, 2, H])
        a_down = L.sb("a_down", [P, HT, RANK])
        b_down = L.sb("b_down", [RANK, D])
        low_in = L.sb("low_in", [LOW, S])
        low_down = L.sb("low_down", [RANK, S])
        silu = L.sb("silu", [P, 2, S])
        hidden = L.sb("hidden", [P, HT, S])

        zeroed = L.sem("zeroed")
        in_loaded = L.sem("in_loaded")
        down_loaded = L.sem("down_loaded")
        silu_ready = L.sem("silu_ready")
        hidden_ready = L.sem("hidden_ready")
        low_filled = L.sem("low_filled")
        low_emptied = L.sem("low_emptied")
        block = ctx.enter_context(nc.Block())

        @block.sync
        def _(sp):
            sp.wait_ge(zeroed, 1)
            for a, at in (("gate_a", 0), ("up_a", RANK)):
                sp.dma_start(a_in[:, :, at:at + RANK], dram[f"{name}_{a}"].rearrange("(c p) n -> p c n", p=P),
                             allow_slow_non_contiguous=True).then_inc(in_loaded, 16)
            for k, b in enumerate(("gate_b", "up_b")):
                sp.dma_start(b_in[k * RANK:(k + 1) * RANK, k, :], dram[f"{name}_{b}"]).then_inc(in_loaded, 16)
            for w, k in ((w_gate, "gate_w"), (w_up, "up_w")):
                sp.dma_start(w[:, :, :], dram[f"{name}_{k}"].rearrange("(c p) n -> p c n", p=P)).then_inc(in_loaded, 16)
            full = P * (HT - 1)
            for w, k in ((w_down, "down_w"), (a_down, "down_a")):
                src = dram[f"{name}_{k}"]
                sp.dma_start(w[:, 0:HT - 1, :], src[0:full, :].rearrange("(j p) n -> p j n", p=P),
                             allow_slow_non_contiguous=True).then_inc(down_loaded, 16)
                sp.dma_start(w[0:H - full, HT - 1, :], src[full:H, :]).then_inc(down_loaded, 16)
            sp.dma_start(b_down[:, :], dram[f"{name}_down_b"]).then_inc(down_loaded, 16)

        @block.gpsimd
        def _(pool):
            nc.gpsimd.memset(b_in[:, :, :], 0.0).then_inc(zeroed, 1)

        @block.vector
        def _(dve):
            with dve.Fori(0, B) as b:
                ln.vector(dve, b)
                for j in range(HT):
                    use, rows = 1 + j, slice(0, ROWS[j])
                    dve.wait_ge(silu_ready, HT * b + j + 1)
                    nc.vector.tensor_tensor(hidden[rows, j, :], silu[rows, j % 2, :],
                                            summed.banks[use % 2][rows, S:2 * S], ALU.mult)\
                        .then_inc(summed.emptied[use % 2], 1)
                for t in range(TPS):
                    results.wait_full(dve, b, t)
                    nc.vector.tensor_tensor(X[:, TPS * b + t, :], X[:, TPS * b + t, :], results.banks[t][:, :],
                                            ALU.add).then_inc(results.emptied[t], 1)

        @block.scalar
        def _(act):
            with act.Fori(0, B) as b:
                ln.scalar(act, b)
                ln.scalar_xT(act, b)
                summed.wait_full(act, b, 0)
                nc.scalar.copy(low_in[:, :], summed.banks[0][0:LOW, 0:S]).then_inc(summed.emptied[0], 1)
                for j in range(HT):
                    use, rows = 1 + j, slice(0, ROWS[j])
                    summed.wait_full(act, b, use)
                    if j >= 2:
                        summed.wait_empty(act, b, use - 2)
                    nc.scalar.activation(silu[rows, j % 2, :], summed.banks[use % 2][rows, 0:S], ACT.Silu)\
                        .then_inc(silu_ready, 1)
                act.wait_ge(low_filled, b + 1)
                nc.scalar.copy(low_down[:, :], low_bank[0:RANK, 0:S]).then_inc(low_emptied, 1)

        @block.tensor
        def _(pe):
            for ring in (turned, summed, results):
                ring.open(pe)
            pe.wait_ge(in_loaded, 16 * 6)
            with pe.Fori(0, B) as b:
                ln.tensor(pe, b)
                for t in range(TPS):
                    ln.wait_xT(pe, b, t)
                summed.wait_free(pe, b, 0)
                for c in range(C):
                    last = nc.tensor.matmul(summed.banks[0][0:LOW, 0:S], a_in[:, c, :], ln.xT[:, c, :],
                                            start=(c == 0), stop=(c == C - 1))
                last.then_inc(summed.filled[0], 1)
                for j in range(HT):
                    use, rows = 1 + j, slice(0, ROWS[j])
                    cols = slice(P * j, P * j + ROWS[j])
                    bank = summed.banks[use % 2]
                    summed.wait_free(pe, b, use)
                    for k, (w, half) in enumerate(((w_gate, 0), (w_up, S))):
                        for c in range(C):
                            nc.tensor.matmul(bank[rows, half:half + S], w[:, c, cols], ln.xT[:, c, :],
                                             start=(c == 0), stop=False)
                        if j == 0 and half == 0:
                            summed.wait_empty(pe, b, 0)
                        last = nc.tensor.matmul(bank[rows, half:half + S], b_in[:, k, cols],
                                                low_in[:, :], start=False, stop=True)
                    last.then_inc(summed.filled[use % 2], 1)
                pe.wait_ge(down_loaded, 16 * 5)
                for j in range(HT):
                    if j in (HT - 2, HT - 1):
                        summed.wait_empty(pe, b, 1 + j)
                    elif j == 0:
                        summed.wait_empty(pe, b, 1 + HT - 3)
                        summed.wait_empty(pe, b, 1 + HT - 4)
                    last = nc.tensor.matmul(low_bank[0:RANK, 0:S], a_down[0:ROWS[j], j, :], hidden[0:ROWS[j], j, :],
                                            start=(j == 0), stop=(j == HT - 1))
                last.then_inc(low_filled, 1)
                for t in range(TPS):
                    results.wait_free(pe, b, t)
                    for j in range(HT):
                        nc.tensor.matmul(results.banks[t][:, :], hidden[0:ROWS[j], j, t * P:(t + 1) * P],
                                         w_down[0:ROWS[j], j, :], start=(j == 0), stop=False)
                    if t == 0:
                        pe.wait_ge(low_emptied, b + 1)
                    nc.tensor.matmul(results.banks[t][:, :], low_down[:, t * P:(t + 1) * P], b_down[:, :],
                                     start=False, stop=True).then_inc(results.filled[t], 1)


def build(nc, dram):
    with ExitStack() as ctx:
        core = Core(nc, ctx, dram)
        load_constants(core)
        narrow_attention(core, "L0_attn", rope=True)
        routed_ffn(core, "L0_ffn", 8, 16, "sequence")
        wide_attention(core, "L1_attn", linear=True)
        gated_ffn(core, "L1_ffn")
        narrow_attention(core, "L2_attn", rope=False)
        routed_ffn(core, "L2_ffn", 4, 8, "top1")
        wide_attention(core, "L3_attn", linear=False)
        routed_ffn(core, "L3_ffn", 8, 16, "top2")
        store_result(core)


def narrow_tables():
    HD = 16
    inv = (1.0 / 10000.0 ** (np.arange(0, HD, 2, dtype=np.float32) / HD)).astype(np.float32)
    ang = np.arange(S, dtype=np.float32)[:, None] * inv[None, :]
    cos, sin = np.cos(ang).astype(np.float32), np.sin(ang).astype(np.float32)
    c2 = np.repeat(cos, 2, axis=1)
    s2 = np.stack([-sin, sin], axis=-1).reshape(S, HD)
    scale = -np.float32(HD) ** -0.5
    out = []
    for t in (c2, s2):
        full = np.concatenate([np.tile(t * scale, (1, HEADS)), np.tile(t, (1, KV_HEADS))], axis=1)
        out.append(np.ascontiguousarray(full.reshape(TPS, P, -1).transpose(1, 0, 2)).astype(np.float32))
    return out


def wide_tables():
    HD = 128
    inv = (1.0 / 10000.0 ** (np.arange(0, HD, 2, dtype=np.float32) / HD)).astype(np.float32)
    ang = np.arange(S, dtype=np.float32)[:, None] * inv[None, :]
    cos, sin = np.cos(ang).astype(np.float32), np.sin(ang).astype(np.float32)
    return [np.ascontiguousarray(t.reshape(TPS, P, HD).transpose(1, 0, 2))
            for t in (np.concatenate([cos, cos], axis=1), np.concatenate([-sin, sin], axis=1))]


def shape_constants():
    k = {"ident": np.eye(P, dtype=np.float32), "eps": np.full((P, 1), EPS, np.float32),
         "one": np.ones((P, 1), np.float32)}
    q, c = np.arange(P)[:, None], np.arange(P)[None, :]
    tri = np.where(c <= q, 0.0, BIG).astype(np.float32)
    k["mask"] = np.concatenate([tri, np.zeros((P, P), np.float32), tri], axis=1)
    k["wide_cos"], k["wide_sin"] = wide_tables()
    qt, kt = np.arange(S)[:, None], np.arange(S)[None, :]
    window = np.where((kt <= qt) & (qt - kt <= WINDOW), 0.0, BIG).astype(np.float32)
    k["window_mask"] = np.concatenate([window[:P, :P], window[P:, :]], axis=1)
    key, blk, query = np.arange(P)[:, None, None, None], np.arange(4)[:, None, None], np.arange(32)
    half = np.broadcast_to(np.where(key <= 32 * blk + query, 0.5, 0.0), (P, 4, GROUP, 32))
    k["half_mask"] = half.reshape(P, 4, GROUP * 32).astype(np.float32)
    tok = np.arange(S)
    rows = ((tok >= MEAN_FROM) & (tok < MEAN_TO)).astype(np.float32) / np.float32(MEAN_TO - MEAN_FROM)
    k["mean_rows"] = np.repeat(rows.reshape(TPS, P).T[:, :, None], P, axis=2).astype(np.float32)
    k["L0_attn_cos"], k["L0_attn_sin"] = narrow_tables()
    k["L0_attn_q_pad"] = np.zeros((P, TPS, HEADS, 32), np.float32)
    k["L0_attn_k_pad"] = np.zeros((P, TPS, KV_HEADS, 4, 32), np.float32)
    start = 2.0 ** (-2.0 ** (-(np.log2(HEADS) - 3)))
    slopes = np.array([start ** (i + 1) for i in range(HEADS)], dtype=np.float32)
    pos = np.arange(S, dtype=np.float32).reshape(TPS, P).T
    qp = np.zeros((P, TPS, HEADS, 32), np.float32)
    qp[:, :, :, 16] = -slopes
    qp[:, :, :, 17] = slopes * pos[:, :, None]
    kp = np.zeros((P, TPS, 1, 4, 32), np.float32)
    kp[:, :, :, :, 16] = pos[:, :, None, None]
    kp[:, :, :, :, 17] = 1.0
    k["L2_attn_q_pad"], k["L2_attn_k_pad"] = qp, kp
    return k


def by_group(*ws):
    return np.concatenate([w.reshape(D, KV_HEADS, -1).transpose(1, 0, 2) for w in ws], axis=2)


def layouts(i):
    a = {k: np.asarray(v) for k, v in i.items()}
    return {
        "x": a["L0_attn_x"],
        "L0_attn_w_qkv": a["L0_attn_w_qkv"].T, "L0_attn_b_qkv": a["L0_attn_b_qkv"],
        "L0_attn_w_o": a["L0_attn_w_o"].T, "L0_attn_b_o": a["L0_attn_b_o"],
        "L0_ffn_w": a["L0_ffn_W"].T, "L0_ffn_b": a["L0_ffn_b"], "L0_ffn_router": a["L0_ffn_router_W"].T,
        "L0_ffn_router_b": a["L0_ffn_router_b"], "L0_ffn_A": a["L0_ffn_A"].reshape(-1, D).T,
        "L0_ffn_B": a["L0_ffn_B"].transpose(0, 2, 1).reshape(-1, D),
        "L2_attn_w_qkv": np.concatenate([a["L2_attn_Wq"], a["L2_attn_Wkv"]], axis=1),
        "L2_attn_w_o": a["L2_attn_Wo"],
        "L2_ffn_w": a["L2_ffn_W_up"].T, "L2_ffn_router": a["L2_ffn_gate_w"].T,
        "L2_ffn_router_b": a["L2_ffn_expert_bias"], "L2_ffn_A": a["L2_ffn_lora_A"].reshape(-1, D).T,
        "L2_ffn_B": a["L2_ffn_lora_B"].transpose(0, 2, 1).reshape(-1, D),
        "L1_attn_w_in": by_group(a["L1_attn_Wq"], a["L1_attn_Wk"], a["L1_attn_Wv"]),
        "L1_attn_w_o": a["L1_attn_Wo"].reshape(KV_HEADS, -1, D),
        **{f"L1_ffn_{k}": a[f"L1_ffn_{k}"].T for k in ("gate_w", "up_w", "down_w", "gate_a", "gate_b", "up_a",
                                                       "up_b", "down_a", "down_b")},
        "L3_attn_w_in": by_group(a["L3_attn_Wq"], a["L3_attn_Wk"], a["L3_attn_Wv"]),
        "L3_attn_w_o": a["L3_attn_Wo"].reshape(KV_HEADS, -1, D),
        "L3_ffn_w": a["L3_ffn_W_base"].T, "L3_ffn_b": a["L3_ffn_b_base"],
        "L3_ffn_router": a["L3_ffn_W_router"].T, "L3_ffn_A": a["L3_ffn_A"].reshape(-1, D).T,
        "L3_ffn_B": a["L3_ffn_B"].transpose(0, 2, 1).reshape(-1, D),
    }


def kernel(**inputs):
    import concourse.bacc as bacc
    from concourse.bass_utils import run_bass_kernel_spmd

    nc = bacc.Bacc("TRN2", target_bir_lowering=False, num_devices=1)
    arrays, dram = {}, {}
    for name, a in {**layouts(inputs), **shape_constants()}.items():
        arrays[f"in_{name}"] = np.ascontiguousarray(a)
        dram[name] = nc.dram_tensor(f"in_{name}", a.shape, mybir.dt.from_np(a.dtype), kind="ExternalInput").ap()
    dram["out"] = nc.dram_tensor("out_x", (B, S, D), F32, kind="ExternalOutput").ap()
    build(nc, dram)
    r = run_bass_kernel_spmd(nc, [arrays], core_ids=[0])
    return r.results[0]["out_x"]
```

```python
from contextlib import ExitStack

import concourse.bass as bass
import concourse.mybir as mybir
import numpy as np

F32 = mybir.dt.float32
F32R = mybir.dt.float32r
BF16 = mybir.dt.bfloat16
U32 = mybir.dt.uint32
ALU = mybir.AluOpType
ACT = mybir.ActivationFunctionType
AX = mybir.AxisListType

P = 128
D = 512
C = D // P
B, S = 4, 256
TPS = S // P
NT = B * TPS
EPS = 1e-5
BIG = 1e30
HEADS, KV_HEADS = 32, 8
WINDOW = 64
MEAN_FROM, MEAN_TO = 34 + 72 + 1, S - 1
GROUP = HEADS // KV_HEADS
SCORE_COLS = P + S
SPAN = [slice(0, P), slice(P, P + S)]


class Core:

    def __init__(self, nc, ctx, dram):
        self.nc, self.dram = nc, dram
        self.X = ctx.enter_context(nc.sbuf_tensor("X", [P, NT, D], F32))
        self.ident = ctx.enter_context(nc.sbuf_tensor("ident", [P, P], F32))
        self.one = ctx.enter_context(nc.sbuf_tensor("one", [P, 1], F32))
        self.eps = ctx.enter_context(nc.sbuf_tensor("eps", [P, 1], F32))
        self.mask = ctx.enter_context(nc.sbuf_tensor("mask", [P, SCORE_COLS], F32))
        self.carrier = ctx.enter_context(nc.semaphore("carrier"))
        self.loaded = ctx.enter_context(nc.semaphore("constants_loaded"))

    def carry_wait(self, eng):
        eng.sem_inc(self.carrier, 1)


class Layer:

    def __init__(self, core, ctx, name):
        self.core, self.ctx, self.name, self.nc = core, ctx, name, core.nc
        self.sems = []
        ctx.callback(self.close)

    def close(self):
        self.nc.clear_and_free_semaphores(self.sems)
        self.nc.all_engine_barrier()

    def sb(self, name, shape, dtype=F32):
        return self.ctx.enter_context(self.nc.sbuf_tensor(f"{self.name}_{name}", shape, dtype))

    def bank(self, name, shape=(P, 512), dtype=F32):
        return self.ctx.enter_context(self.nc.psum_tensor(f"{self.name}_{name}", list(shape), dtype))

    def sem(self, name):
        self.sems.append(self.nc.alloc_semaphore(f"{self.name}_{name}"))
        return self.sems[-1]


def split_matmul(nc, out, left, right, start, stop):
    pairs = [(left[0], right[0]), (left[0], right[1])]
    if len(left) == 2:
        pairs.append((left[1], right[0]))
    for n, (a, b) in enumerate(pairs):
        last = nc.tensor.matmul(out, a, b, start=start and n == 0, stop=stop and n == len(pairs) - 1)
    return last


class Ring:

    def __init__(self, layer, name, per):
        assert per % 2 == 0
        self.banks = [layer.bank(f"{name}{k}") for k in range(2)]
        self.filled = [layer.sem(f"{name}{k}_filled") for k in range(2)]
        self.emptied = [layer.sem(f"{name}{k}_emptied") for k in range(2)]
        self.per = per // 2

    def wait_free(self, pe, i, n):
        pe.wait_ge(self.emptied[n % 2], 1 + i * self.per + n // 2)

    def wait_empty(self, eng, i, n):
        eng.wait_ge(self.emptied[n % 2], 1 + i * self.per + n // 2 + 1)

    def open(self, pe):
        for k in self.emptied:
            pe.sem_inc(k, 1)

    def wait_full(self, eng, i, n):
        eng.wait_ge(self.filled[n % 2], i * self.per + n // 2 + 1)


class LayerNorm:

    def __init__(self, layer, ring):
        self.core, self.nc, self.ring = layer.core, layer.nc, ring
        self.xn = layer.sb("xn", [P, TPS, D])
        self.xT = layer.sb("xT", [P, C, S])
        self.stats = layer.sb("stats", [P, NT, 6])
        self.moments = layer.sb("moments", [P, NT, 2])
        self.std = layer.sb("std", [P, NT])
        self.rstd = layer.sb("rstd", [P, NT, 1])
        self.stats_ready = layer.sem("stats_ready")
        self.moments_ready = layer.sem("moments_ready")
        self.std_ready = layer.sem("std_ready")
        self.rstd_ready = layer.sem("rstd_ready")
        self.xn_ready = layer.sem("xn_ready")
        self.xT_ready = layer.sem("xT_ready")

    def vector_all(self, dve):
        nc, X = self.nc, self.core.X
        for j in range(NT):
            nc.vector.bn_stats(self.stats[:, j, :], X[:, j, :]).then_inc(self.stats_ready, 1)
        for j in range(NT):
            dve.wait_ge(self.stats_ready, j + 1)
            nc.vector.bn_aggr(self.moments[:, j, :], self.stats[:, j, :]).then_inc(self.moments_ready, 1)
        dve.wait_ge(self.std_ready, 1)
        nc.vector.reciprocal(self.rstd[:, :, 0], self.std[:, :]).then_inc(self.rstd_ready, 1)
        dve.wait_ge(self.rstd_ready, 1)

    def normalise(self, dve, b, alone=False):
        for t in range(TPS):
            if alone:
                self.ring.wait_empty(dve, b - 1, t)
            j = TPS * b + t
            self.nc.vector.tensor_scalar(self.xn[:, t, :], self.core.X[:, j, :], self.moments[:, j, 0:1],
                                         self.rstd[:, j, :], ALU.subtract, ALU.mult).then_inc(self.xn_ready, 1)

    def scalar_all(self, act):
        act.wait_ge(self.moments_ready, NT)
        self.nc.scalar.activation(self.std[:, :], self.moments[:, :, 1], ACT.Sqrt, bias=self.core.eps[:, 0:1])\
            .then_inc(self.std_ready, 1)

    def scalar_xT(self, act, i, xT=None, n0=0):
        nc, xT = self.nc, self.xT if xT is None else xT
        for t in range(TPS):
            self.ring.wait_full(act, i, n0 + t)
            nc.scalar.copy(xT[:, :, t * P:(t + 1) * P],
                           self.ring.banks[t].rearrange("p (c n) -> p c n", c=C))\
                .then_inc(self.ring.emptied[t], 1)

    def tensor(self, pe, b, i=None, n0=0):
        nc, i = self.nc, b if i is None else i
        for t in range(TPS):
            pe.wait_ge(self.xn_ready, TPS * b + t + 1)
            self.ring.wait_free(pe, i, n0 + t)
            for c in range(C):
                last = nc.tensor.transpose(self.ring.banks[t][:, c * P:(c + 1) * P],
                                           self.xn[:, t, c * P:(c + 1) * P], self.core.ident[:, :])
            last.then_inc(self.ring.filled[t], 1)

    def wait_xT(self, eng, i, t, n0=0):
        self.ring.wait_empty(eng, i, n0 + t)


class NarrowWeights:

    def __init__(self, core, ctx, name, rope):
        self.core, self.name, self.rope = core, name, rope
        kv_heads = KV_HEADS if rope else 1
        columns = (HEADS + 2 * kv_heads) * 16
        L = Layer(core, ctx, f"{name}_weights")
        self.w_qkv = L.sb("w_qkv", [P, C, columns])
        self.w_o = L.sb("w_o", [P, C, D])
        self.q_pad = L.sb("q_pad", [P, TPS, HEADS, 32])
        self.k_pad = L.sb("k_pad", [P, TPS, kv_heads, 4, 32])
        if rope:
            self.b_qkv = L.sb("b_qkv", [P, columns])
            self.b_o = L.sb("b_o", [P, D])
            self.cos = L.sb("cos", [P, TPS, 16])
            self.sin = L.sb("sin", [P, TPS, 16])
        self.loaded = L.sem("loaded")
        self.padded = L.sem("padded")

    def load(self, sp):
        dram, name, loaded = self.core.dram, self.name, self.loaded
        sp.dma_start(self.w_qkv[:, :, :], dram[f"{name}_w_qkv"].rearrange("(c p) n -> p c n", p=P))\
            .then_inc(loaded, 16)
        if self.rope:
            sp.dma_start(self.b_qkv[:, :], dram[f"{name}_b_qkv"].partition_broadcast(P)).then_inc(loaded, 16)
            sp.dma_start(self.b_o[:, :], dram[f"{name}_b_o"].partition_broadcast(P)).then_inc(loaded, 16)
            sp.dma_start(self.cos[:, :, :], dram[f"{name}_cos"]).then_inc(loaded, 16)
            sp.dma_start(self.sin[:, :, :], dram[f"{name}_sin"]).then_inc(loaded, 16)
        else:
            sp.dma_start(self.q_pad[:, :, :, :], dram[f"{name}_q_pad"]).then_inc(self.padded, 16)
            sp.dma_start(self.k_pad[:, :, :, :, :], dram[f"{name}_k_pad"]).then_inc(self.padded, 16)
        sp.dma_start(self.w_o[:, :, :], dram[f"{name}_w_o"].rearrange("(c p) n -> p c n", p=P))\
            .then_inc(loaded, 16)


class RoutedWeights:

    def __init__(self, core, ctx, name, experts, rank, mode):
        self.core, self.name, self.mode = core, name, mode
        self.experts, self.rank = experts, rank
        self.bias = mode != "top1"
        self.logit_bias = mode != "top2"
        L = Layer(core, ctx, f"{name}_weights")
        self.w = L.sb("w", [P, C, D])
        self.w_ra = L.sb("w_ra", [P, C, experts * (1 + rank)])
        self.w_b = L.sb("w_b", [experts * rank, D])
        if self.bias:
            self.b_out = L.sb("b_out", [P, D])
        if self.logit_bias:
            self.b_logit = L.sb("b_logit", [P, experts])
        if mode == "sequence":
            self.mean_rows = L.sb("mean_rows", [P, TPS, P])
        self.loaded = L.sem("loaded")
        self.n_loads = 4 + self.bias + self.logit_bias + (mode == "sequence")

    def load(self, sp):
        dram, name, loaded, E = self.core.dram, self.name, self.loaded, self.experts
        sp.dma_start(self.w[:, :, :], dram[f"{name}_w"].rearrange("(c p) n -> p c n", p=P)).then_inc(loaded, 16)
        sp.dma_start(self.w_ra[:, :, 0:E], dram[f"{name}_router"].rearrange("(c p) n -> p c n", p=P),
                     allow_slow_non_contiguous=True).then_inc(loaded, 16)
        sp.dma_start(self.w_ra[:, :, E:], dram[f"{name}_A"].rearrange("(c p) n -> p c n", p=P)).then_inc(loaded, 16)
        sp.dma_start(self.w_b[:, :], dram[f"{name}_B"]).then_inc(loaded, 16)
        if self.bias:
            sp.dma_start(self.b_out[:, :], dram[f"{name}_b"].partition_broadcast(P)).then_inc(loaded, 16)
        if self.logit_bias:
            sp.dma_start(self.b_logit[:, :], dram[f"{name}_router_b"].partition_broadcast(P)).then_inc(loaded, 16)
        if self.mode == "sequence":
            sp.dma_start(self.mean_rows[:, :, :], dram["mean_rows"]).then_inc(loaded, 16)


def load_constants(core, following):
    nc, dram = core.nc, core.dram
    loaded = core.loaded
    with ExitStack() as ctx:
        block = ctx.enter_context(nc.Block())

        @block.sync
        def _(sp):
            sp.dma_start(core.eps[:, :], dram["eps"]).then_inc(loaded, 16)
            xv = dram["x"].rearrange("b (t p) d -> p (b t) d", p=P)
            sp.dma_start(core.X[:, :, :], xv).then_inc(loaded, 16)
            sp.dma_start(core.ident[:, :], dram["ident"]).then_inc(loaded, 16)
            sp.dma_start(core.mask[:, :], dram["mask"]).then_inc(loaded, 16)
            sp.dma_start(core.one[:, :], dram["one"]).then_inc(loaded, 16)
            following.load(sp)
            sp.wait_ge(loaded, 80)


def store_result(core):
    nc = core.nc
    with ExitStack() as ctx:
        stored = ctx.enter_context(nc.semaphore("stored"))
        block = ctx.enter_context(nc.Block())

        @block.sync
        def _(sp):
            ov = core.dram["out"].rearrange("b (t p) d -> p (b t) d", p=P)
            sp.dma_start(ov, core.X[:, :, :]).then_inc(stored, 16)
            sp.wait_ge(stored, 16)


def narrow_attention(core, weights, following):
    nc, X, ident = core.nc, core.X, core.ident
    name, rope = weights.name, weights.rope
    HD = 16
    SLOT = 32
    SLOTS = P // SLOT
    QG = HEADS // SLOTS
    KG = KV_HEADS if rope else 1
    KV = KG * HD
    QKV = HEADS * HD + 2 * KV
    PIECES = [(0, 512), (512, QKV - 512)]
    QU, KU = QG * P // 512, max(1, KG * P // 512)
    KB = KG // KU
    QK_USES = TPS * (QU + KU)
    LN_AT = 20
    LEAD = TPS + QK_USES
    LN1 = LEAD + LN_AT

    def head_use(h, more):
        return LEAD + h + (TPS if more and h >= LN_AT else 0)

    def out_use(t, more):
        return head_use(HEADS - 1, more) + 1 + t

    def qk_use(i, more):
        return out_use(0, more) + TPS + i

    T_USES = HEADS + TPS + TPS + QK_USES
    A_LEAD = TPS * 2
    A_USES = TPS * 2 + TPS

    def wo_use(t, more):
        return A_LEAD + (TPS * 2 if more else 0) + t

    with ExitStack() as ctx:
        L = Layer(core, ctx, name)
        turned = Ring(L, "turned", T_USES)
        summed = Ring(L, "summed", A_USES)
        ln = LayerNorm(L, turned)
        scores = [L.bank(f"scores{k}") for k in range(2)]
        heads_out = [L.bank(f"heads_out{t}") for t in range(TPS)]

        w_qkv, w_o, q_pad, k_pad = weights.w_qkv, weights.w_o, weights.q_pad, weights.k_pad
        v = L.sb("v", [P, TPS, KG, HD])
        qT = L.sb("qT", [P, QG, S])
        kT = L.sb("kT", [P, SLOTS, KG, S])
        masked = L.sb("masked", [P, 2, SCORE_COLS])
        neg_max = L.sb("neg_max", [P, TPS, HEADS])
        total = L.sb("total", [P, TPS, HEADS])
        r_total = L.sb("r_total", [P, TPS, HEADS])
        probs = L.sb("probs", [P, 2, SCORE_COLS])
        probsT = L.sb("probsT", [P, 2, SCORE_COLS])
        out = L.sb("out", [P, TPS, HEADS, HD])
        outT = L.sb("outT", [P, C, S])
        if rope:
            b_qkv, b_o, cos, sin = weights.b_qkv, weights.b_o, weights.cos, weights.sin
            qkv = L.sb("qkv", [P, TPS, QKV])
            straight = L.sb("straight", [P, TPS, (HEADS + KG) * HD])
            crossed = L.sb("crossed", [P, TPS, (HEADS + KG) * HD])

        weights_loaded, padded = weights.loaded, weights.padded
        zeroed = L.sem("zeroed")
        turned_parts_ready = L.sem("rope_parts_ready")
        q_pad_ready = L.sem("q_pad_ready")
        kv_ready = L.sem("kv_ready")
        scores_filled = L.sem("scores_filled")
        masked_ready = L.sem("masked_ready")
        probs_ready = L.sem("probs_ready")
        pv_done = L.sem("pv_done")
        r_total_ready = L.sem("r_total_ready")
        out_ready = L.sem("out_ready")
        bias_added = L.sem("bias_added")
        block = ctx.enter_context(nc.Block())

        @block.sync
        def _(sp):
            following.load(sp)

        loads = 16 * (6 if rope else 2)

        @block.vector
        def _(dve):
            def take_qkv(b, i, at0):
                for t in range(TPS):
                    if rope:
                        for j, (at, n) in enumerate(PIECES):
                            summed.wait_full(dve, i, at0 + 2 * t + j)
                            nc.vector.tensor_tensor(qkv[:, t, at:at + n], summed.banks[j][:, 0:n],
                                                    b_qkv[:, at:at + n], ALU.add)\
                                .then_inc(summed.emptied[j], 1)
                        NR = (HEADS + KG) * HD
                        summed.wait_empty(dve, i, at0 + 2 * t)
                        summed.wait_empty(dve, i, at0 + 2 * t + 1)
                        heads = HEADS + KG
                        nc.vector.tensor_tensor(straight[:, t, :].rearrange("p (h d) -> p h d", d=HD),
                                                qkv[:, t, 0:NR].rearrange("p (h d) -> p h d", d=HD),
                                                cos[:, t, :].unsqueeze(1).to_broadcast([P, heads, HD]), ALU.mult)\
                            .then_inc(turned_parts_ready, 1)
                        src = qkv[:, t, 0:NR].rearrange("p (h n two) -> p h n two", two=2, h=heads)
                        dst = crossed[:, t, :].rearrange("p (h n two) -> p h n two", two=2, h=heads)
                        sn = sin[:, t, :].rearrange("p (n two) -> p n two", two=2)
                        for e in range(2):
                            nc.vector.tensor_tensor(dst[:, :, :, e], src[:, :, :, 1 - e],
                                                    sn[:, :, e].unsqueeze(1).to_broadcast([P, heads, HD // 2]),
                                                    ALU.mult).then_inc(turned_parts_ready, 1)
                        dve.wait_ge(turned_parts_ready, 3 * (TPS * b + t + 1))
                        QN = HEADS * HD
                        nc.vector.tensor_tensor(
                            q_pad[:, t, :, 0:HD], straight[:, t, 0:QN].rearrange("p (h d) -> p h d", d=HD),
                            crossed[:, t, 0:QN].rearrange("p (h d) -> p h d", d=HD), ALU.add)\
                            .then_inc(q_pad_ready, 1)
                        for s in range(SLOTS):
                            nc.vector.tensor_tensor(
                                k_pad[:, t, :, s, 0:HD],
                                straight[:, t, QN:NR].rearrange("p (h d) -> p h d", d=HD),
                                crossed[:, t, QN:NR].rearrange("p (h d) -> p h d", d=HD), ALU.add)\
                                .then_inc(kv_ready, 1)
                        nc.vector.tensor_copy(v[:, t, :, :],
                                              qkv[:, t, NR:QKV].rearrange("p (h d) -> p h d", d=HD))\
                            .then_inc(kv_ready, 1)
                    else:
                        summed.wait_full(dve, i, at0 + 2 * t)
                        nc.vector.tensor_scalar(
                            q_pad[:, t, :, 0:HD], summed.banks[0].rearrange("p (h d) -> p h d", d=HD),
                            -float(HD) ** -0.5, None, ALU.mult).then_inc(summed.emptied[0], 1)
                        summed.wait_full(dve, i, at0 + 2 * t + 1)
                        for s in range(SLOTS):
                            nc.vector.tensor_copy(k_pad[:, t, 0, s, 0:HD], summed.banks[1][:, 0:HD])\
                                .then_inc(kv_ready, 1)
                        nc.vector.tensor_copy(v[:, t, 0, :], summed.banks[1][:, HD:2 * HD])\
                            .then_inc(summed.emptied[1], 1)

            def take_keys(i, n0, t):
                for u in range(1, KU):
                    n = n0 + t * (QU + KU) + QU + u
                    turned.wait_full(dve, i, n)
                    for s in range(SLOTS):
                        rows = slice(SLOT * s, SLOT * (s + 1))
                        last = nc.vector.tensor_copy(kT[rows, s, KB * u:KB * (u + 1), t * P:(t + 1) * P],
                                                     turned.banks[n % 2][rows, 0:KB * P]
                                                     .rearrange("p (g n) -> p g n", g=KB))
                    last.then_inc(turned.emptied[n % 2], 1)

            def mask_scores(b, h):
                k = h % 2
                dve.wait_ge(scores_filled, HEADS * b + h + 1)
                if h >= 2:
                    dve.wait_ge(probs_ready, TPS * (HEADS * b + h - 1))
                core.carry_wait(dve)
                for t in range(TPS):
                    nc.vector.tensor_tensor_reduce(masked[:, k, SPAN[t]], scores[k][:, SPAN[t]],
                                                   core.mask[:, SPAN[t]], 1.0, 3e38, ALU.add, ALU.min,
                                                   neg_max[:, t, h:h + 1]).then_inc(masked_ready, 1)

            def step(b, more):
                mask_scores(b, 0)
                for h in range(HEADS):
                    if h + 1 < HEADS:
                        mask_scores(b, h + 1)
                    if h == LN_AT - 2 and more:
                        ln.normalise(dve, b + 1)
                    if h % 2 == 0:
                        n = head_use(h, more)
                        turned.wait_full(dve, b, n)
                        if h >= 2:
                            dve.wait_ge(pv_done, HEADS * b + h - 1)
                        nc.vector.tensor_copy(probsT[:, h % 2, :], turned.banks[n % 2][:, 0:SCORE_COLS])\
                            .then_inc(turned.emptied[n % 2], 1)
                dve.wait_ge(probs_ready, TPS * HEADS * (b + 1))
                for t in range(TPS):
                    nc.vector.reciprocal(r_total[:, t, :], total[:, t, :]).then_inc(r_total_ready, 1)
                dve.wait_ge(pv_done, HEADS * (b + 1))
                for t in range(TPS):
                    dve.wait_ge(r_total_ready, TPS * b + t + 1)
                    nc.vector.tensor_tensor(out[:, t, :, :],
                                            heads_out[t].rearrange("p (h d) -> p h d", d=HD),
                                            r_total[:, t, :].unsqueeze(2).to_broadcast([P, HEADS, HD]),
                                            ALU.mult).then_inc(out_ready, 1)
                if more:
                    take_qkv(b + 1, b, A_LEAD)
                if rope:
                    dve.wait_ge(bias_added, TPS * (b + 1))
                for t in range(TPS):
                    n = wo_use(t, more)
                    summed.wait_full(dve, b, n)
                    nc.vector.tensor_tensor(X[:, TPS * b + t, :], X[:, TPS * b + t, :],
                                            summed.banks[n % 2][:, :], ALU.add)\
                        .then_inc(summed.emptied[n % 2], 1)
                    if more:
                        take_keys(b, qk_use(0, more), t)

            ln.vector_all(dve)
            ln.normalise(dve, 0)
            dve.wait_ge(zeroed, 1)
            dve.wait_ge(padded, 32)
            if rope:
                dve.wait_ge(weights_loaded, loads)
            take_qkv(0, 0, 0)
            for t in range(TPS):
                take_keys(0, TPS, t)
            with dve.Fori(0, B - 1) as b:
                step(b, True)
            step(B - 1, False)

        @block.gpsimd
        def _(pool):
            if rope:
                nc.gpsimd.memset(q_pad[:, :, :, :], 0.0).then_inc(padded, 16)
                nc.gpsimd.memset(k_pad[:, :, :, :, :], 0.0).then_inc(padded, 16)
            nc.gpsimd.memset(kT[:, :, :, :], 0.0).then_inc(zeroed, 1)
            if rope:
                pool.wait_ge(weights_loaded, loads)
                with pool.Fori(0, B) as b:
                    for t in range(TPS):
                        pool.wait_ge(ln.xn_ready, TPS * b + t + 1)
                        nc.gpsimd.tensor_tensor(X[:, TPS * b + t, :], X[:, TPS * b + t, :], b_o[:, :], ALU.add)\
                            .then_inc(bias_added, 1)

        @block.scalar
        def _(act):
            def take_turned(i, n0):
                for t in range(TPS):
                    for j in range(QU + KU):
                        n = n0 + t * (QU + KU) + j
                        turned.wait_full(act, i, n)
                        src = turned.banks[n % 2]
                        if j < QU:
                            nc.scalar.mul(qT[:, 4 * j:4 * j + 4, t * P:(t + 1) * P],
                                          src.rearrange("p (g n) -> p g n", g=4), -float(HD) ** -0.5 if rope else 1.0)\
                                .then_inc(turned.emptied[n % 2], 1)
                        elif j == QU:
                            u = j - QU
                            for s in range(SLOTS):
                                rows = slice(SLOT * s, SLOT * (s + 1))
                                last = nc.scalar.copy(kT[rows, s, KB * u:KB * (u + 1), t * P:(t + 1) * P],
                                                      src[rows, 0:KB * P].rearrange("p (g n) -> p g n", g=KB))
                            last.then_inc(turned.emptied[n % 2], 1)

            def exponentials(b, h, more):
                k = h % 2
                for t in range(TPS):
                    act.wait_ge(masked_ready, TPS * (HEADS * b + h) + t + 1)
                    if t == 0 and h >= 2:
                        turned.wait_full(act, b, head_use(h - 2, more))
                    nc.scalar.activation(probs[:, k, SPAN[t]], masked[:, k, SPAN[t]], ACT.Exp,
                                         bias=neg_max[:, t, h:h + 1], scale=-1.0,
                                         accum_out=total[:, t, h:h + 1]).then_inc(probs_ready, 1)

            def step(b, more):
                exponentials(b, 0, more)
                for h in range(HEADS):
                    if h == LN_AT and more:
                        ln.scalar_xT(act, b, n0=LN1)
                    if h + 1 < HEADS:
                        exponentials(b, h + 1, more)
                    if h % 2 == 1:
                        n = head_use(h, more)
                        turned.wait_full(act, b, n)
                        if h >= 2:
                            act.wait_ge(pv_done, HEADS * b + h - 1)
                        nc.scalar.copy(probsT[:, h % 2, :], turned.banks[n % 2][:, 0:SCORE_COLS])\
                            .then_inc(turned.emptied[n % 2], 1)
                for t in range(TPS):
                    n = out_use(t, more)
                    turned.wait_full(act, b, n)
                    nc.scalar.copy(outT[:, :, t * P:(t + 1) * P],
                                   turned.banks[n % 2].rearrange("p (c n) -> p c n", c=C))\
                        .then_inc(turned.emptied[n % 2], 1)
                if more:
                    take_turned(b, qk_use(0, more))

            act.wait_ge(zeroed, 1)
            ln.scalar_all(act)
            ln.scalar_xT(act, 0)
            take_turned(0, TPS)
            with act.Fori(0, B - 1) as b:
                step(b, True)
            step(B - 1, False)

        @block.tensor
        def _(pe):
            turned.open(pe)
            summed.open(pe)
            def project_qkv(i, at0, ln_use):
                for t in range(TPS):
                    ln.wait_xT(pe, i, t, ln_use)
                    for j, (at, n) in enumerate(PIECES):
                        use = at0 + 2 * t + j
                        summed.wait_free(pe, i, use)
                        for c in range(C):
                            last = nc.tensor.matmul(summed.banks[use % 2][:, 0:n],
                                                    ln.xT[:, c, t * P:(t + 1) * P], w_qkv[:, c, at:at + n],
                                                    start=(c == 0), stop=(c == C - 1))
                        last.then_inc(summed.filled[use % 2], 1)

            def turn_qk(b, i, n0, at0, tiles):
                for t in tiles:
                    for j in range(QU + KU):
                        n = n0 + t * (QU + KU) + j
                        if j == 0:
                            if rope:
                                pe.wait_ge(q_pad_ready, TPS * b + t + 1)
                            else:
                                summed.wait_empty(pe, i, at0 + 2 * t)
                        if j == QU:
                            if rope:
                                pe.wait_ge(kv_ready, (SLOTS + 1) * (TPS * b + t + 1))
                            else:
                                pe.wait_ge(kv_ready, SLOTS * (TPS * b + t + 1))
                        turned.wait_free(pe, i, n)
                        for g in range(4 if j < QU else KB):
                            if j < QU:
                                src = q_pad[:, t, SLOTS * (4 * j + g):SLOTS * (4 * j + g + 1), :]
                            else:
                                src = k_pad[:, t, KB * (j - QU) + g, :, :]
                            last = nc.tensor.transpose(turned.banks[n % 2][:, g * P:(g + 1) * P],
                                                       src.rearrange("p s d -> p (s d)"), ident[:, :])
                        last.then_inc(turned.filled[n % 2], 1)

            def wait_qkv(i, n0, at0):
                for k in range(2):
                    turned.wait_empty(pe, i, n0 + QK_USES - 1 - k)
                if not rope:
                    summed.wait_empty(pe, i, at0 + 2 * TPS - 1)

            def score(b, h):
                g, s = divmod(h, SLOTS)
                kg = g if rope else 0
                if h >= 2:
                    pe.wait_ge(masked_ready, TPS * (HEADS * b + h - 1))
                for t in range(TPS):
                    last = nc.tensor.matmul(scores[h % 2][:, SPAN[t]], qT[:, g, t * P:(t + 1) * P],
                                            kT[:, s, kg, 0:(t + 1) * P], start=True, stop=True)
                last.then_inc(scores_filled, 1)

            def turn_probs(b, h, more):
                n = head_use(h, more)
                pe.wait_ge(probs_ready, TPS * (HEADS * b + h + 1))
                turned.wait_free(pe, b, n)
                for j in range(SCORE_COLS // P):
                    last = nc.tensor.transpose(turned.banks[n % 2][:, j * P:(j + 1) * P],
                                               probs[:, h % 2, j * P:(j + 1) * P], ident[:, :])
                last.then_inc(turned.filled[n % 2], 1)

            def weigh_values(b, h, more):
                kg = h // GROUP if rope else 0
                turned.wait_empty(pe, b, head_use(h, more))
                pT = probsT[:, h % 2, :]
                cols = slice(HD * h, HD * (h + 1))
                nc.tensor.matmul(heads_out[0][:, cols], pT[:, 0:P], v[:, 0, kg, :], start=True, stop=True)
                nc.tensor.matmul(heads_out[1][:, cols], pT[:, P:2 * P], v[:, 0, kg, :], start=True, stop=False)
                nc.tensor.matmul(heads_out[1][:, cols], pT[:, 2 * P:3 * P], v[:, 1, kg, :],
                                 start=False, stop=True).then_inc(pv_done, 1)

            def step(b, more):
                score(b, 0)
                score(b, 1)
                for h in range(HEADS):
                    if h == LN_AT and more:
                        ln.tensor(pe, b + 1, b, LN1)
                    turn_probs(b, h, more)
                    if h + 2 < HEADS:
                        score(b, h + 2)
                    if h >= 1:
                        weigh_values(b, h - 1, more)
                weigh_values(b, HEADS - 1, more)
                if more:
                    project_qkv(b, A_LEAD, LN1)
                for t in range(TPS):
                    n = out_use(t, more)
                    pe.wait_ge(out_ready, TPS * b + t + 1)
                    turned.wait_free(pe, b, n)
                    for c in range(C):
                        last = nc.tensor.transpose(
                            turned.banks[n % 2][:, c * P:(c + 1) * P],
                            out[:, t, :, :].rearrange("p h d -> p (h d)")[:, c * P:(c + 1) * P], ident[:, :])
                    last.then_inc(turned.filled[n % 2], 1)
                for t in range(TPS):
                    use = wo_use(t, more)
                    turned.wait_empty(pe, b, out_use(t, more))
                    summed.wait_free(pe, b, use)
                    for c in range(C):
                        last = nc.tensor.matmul(summed.banks[use % 2][:, :], outT[:, c, t * P:(t + 1) * P],
                                                w_o[:, c, :], start=(c == 0), stop=(c == C - 1))
                    last.then_inc(summed.filled[use % 2], 1)
                    if more:
                        turn_qk(b + 1, b, qk_use(0, more), A_LEAD, [t])
                if more:
                    wait_qkv(b, qk_use(0, more), A_LEAD)

            ln.tensor(pe, 0)
            pe.wait_ge(weights_loaded, loads)
            project_qkv(0, 0, 0)
            turn_qk(0, 0, TPS, 0, range(TPS))
            wait_qkv(0, TPS, 0)
            with pe.Fori(0, B - 1) as b:
                step(b, True)
            step(B - 1, False)


class Bank:

    def __init__(self, layer, name, lead, first, body, last, rounds):
        self.tile = layer.bank(name)
        self.filled = layer.sem(f"{name}_filled")
        self.emptied = layer.sem(f"{name}_emptied")
        self.order = {"lead": lead, "first": first, "body": body, "last": last}
        head = len(lead) + len(first)
        self.start = {"lead": lambda r: 0, "first": lambda r: len(lead),
                      "body": lambda r: head + len(body) * (r - 1),
                      "last": lambda r: head + len(body) * (rounds - 1)}

    def before(self, step, use):
        phase, r = step
        return self.start[phase](r) + self.order[phase].index(use)

    def wait_free(self, pe, step, use):
        pe.wait_ge(self.emptied, 1 + self.before(step, use))

    def open(self, pe):
        pe.sem_inc(self.emptied, 1)

    def wait_full(self, eng, step, use):
        eng.wait_ge(self.filled, self.before(step, use) + 1)

    def wait_empty(self, eng, step, use):
        eng.wait_ge(self.emptied, 1 + self.before(step, use) + 1)


def normalise_all(core, name, xT_all, first_loads):
    with ExitStack() as ctx:
        L = Layer(core, ctx, f"{name}_norm")
        turned = Ring(L, "turned", TPS)
        ln = LayerNorm(L, turned)
        block = ctx.enter_context(core.nc.Block())

        @block.sync
        def _(sp):
            first_loads(sp)

        @block.vector
        def _(dve):
            ln.vector_all(dve)
            with dve.Fori(0, B) as b:
                ln.normalise(dve, b, alone=True)

        @block.scalar
        def _(act):
            ln.scalar_all(act)
            with act.Fori(0, B) as b:
                ln.scalar_xT(act, b, xT_all[:, b, :, :])

        @block.tensor
        def _(pe):
            turned.open(pe)
            with pe.Fori(0, B) as b:
                ln.tensor(pe, b)


def wide_attention(core, name, linear, following=None):
    nc, dram, X, ident = core.nc, core.dram, core.X, core.ident
    HD = 128
    UNITS = KV_HEADS * B
    QN = GROUP * HD
    RN = QN + HD
    QKV = RN + HD
    BLK = 32
    NB = S // BLK
    BPT = P // BLK
    ROUNDS = UNITS - 1
    CHUNKS = KV_HEADS * C
    IN_AHEAD, OUT_AHEAD = 5, 3

    with ExitStack() as ctx:
        xT_all = ctx.enter_context(nc.sbuf_tensor(f"{name}_xT_all", [P, B, C, S], F32))
        L = Layer(core, ctx, name)
        lin = linear
        raw_in = L.sb("raw_in", [P, 2, QKV])
        raw_out = L.sb("raw_out", [P, 2, D])
        cos = L.sb("cos", [P, TPS, HD])
        sin = L.sb("sin", [P, TPS, HD])
        if lin:
            mask = L.sb("mask", [P, SCORE_COLS])
            half_mask = L.sb("half_mask", [P, BPT, GROUP * BLK])
        else:
            mask = core.mask
        in_loaded = L.sem("in_loaded")
        out_loaded = L.sem("out_loaded")
        in_split = L.sem("in_split")
        out_split = L.sem("out_split")
        tables_loaded = L.sem("tables_loaded")
        ins = dram[f"{name}_w_in"].rearrange("g (c p) n -> (g c) p n", p=P)
        outs = dram[f"{name}_w_o"].rearrange("g (h p) n -> (g h) p n", p=P)

        def load_in(sp, p):
            if p >= 1:
                sp.wait_ge(in_loaded, 16 * p)
            if p >= 2:
                sp.wait_ge(in_split, p - 1)
            sp.dma_start(raw_in[:, p % 2, :], ins[p, :, :]).then_inc(in_loaded, 16)

        def load_out(sp, p):
            if p >= 1:
                sp.wait_ge(out_loaded, 16 * p)
            if p >= 2:
                sp.wait_ge(out_split, p - 1)
            sp.dma_start(raw_out[:, p % 2, :], outs[p, :, :]).then_inc(out_loaded, 16)

        def first_loads(sp):
            load_in(sp, 0)
            sp.dma_start(cos[:, :, :], dram["wide_cos"]).then_inc(tables_loaded, 16)
            sp.dma_start(sin[:, :, :], dram["wide_sin"]).then_inc(tables_loaded, 16)
            if lin:
                sp.dma_start(mask[:, :], dram["window_mask"]).then_inc(tables_loaded, 16)
                sp.dma_start(half_mask[:, :, :], dram["half_mask"]).then_inc(tables_loaded, 16)
            load_out(sp, 0)
            load_in(sp, 1)
            load_out(sp, 1)

        normalise_all(core, name, xT_all, first_loads)
        summed = [Bank(L, "summed0", ["q0", "kv"], ["q0", "kv"], ["q0", "kv", "wo1"], ["wo1", "end_wo1"], ROUNDS),
                  Bank(L, "summed1", ["q1"], ["q1"], ["q1", "wo0"], ["wo0", "end_wo0"], ROUNDS)]
        if lin:
            t0, t1 = ["q0", "qs0"], ["kk", "q1", "qs1"]
            s0, s1 = ["S0", "S2", "G0", "G2"], ["S1", "S3", "G1"]
        else:
            t0, t1 = ["q0"], ["q1"]
            s0, s1 = ["S0", "S2"], ["S1", "S3"]
        turned = [Bank(L, f"turned{k}", t, p + t, p + t, p, ROUNDS)
                  for k, (p, t) in enumerate(((["P0", "P2"], t0), (["P1", "P3"], t1)))]
        scores = [Bank(L, f"scores{k}", x, n + x, n + x, n, ROUNDS) for k, (n, x) in enumerate(((s0, ["k"]), (s1, [])))]
        heads = [L.bank(f"heads{t}") for t in range(TPS)]

        w_in = [L.sb(f"w_in_{part}", [P, 2 * C, QKV], F32R) for part in ("high", "low")]
        w_out = [L.sb(f"w_out_{part}", [P, 2 * GROUP, D], F32R) for part in ("high", "low")]
        xT = [L.sb(f"xT_{part}", [P, C, S], F32R) for part in ("high", "low")]
        qkv = L.sb("qkv", [P, TPS, QKV])
        straight = L.sb("straight", [P, TPS, RN])
        crossed = L.sb("crossed", [P, RN])
        v = L.sb("v", [P, TPS, HD])
        qT = L.sb("qT", [P, TPS, GROUP, P])
        kT = L.sb("kT", [P, S])
        masked = L.sb("masked", [P, 2, SCORE_COLS])
        neg_max = L.sb("neg_max", [P, GROUP, TPS])
        total = L.sb("total", [P, GROUP, TPS])
        r_total = L.sb("r_total", [P, GROUP, TPS])
        probs = L.sb("probs", [P, 2, SCORE_COLS])
        probsT = L.sb("probsT", [P, 2, SCORE_COLS])
        outT = [L.sb(f"outT_{part}", [P, TPS, GROUP, P], F32R)
                for part in (("high",) if lin else ("high", "low"))]
        if lin:
            out_bf = L.sb("out_bf", [P, TPS, GROUP, P], BF16)
            neg_kq_max = L.sb("neg_kq_max", [P, TPS, GROUP + 1])
            kq_total = L.sb("kq_total", [P, TPS, GROUP + 1])
            r_kq_total = L.sb("r_kq_total", [P, TPS, GROUP + 1])
            r_half_k_total = L.sb("r_half_k_total", [P, TPS])
            kq_exp = L.sb("kq_exp", [P, TPS, RN])
            shifted_k = L.sb("shifted_k", [P, TPS, HD])
            kk = L.sb("kk", [P, 2, S])
            min_k = L.sb("min_k", [P, S])
            neg_abs_k = L.sb("neg_abs_k", [P, S])
            exp_abs_k = L.sb("exp_abs_k", [P, S])
            soft = L.sb("soft", [P, S])
            G = L.sb("G", [P, S])
            R = L.sb("R", [P, NB])
            key_log = L.sb("key_log", [P, S])
            decay_log = L.sb("decay_log", [P, S])
            decay = L.sb("decay", [P, S])
            qf = L.sb("qf", [P, GROUP, S])
            kf = [L.sb(f"kf{n}", [P, BPT, P]) for n in range(3)]
            A = [L.sb(f"A{n}", [P, BPT, GROUP * BLK]) for n in range(3)]

        in_high_ready = L.sem("in_high_ready")
        out_high_ready = L.sem("out_high_ready")
        xT_high_ready = L.sem("xT_high_ready")
        heads_high_ready = L.sem("heads_high_ready")
        kT_ready = L.sem("kT_ready")
        heads_emptied = L.sem("heads_emptied")
        xT_ready = L.sem("xT_ready")
        v_ready = L.sem("v_ready")
        rope_parts = L.sem("rope_parts")
        rope_ready = L.sem("rope_ready")
        exp_ready = L.sem("exp_ready")
        r_total_ready = L.sem("r_total_ready")
        probs_scaled = L.sem("probs_scaled")
        masked_ready = L.sem("masked_ready")
        pv_done = L.sem("pv_done")
        out_f32 = L.sem("out_f32")
        if lin:
            zeroed = L.sem("zeroed")
            max_ready = L.sem("kq_max_ready")
            kq_exp_ready = L.sem("kq_exp_ready")
            r_kq_ready = L.sem("r_kq_ready")
            r_half_ready = L.sem("r_half_ready")
            shifted_ready = L.sem("shifted_ready")
            qs_ready = L.sem("qs_ready")
            min_ready = L.sem("min_ready")
            abs_ready = L.sem("abs_ready")
            exp_abs_ready = L.sem("exp_abs_ready")
            soft_ready = L.sem("soft_ready")
            G_ready = L.sem("G_ready")
            R_ready = L.sem("R_ready")
            decay_log_ready = L.sem("decay_log_ready")
            decay_ready = L.sem("decay_ready")
            kf_ready = L.sem("kf_ready")
            linear_kept = [L.sem(f"linear_kept{k}") for k in range(2)]
            linear_done = L.sem("linear_done")
        block = ctx.enter_context(nc.Block())

        def wait_heads(eng, u):
            if lin:
                eng.wait_ge(linear_done, u + 1)
            else:
                eng.wait_ge(pv_done, GROUP * (u + 1))

        def wait_projected(eng, step):
            summed[0].wait_full(eng, step, "wo1")

        @block.sync
        def _(sp):
            for p in range(2, IN_AHEAD):
                load_in(sp, p)
            for p in range(2, OUT_AHEAD):
                load_out(sp, p)
            if following:
                following.load(sp)
            with sp.Fori(0, ROUNDS) as u:
                sp.wait_ge(in_loaded, 16 * (u + IN_AHEAD))
                core.carry_wait(sp)
                sp.wait_ge(in_split, u + IN_AHEAD - 1)
                core.carry_wait(sp)
                sp.dma_start(raw_in[:, (u + IN_AHEAD) % 2, :], ins[(u + IN_AHEAD) % CHUNKS, :, :])\
                    .then_inc(in_loaded, 16)
                sp.wait_ge(out_loaded, 16 * (u + OUT_AHEAD))
                core.carry_wait(sp)
                sp.wait_ge(out_split, u + OUT_AHEAD - 1)
                core.carry_wait(sp)
                sp.dma_start(raw_out[:, (u + OUT_AHEAD) % 2, :], outs[(u + OUT_AHEAD) % CHUNKS, :, :])\
                    .then_inc(out_loaded, 16)

        tables = 16 * (4 if lin else 2)

        @block.gpsimd
        def _(pool):
            if lin:
                for n in (0, 2):
                    nc.gpsimd.memset(kf[n][:, :, :], 0.0).then_inc(zeroed, 1)

            def copy_v(step, u):
                summed[0].wait_empty(pool, step, "kv")
                core.carry_wait(pool)
                nc.gpsimd.tensor_copy(v[:, :, :], qkv[:, :, RN:QKV]).then_inc(v_ready, 1)

            def round_out(step, u):
                for t in range(TPS):
                    pool.wait_ge(heads_emptied, 1 + TPS * u + t + 1)
                    if t == 0 and step[0] != "first":
                        wait_projected(pool, step)
                    core.carry_wait(pool)
                    nc.gpsimd.tensor_copy(outT[0][:, t, :, :], out_bf[:, t, :, :]).then_inc(out_f32, 1)

            if lin:
                pool.sem_inc(out_f32, 1)
            copy_v(("lead", 0), 0)

            def advance(step, u):
                summed[0].wait_full(pool, step, "q0")
                pool.wait_ge(in_loaded, 16 * (u + IN_AHEAD + 1))
                pool.wait_ge(out_loaded, 16 * (u + OUT_AHEAD + 1))
                core.carry_wait(pool)
                p = u + IN_AHEAD
                nc.gpsimd.tensor_copy(w_in[0][:, p % (2 * C), :], raw_in[:, p % 2, :]).then_inc(in_high_ready, 1)
                p = u + OUT_AHEAD
                nc.gpsimd.tensor_copy(w_out[0][:, p % (2 * GROUP), :], raw_out[:, p % 2, :])\
                    .then_inc(out_high_ready, 1)
                wait_heads(pool, u)
                copy_v(step, u + 1)
                if lin:
                    round_out(step, u)

            advance(("first", 0), 0)
            with pool.Fori(1, ROUNDS) as u:
                advance(("body", u), u)
            if lin:
                round_out(("last", 0), ROUNDS)

        @block.vector
        def _(dve):
            dve.wait_ge(tables_loaded, tables)

            def rope(w):
                for t in range(TPS):
                    heads_of = qkv[:, t, 0:RN].rearrange("p (h d) -> p h d", d=HD)
                    nc.vector.tensor_tensor(straight[:, t, :].rearrange("p (h d) -> p h d", d=HD), heads_of,
                                            cos[:, t, :].unsqueeze(1).to_broadcast([P, GROUP + 1, HD]), ALU.mult)\
                        .then_inc(rope_parts, 1)
                    if t > 0:
                        dve.wait_ge(rope_ready, TPS * w + t)
                    src = qkv[:, t, 0:RN].rearrange("p (h e d) -> p h e d", e=2, d=HD // 2)
                    dst = crossed.rearrange("p (h e d) -> p h e d", e=2, d=HD // 2)
                    sn = sin[:, t, :].rearrange("p (e d) -> p e d", e=2)
                    for e in range(2):
                        nc.vector.tensor_tensor(dst[:, :, e, :], src[:, :, 1 - e, :],
                                                sn[:, e, :].unsqueeze(1).to_broadcast([P, GROUP + 1, HD // 2]),
                                                ALU.mult).then_inc(rope_parts, 1)
                    dve.wait_ge(rope_parts, 3 * (TPS * w + t + 1))
                    nc.vector.tensor_tensor(straight[:, t, :], straight[:, t, :], crossed[:, :], ALU.add)\
                        .then_inc(rope_ready, 1)

            def split_xT(w, b):
                dve.wait_ge(xT_high_ready, w + 1)
                nc.vector.tensor_tensor(xT[1][:, :, :], xT_all[:, b, :, :], xT[0].bitcast(F32)[:, :, :],
                                        ALU.subtract).then_inc(xT_ready, 1)

            def split_in(p):
                dve.wait_ge(in_high_ready, p + 1)
                k = p % (2 * C)
                nc.vector.tensor_tensor(w_in[1][:, k, :], raw_in[:, p % 2, :], w_in[0].bitcast(F32)[:, k, :],
                                        ALU.subtract).then_inc(in_split, 1)

            def split_out(p):
                dve.wait_ge(out_high_ready, p + 1)
                k = p % (2 * GROUP)
                nc.vector.tensor_tensor(w_out[1][:, k, :], raw_out[:, p % 2, :], w_out[0].bitcast(F32)[:, k, :],
                                        ALU.subtract).then_inc(out_split, 1)

            def split_heads(u):
                for t in range(TPS):
                    dve.wait_ge(heads_high_ready, TPS * u + t + 1)
                    nc.vector.tensor_tensor(outT[1][:, t, :, :], heads[t].rearrange("p (h n) -> p h n", h=GROUP),
                                            outT[0].bitcast(F32)[:, t, :, :], ALU.subtract)\
                        .then_inc(heads_emptied, 1)

            def prepare(step, w):
                summed[0].wait_empty(dve, step, "q0")
                summed[1].wait_empty(dve, step, "q1")
                summed[0].wait_empty(dve, step, "kv")
                if lin:
                    for t in range(TPS):
                        nc.vector.tensor_reduce(neg_kq_max[:, t, :],
                                                qkv[:, t, 0:RN].rearrange("p (h d) -> p h d", d=HD),
                                                AX.X, ALU.max, negate=True).then_inc(max_ready, 1)
                    for t in range(TPS):
                        dve.wait_ge(max_ready, TPS * w + t + 1)
                        nc.vector.tensor_scalar(shifted_k[:, t, :], qkv[:, t, QN:RN],
                                                neg_kq_max[:, t, GROUP:GROUP + 1], None, ALU.add)\
                            .then_inc(shifted_ready, 1)
                    if step[0] != "lead":
                        keep_linear(step, 2)
                rope(w)
                if lin:
                    turned[1].wait_empty(dve, step, "kk")
                    nc.vector.tensor_scalar(min_k[:, :], kk[:, 0, :], 0.0, None, ALU.min).then_inc(min_ready, 1)
                    dve.wait_ge(min_ready, w + 1)
                    nc.vector.scalar_tensor_tensor(neg_abs_k[:, :], min_k[:, :], 2.0, kk[:, 0, :], ALU.mult,
                                                   ALU.subtract).then_inc(abs_ready, 1)

            def normalise_q(step, w):
                dve.wait_ge(kq_exp_ready, TPS * (GROUP + 1) * (w + 1))
                if step[0] != "lead":
                    dve.wait_ge(linear_kept[0], 2 * w)
                    dve.wait_ge(linear_kept[1], w)
                nc.vector.reciprocal(r_kq_total[:, :, :], kq_total[:, :, :]).then_inc(r_kq_ready, 1)
                dve.wait_ge(r_kq_ready, w + 1)
                nc.vector.tensor_scalar(r_half_k_total[:, :], r_kq_total[:, :, GROUP], 0.5, None, ALU.mult)\
                    .then_inc(r_half_ready, 1)
                for t in range(TPS):
                    nc.vector.tensor_tensor(kq_exp[:, t, 0:QN].rearrange("p (h d) -> p h d", d=HD),
                                            kq_exp[:, t, 0:QN].rearrange("p (h d) -> p h d", d=HD),
                                            r_kq_total[:, t, 0:GROUP].unsqueeze(2).to_broadcast([P, GROUP, HD]),
                                            ALU.mult).then_inc(qs_ready, 1)

            def decays(step, w):
                if step[0] != "lead":
                    dve.wait_ge(kf_ready, 3 * BPT * w)
                dve.wait_ge(soft_ready, w + 1)
                nc.vector.tensor_tensor_scan(G[:, :], min_k[:, :], soft[:, :], 0.0, ALU.add, ALU.subtract)\
                    .then_inc(G_ready, 1)
                dve.wait_ge(G_ready, w + 1)
                nc.vector.tensor_scalar(R[:, :], G[:, BLK // 2 - 1:S:BLK], 1.0 / 16, None, ALU.mult)\
                    .then_inc(R_ready, 1)
                nc.vector.scalar_tensor_tensor(key_log[:, :], G[:, :], -1.0 / 16, kk[:, 1, :], ALU.mult, ALU.add)\
                    .then_inc(R_ready, 1)
                nc.vector.tensor_tensor(decay_log[:, :].rearrange("p (n s) -> p n s", s=BLK),
                                        G[:, :].rearrange("p (n s) -> p n s", s=BLK),
                                        G[:, BLK // 2 - 1:S:BLK].unsqueeze(2).to_broadcast([P, NB, BLK]),
                                        ALU.subtract).then_inc(decay_log_ready, 1)

            def decayed_queries(step, w):
                dve.wait_ge(decay_ready, w + 1)
                for t in range(TPS):
                    turned[t].wait_full(dve, step, f"qs{t}")
                    nc.vector.tensor_tensor(qf[:, :, t * P:(t + 1) * P],
                                            turned[t].tile.rearrange("p (h n) -> p h n", h=GROUP),
                                            decay[:, t * P:(t + 1) * P].unsqueeze(1).to_broadcast([P, GROUP, P]),
                                            ALU.mult).then_inc(turned[t].emptied, 1)

            def mask_scores(step, u, h):
                k = h % 2
                scores[k].wait_full(dve, step, f"S{h}")
                core.carry_wait(dve)
                if h >= 2:
                    dve.wait_ge(exp_ready, TPS * (GROUP * u + h - 1))
                    core.carry_wait(dve)
                for t in range(TPS):
                    ins = nc.vector.tensor_tensor_reduce(masked[:, k, SPAN[t]], scores[k].tile[:, SPAN[t]],
                                                         mask[:, SPAN[t]], 1.0, 3e38, ALU.add, ALU.min,
                                                         neg_max[:, h, t:t + 1])
                    ins.then_inc(masked_ready, 1)

            def scale_probs(u, h):
                k = h % 2
                dve.wait_ge(exp_ready, TPS * (GROUP * u + h + 1))
                nc.vector.reciprocal(r_total[:, h, :], total[:, h, :]).then_inc(r_total_ready, 1)
                dve.wait_ge(r_total_ready, GROUP * u + h + 1)
                for t in range(TPS):
                    nc.vector.tensor_scalar(probs[:, k, SPAN[t]], probs[:, k, SPAN[t]], r_total[:, h, t:t + 1],
                                            0.5 if lin else 1.0, ALU.mult, ALU.mult).then_inc(probs_scaled, 1)

            def keep_linear(step, n):
                k = scores[n % 2]
                k.wait_full(dve, step, f"G{n}")
                nc.vector.scalar_tensor_tensor(A[n][:, :, :], k.tile.rearrange("p (i m) -> p i m", i=BPT),
                                               r_kq_total[:, n // 2, GROUP:GROUP + 1], half_mask[:, :, :],
                                               ALU.mult, ALU.mult).then_inc(linear_kept[0], 1)

            def attend(step, u, more):
                mask_scores(step, u, 0)
                mask_scores(step, u, 1)
                if lin:
                    decayed_queries(("lead", 0) if step[0] == "first" else ("body", u - 1), u)
                elif step[0] != "first":
                    split_heads(u - 1)
                for h in range(GROUP):
                    scale_probs(u, h)
                    if h == 2 and more:
                        split_in(u + IN_AHEAD)
                        split_out(u + OUT_AHEAD)
                    if h + 2 < GROUP:
                        mask_scores(step, u, h + 2)
                if lin:
                    keep_linear(step, 0)

            def add_out(step, b, end=""):
                for t in range(TPS):
                    k = summed[1 - t]
                    k.wait_full(dve, step, f"{end}wo{t}")
                    nc.vector.tensor_tensor(X[:, TPS * b + t, :], X[:, TPS * b + t, :], k.tile[:, :], ALU.add)\
                        .then_inc(k.emptied, 1)

            def advance(step, u, more=True, out=True):
                attend(step, u, more)
                if more:
                    split_xT(u + 2, (u + 2) % B)
                    prepare(step, u + 1)
                elif lin:
                    keep_linear(step, 2)
                if lin and more:
                    normalise_q(step, u + 1)
                if out:
                    add_out(step, (u + B - 1) % B)
                if lin and more:
                    decays(step, u + 1)

            split_xT(0, 0)
            for p in range(IN_AHEAD):
                split_in(p)
                if p == C - 1:
                    split_xT(1, 1)
                    prepare(("lead", 0), 0)
            for p in range(OUT_AHEAD):
                split_out(p)
            if lin:
                normalise_q(("lead", 0), 0)
                decays(("lead", 0), 0)
            advance(("first", 0), 0, out=False)
            with dve.Fori(1, ROUNDS) as u:
                advance(("body", u), u)
            advance(("last", 0), ROUNDS, more=False)
            if not lin:
                split_heads(ROUNDS)
            add_out(("last", 0), ROUNDS % B, "end_")

        @block.scalar
        def _(act):
            def take_q(step, w, t):
                k = summed[t]
                k.wait_full(act, step, f"q{t}")
                if w is not None:
                    act.wait_ge(rope_ready, TPS * w)
                    if lin:
                        act.wait_ge(kq_exp_ready, TPS * (GROUP + 1) * w)
                nc.scalar.copy(qkv[:, t, 0:QN], k.tile[:, :]).then_inc(k.emptied, 1)

            def take_kv(step, w):
                summed[0].wait_full(act, step, "kv")
                if w is not None:
                    act.wait_ge(v_ready, w)
                    if lin:
                        act.wait_ge(shifted_ready, TPS * w)
                nc.scalar.copy(qkv[:, :, QN:QKV], summed[0].tile.rearrange("p (t n) -> p t n", t=TPS))\
                    .then_inc(summed[0].emptied, 1)

            def take_xT(w, b):
                nc.scalar.copy(xT[0][:, :, :], xT_all[:, b, :, :]).then_inc(xT_high_ready, 1)

            def high_in(p):
                act.wait_ge(in_loaded, 16 * (p + 1))
                nc.scalar.copy(w_in[0][:, p, :], raw_in[:, p % 2, :]).then_inc(in_high_ready, 1)

            def high_out(p):
                act.wait_ge(out_loaded, 16 * (p + 1))
                nc.scalar.copy(w_out[0][:, p, :], raw_out[:, p % 2, :]).then_inc(out_high_ready, 1)

            def softmax_qk(step, w):
                if step[0] != "lead":
                    before = ("lead", 0) if step[0] == "first" else ("body", w - 2)
                    turned[0].wait_full(act, before, "qs0")
                    turned[1].wait_full(act, before, "qs1")
                for t in range(TPS):
                    act.wait_ge(max_ready, TPS * w + t + 1)
                    for h in reversed(range(GROUP + 1)):
                        cols = slice(HD * h, HD * (h + 1))
                        nc.scalar.activation(kq_exp[:, t, cols], qkv[:, t, cols], ACT.Exp,
                                             bias=neg_kq_max[:, t, h:h + 1], accum_out=kq_total[:, t, h:h + 1])\
                            .then_inc(kq_exp_ready, 1)
                    if t == 0:
                        turned[1].wait_full(act, step, "kk")
                        nc.scalar.copy(kk[:, :, :], turned[1].tile.rearrange("p (a n) -> p a n", a=2))\
                            .then_inc(turned[1].emptied, 1)

            def turn_in(step, w):
                def take_q_turned(t):
                    turned[t].wait_full(act, step, f"q{t}")
                    nc.scalar.copy(qT[:, t, :, :], turned[t].tile.rearrange("p (h n) -> p h n", h=GROUP))\
                        .then_inc(turned[t].emptied, 1)

                take_q_turned(0)
                scores[0].wait_full(act, step, "k")
                nc.scalar.mul(kT[:, :], scores[0].tile[:, 0:S], -float(HD) ** -0.5).then_inc(kT_ready, 1)
                take_q_turned(1)
                if lin:
                    act.wait_ge(abs_ready, w + 1)
                    nc.scalar.activation(exp_abs_k[:, :], neg_abs_k[:, :], ACT.Exp).then_inc(exp_abs_ready, 1)
                    act.wait_ge(exp_abs_ready, w + 1)
                    nc.scalar.activation(soft[:, :], exp_abs_k[:, :], ACT.Ln, bias=core.one[:, 0:1])\
                        .then_inc(soft_ready, 1)
                if lin:
                    act.wait_ge(decay_log_ready, w + 1)
                    nc.scalar.activation(decay[:, :], decay_log[:, :], ACT.Exp, scale=1.0 / 16)\
                        .then_inc(decay_ready, 1)

            def decayed_keys(u, n):
                block0, key0 = ((0, 0), (BPT, 0), (BPT, P))[n]
                if n == 0:
                    act.wait_ge(R_ready, 2 * (u + 1))
                    act.wait_ge(zeroed, 2)
                for i in range(BPT):
                    cols = P if n == 1 else BLK * (i + 1)
                    nc.scalar.activation(kf[n][:, i, 0:cols], key_log[:, key0:key0 + cols], ACT.Exp,
                                         bias=R[:, block0 + i:block0 + i + 1]).then_inc(kf_ready, 1)

            def exponentials(u, h):
                k = h % 2
                for t in range(TPS):
                    act.wait_ge(masked_ready, TPS * (GROUP * u + h) + t + 1)
                    nc.scalar.activation(probs[:, k, SPAN[t]], masked[:, k, SPAN[t]], ACT.Exp,
                                         bias=neg_max[:, h, t:t + 1], scale=-1.0,
                                         accum_out=total[:, h, t:t + 1]).then_inc(exp_ready, 1)

            def take_probsT(step, u, h):
                k = h % 2
                turned[k].wait_full(act, step, f"P{h}")
                if h >= 2:
                    act.wait_ge(pv_done, GROUP * u + h - 1)
                nc.scalar.copy(probsT[:, k, :], turned[k].tile[:, 0:SCORE_COLS]).then_inc(turned[k].emptied, 1)

            def take_out(step, u):
                wait_heads(act, u)
                if lin:
                    act.wait_ge(out_f32, 1 + TPS * u)
                elif step[0] != "first":
                    wait_projected(act, step)
                for t in range(TPS):
                    nc.scalar.copy((out_bf if lin else outT[0])[:, t, :, :],
                                   heads[t].rearrange("p (h n) -> p h n", h=GROUP))\
                        .then_inc(heads_emptied if lin else heads_high_ready, 1)

            def attend(step, u, more):
                exponentials(u, 0)
                exponentials(u, 1)
                if more:
                    take_q(step, u + 1, 0)
                if lin:
                    decayed_keys(u, 0)
                if more:
                    take_q(step, u + 1, 1)
                take_probsT(step, u, 0)
                exponentials(u, 2)
                take_probsT(step, u, 1)
                exponentials(u, 3)
                if lin:
                    decayed_keys(u, 1)
                if more:
                    take_kv(step, u + 1)
                    take_xT(u + 2, (u + 2) % B)
                take_probsT(step, u, 2)
                if lin:
                    decayed_keys(u, 2)
                take_probsT(step, u, 3)
                if lin:
                    scores[1].wait_full(act, step, "G1")
                    act.wait_ge(r_half_ready, u + 1)
                    nc.scalar.mul(A[1][:, :, :], scores[1].tile.rearrange("p (i m) -> p i m", i=BPT),
                                  r_half_k_total[:, 0:1]).then_inc(linear_kept[1], 1)
                    if more:
                        softmax_qk(step, u + 1)
                    take_out(step, u)
                if more:
                    turn_in(step, u + 1)
                if not lin:
                    take_out(step, u)

            lead = ("lead", 0)
            take_xT(0, 0)
            for p in range(C):
                high_in(p)
            take_q(lead, None, 0)
            take_q(lead, None, 1)
            take_kv(lead, None)
            take_xT(1, 1)
            if lin:
                softmax_qk(lead, 0)
            for p in range(C, IN_AHEAD):
                high_in(p)
            for p in range(OUT_AHEAD):
                high_out(p)
            turn_in(lead, 0)
            attend(("first", 0), 0, True)
            with act.Fori(1, ROUNDS) as u:
                attend(("body", u), u, True)
            attend(("last", 0), ROUNDS, False)

        @block.tensor
        def _(pe):
            def weights(w):
                return w // B % 2 * C

            def project_q(step, w, g2, t):
                k = summed[t]
                if t == 0:
                    pe.wait_ge(xT_ready, w + 1)
                    pe.wait_ge(in_split, C * (w // B + 1))
                k.wait_free(pe, step, f"q{t}")
                for c in range(C):
                    last = split_matmul(nc, k.tile[:, :], [x[:, c, t * P:(t + 1) * P] for x in xT],
                                        [w_[:, g2 + c, 0:QN] for w_ in w_in], c == 0, c == C - 1)
                last.then_inc(k.filled, 1)

            def project_kv(step, w, g2):
                k = summed[0]
                k.wait_free(pe, step, "kv")
                for t in range(TPS):
                    for c in range(C):
                        last = split_matmul(nc, k.tile[:, t * 2 * HD:(t + 1) * 2 * HD],
                                            [x[:, c, t * P:(t + 1) * P] for x in xT],
                                            [w_[:, g2 + c, QN:QKV] for w_ in w_in], c == 0, c == C - 1)
                last.then_inc(k.filled, 1)

            def turn_kk(step, w):
                turned[1].wait_free(pe, step, "kk")
                pe.wait_ge(shifted_ready, TPS * (w + 1))
                for a in range(2):
                    for t in range(TPS):
                        src = qkv[:, t, QN:RN] if a == 0 else shifted_k[:, t, :]
                        last = nc.tensor.transpose(turned[1].tile[:, a * S + t * P:a * S + (t + 1) * P],
                                                   src, ident[:, :])
                last.then_inc(turned[1].filled, 1)

            def turn_in(step, w):
                for t in range(TPS):
                    pe.wait_ge(rope_ready, TPS * w + t + 1)
                    turned[t].wait_free(pe, step, f"q{t}")
                    for h in range(GROUP):
                        last = nc.tensor.transpose(turned[t].tile[:, h * P:(h + 1) * P],
                                                   straight[:, t, h * HD:(h + 1) * HD], ident[:, :])
                    last.then_inc(turned[t].filled, 1)
                    if t == 0:
                        pe.wait_ge(rope_ready, TPS * (w + 1))
                        if lin and step[0] != "lead":
                            pe.wait_ge(linear_kept[0], 2 * w)
                        for k in range(TPS):
                            last = nc.tensor.transpose(scores[0].tile[:, k * P:(k + 1) * P], straight[:, k, QN:RN],
                                                       ident[:, :])
                        last.then_inc(scores[0].filled, 1)
                if lin:
                    for t in range(TPS):
                        pe.wait_ge(qs_ready, TPS * w + t + 1)
                        turned[t].wait_free(pe, step, f"qs{t}")
                        for h in range(GROUP):
                            last = nc.tensor.transpose(turned[t].tile[:, h * P:(h + 1) * P],
                                                       kq_exp[:, t, h * HD:(h + 1) * HD], ident[:, :])
                        last.then_inc(turned[t].filled, 1)

            def score(step, u, h):
                k = scores[h % 2]
                if h >= 2:
                    pe.wait_ge(masked_ready, TPS * (GROUP * u + h - 1))
                for t in range(TPS):
                    last = nc.tensor.matmul(k.tile[:, SPAN[t]], qT[:, t, h, :], kT[:, 0:(t + 1) * P],
                                            start=True, stop=True)
                last.then_inc(k.filled, 1)

            def turn_probs(step, u, h):
                k = turned[h % 2]
                pe.wait_ge(probs_scaled, TPS * (GROUP * u + h + 1))
                k.wait_free(pe, step, f"P{h}")
                for j in range(SCORE_COLS // P):
                    last = nc.tensor.transpose(k.tile[:, j * P:(j + 1) * P], probs[:, h % 2, j * P:(j + 1) * P],
                                               ident[:, :])
                last.then_inc(k.filled, 1)

            def weigh(step, u, h):
                turned[h % 2].wait_empty(pe, step, f"P{h}")
                pT = probsT[:, h % 2, :]
                if h == 0:
                    pe.wait_ge(v_ready, u + 1)
                    pe.wait_ge(heads_emptied, 1 + TPS * u)
                cols = slice(h * P, (h + 1) * P)
                end = not lin
                nc.tensor.matmul(heads[0][:, cols], v[:, 0, :], pT[:, 0:P], start=(h == 0), stop=end,
                                 skip_group_check=True)
                nc.tensor.matmul(heads[1][:, cols], v[:, 0, :], pT[:, P:2 * P], start=(h == 0), stop=False,
                                 skip_group_check=True)
                nc.tensor.matmul(heads[1][:, cols], v[:, 1, :], pT[:, 2 * P:3 * P], start=False, stop=end,
                                 skip_group_check=True).then_inc(pv_done, 1)

            def linear_scores(step, u, n):
                k = scores[n % 2]
                pe.wait_ge(kf_ready, BPT * (3 * u + n + 1))
                if n == 0:
                    pe.wait_ge(masked_ready, TPS * (GROUP * u + 3))
                elif n == 1:
                    pe.wait_ge(masked_ready, TPS * (GROUP * u + 4))
                else:
                    pe.wait_ge(linear_kept[0], 2 * u + 1)
                block0 = 0 if n == 0 else BPT
                for i in range(BPT):
                    at = BLK * (block0 + i)
                    last = nc.tensor.matmul(k.tile[:, i * P:(i + 1) * P], kf[n][:, i, :], qf[:, :, at:at + BLK],
                                            start=True, stop=True)
                last.then_inc(k.filled, 1)

            def linear_values(u, n):
                pe.wait_ge(linear_kept[n % 2], {0: 2 * u + 1, 1: u + 1, 2: 2 * u + 2}[n])
                out = heads[0 if n == 0 else 1].rearrange("p (h n) -> p h n", h=GROUP)
                for i in range(BPT):
                    last = nc.tensor.matmul(out[:, :, BLK * i:BLK * (i + 1)], v[:, n // 2, :],
                                            A[n][:, i, :].rearrange("p (h s) -> p h s", h=GROUP),
                                            start=False, stop=(n != 1), skip_group_check=True)
                if n == 2:
                    last.then_inc(linear_done, 1)

            def project_out(step, u, tiles, end=""):
                pe.wait_ge(out_split, GROUP * (u // B + 1))
                for t in tiles:
                    k = summed[1 - t]
                    if lin:
                        pe.wait_ge(out_f32, 1 + TPS * u + t + 1)
                    else:
                        pe.wait_ge(heads_emptied, 1 + TPS * u + t + 1)
                    k.wait_free(pe, step, f"{end}wo{t}")
                    for h in range(GROUP):
                        last = split_matmul(nc, k.tile[:, :], [o[:, t, h, :] for o in outT],
                                            [w_[:, weights(u) + h, :] for w_ in w_out], h == 0, h == GROUP - 1)
                    last.then_inc(k.filled, 1)

            def attend(step, arrived, u, more=True, out=True):
                g2 = weights(u + 1) if more else None
                turned[0].wait_empty(pe, arrived, "q0")
                turned[1].wait_empty(pe, arrived, "q1")
                pe.wait_ge(kT_ready, u + 1)
                score(step, u, 0)
                score(step, u, 1)
                if more:
                    project_q(step, u + 1, g2, 0)
                score(step, u, 2)
                if more:
                    project_q(step, u + 1, g2, 1)
                score(step, u, 3)
                turn_probs(step, u, 0)
                turn_probs(step, u, 1)
                if more:
                    project_kv(step, u + 1, g2)
                weigh(step, u, 0)
                turn_probs(step, u, 2)
                weigh(step, u, 1)
                if lin:
                    turned[0].wait_empty(pe, arrived, "qs0")
                    turned[1].wait_empty(pe, arrived, "qs1")
                    linear_scores(step, u, 0)
                    linear_scores(step, u, 1)
                turn_probs(step, u, 3)
                if out and not lin:
                    project_out(step, u - 1, [0])
                weigh(step, u, 2)
                if out and not lin:
                    project_out(step, u - 1, [1])
                if lin:
                    linear_scores(step, u, 2)
                weigh(step, u, 3)
                if lin:
                    linear_values(u, 0)
                    linear_values(u, 1)
                    if more:
                        turn_kk(step, u + 1)
                    linear_values(u, 2)
                if out and lin:
                    project_out(step, u - 1, range(TPS))
                if more:
                    turn_in(step, u + 1)

            for k in summed + turned:
                k.open(pe)
            pe.sem_inc(heads_emptied, 1)
            lead = ("lead", 0)
            project_q(lead, 0, 0, 0)
            project_q(lead, 0, 0, 1)
            project_kv(lead, 0, 0)
            if lin:
                turn_kk(lead, 0)
            turn_in(lead, 0)
            attend(("first", 0), lead, 0, out=False)
            with pe.Fori(1, ROUNDS) as u:
                attend(("body", u), ("body", u - 1), u)
            attend(("last", 0), ("body", ROUNDS - 1), ROUNDS, more=False)
            project_out(("last", 0), ROUNDS, range(TPS), "end_")


def routed_ffn(core, weights):
    nc, X, ident = core.nc, core.X, core.ident
    name, mode, rank = weights.name, weights.mode, weights.rank
    E, ER = weights.experts, weights.experts * rank
    RC = E + ER
    bias, logit_bias = weights.bias, weights.logit_bias
    T_USES = 2 * TPS
    R_USES = 2 * TPS if mode == "sequence" else TPS

    with ExitStack() as ctx:
        L = Layer(core, ctx, name)
        turned = Ring(L, "turned", T_USES)
        routed = Ring(L, "routed", R_USES)
        summed = Ring(L, "summed", TPS)
        ln = LayerNorm(L, turned)
        w, w_ra, w_b = weights.w, weights.w_ra, weights.w_b
        if bias:
            b_out = weights.b_out
        if logit_bias:
            b_logit = weights.b_logit
        if mode == "sequence":
            mean_rows = weights.mean_rows
        KEYS = max(8, E)
        logits = L.sb("logits", [P, TPS, KEYS])
        za = L.sb("za", [P, TPS, ER])
        top = L.sb("top", [P, TPS, 8])
        top_at = L.sb("top_at", [P, TPS, 8], U32)
        top_atf = L.sb("top_atf", [P, TPS, 8])
        iota = L.sb("iota", [P, E])
        expd = L.sb("expd", [P, TPS, 8])
        total = L.sb("total", [P, TPS])
        r_total = L.sb("r_total", [P, TPS])
        p2 = L.sb("p2", [P, TPS])
        weight = L.sb("weight", [P, TPS, E])
        weight2 = L.sb("weight2", [P, TPS, E])
        zw = L.sb("zw", [P, TPS, ER])
        zwT = L.sb("zwT", [P, TPS, P])

        weights_loaded, n_loads = weights.loaded, weights.n_loads
        logits_ready = L.sem("logits_ready")
        step = L.sem("routing_step")
        expd_ready = L.sem("expd_ready")
        max_ready = L.sem("max_ready")
        zw_ready = L.sem("zw_ready")
        bias_added = L.sem("bias_added")
        block = ctx.enter_context(nc.Block())

        def apply_weights(dve, t):
            nc.vector.tensor_tensor(zw[:, t, :].rearrange("p (e r) -> p e r", e=E),
                                    za[:, t, :].rearrange("p (e r) -> p e r", e=E),
                                    weight[:, t, :].unsqueeze(2).to_broadcast([P, E, rank]),
                                    ALU.mult).then_inc(zw_ready, 1)

        @block.gpsimd
        def _(pool):
            if bias:
                pool.wait_ge(weights_loaded, 16 * n_loads)
                with pool.Fori(0, B) as b:
                    for t in range(TPS):
                        pool.wait_ge(ln.xn_ready, TPS * b + t + 1)
                        nc.gpsimd.tensor_tensor(X[:, TPS * b + t, :], X[:, TPS * b + t, :], b_out[:, :], ALU.add)\
                            .then_inc(bias_added, 1)

        @block.vector
        def _(dve):
            dve.wait_ge(weights_loaded, 16 * n_loads)
            if mode != "sequence":
                for e in range(E):
                    nc.vector.memset(iota[:, e:e + 1], float(e)).then_inc(step, 1)
                nc.vector.memset(logits[:, :, :], -3e38).then_inc(step, 1)
                base = E + 1
                dve.wait_ge(step, base)
            else:
                base = 0
            ln.vector_all(dve)
            with dve.Fori(0, B) as b:
                count = [0]
                per = {"sequence": 6, "top1": 4 * TPS, "top2": 10 * TPS}[mode]

                def stepped(ins):
                    count[0] += 1
                    ins.then_inc(step, 1)
                    dve.wait_ge(step, base + b * per + count[0])

                ln.normalise(dve, b)
                for t in range(TPS):
                    routed.wait_full(dve, b, t)
                    src = routed.banks[t]
                    if mode == "sequence":
                        nc.vector.tensor_copy(logits[:, t, 0:E], src[:, 0:E]).then_inc(logits_ready, 1)
                    elif mode == "top1":
                        nc.vector.tensor_tensor(logits[:, t, 0:E], src[:, 0:E], b_logit[:, :], ALU.add)\
                            .then_inc(logits_ready, 1)
                    else:
                        nc.vector.tensor_copy(logits[:, t, 0:E], src[:, 0:E]).then_inc(logits_ready, 1)
                    nc.vector.tensor_copy(za[:, t, :], src[:, E:RC]).then_inc(routed.emptied[t], 1)
                if mode == "sequence":
                    n = TPS
                    routed.wait_full(dve, b, n)
                    stepped(nc.vector.tensor_tensor(top[:, 0, 0:E], routed.banks[n % 2][:, 0:E],
                                                    b_logit[:, :], ALU.add))
                    nc.vector.tensor_reduce(total[:, 1:2], top[:, 0, 0:E], AX.X, ALU.max, negate=True)\
                        .then_inc(max_ready, 1)
                    dve.wait_ge(expd_ready, b + 1)
                    stepped(nc.vector.reciprocal(r_total[:, 0:1], total[:, 0:1]))
                    stepped(nc.vector.tensor_scalar(weight[:, 0, :], expd[:, 0, 0:E], r_total[:, 0:1], 2.0,
                                                    ALU.mult, ALU.mult))
                    stepped(nc.vector.tensor_scalar(weight[:, 1, :], expd[:, 0, 0:E], r_total[:, 0:1], 2.0,
                                                    ALU.mult, ALU.mult))
                    routed.wait_full(dve, b, n + 1)
                    nc.vector.tensor_copy(total[:, 1:2], routed.banks[(n + 1) % 2][:, 0:1])\
                        .then_inc(routed.emptied[(n + 1) % 2], 1)
                    nc.vector.tensor_copy(p2[:, 0:1], routed.banks[n % 2][:, 0:1])\
                        .then_inc(routed.emptied[n % 2], 1)
                    for t in range(TPS):
                        apply_weights(dve, t)
                else:
                    for t in range(TPS):
                        dve.wait_ge(logits_ready, TPS * b + t + 1)
                        core.carry_wait(dve)
                        stepped(nc.vector.max(top[:, t, :], logits[:, t, :]))
                        core.carry_wait(dve)
                        stepped(nc.vector.max_index(top_at[:, t, :], top[:, t, :], logits[:, t, :]))
                        stepped(nc.vector.tensor_copy(top_atf[:, t, :], top_at[:, t, :]))
                        if mode == "top1":
                            stepped(nc.vector.tensor_scalar(weight[:, t, :], iota[:, :], top_atf[:, t, 0:1],
                                                            None, ALU.is_equal))
                        else:
                            stepped(nc.vector.tensor_tensor(expd[:, t, 0:1], top[:, t, 1:2], top[:, t, 0:1],
                                                            ALU.subtract))
                            nc.vector.tensor_copy(expd[:, t, 2:3], expd[:, t, 0:1]).then_inc(max_ready, 1)
                            dve.wait_ge(expd_ready, TPS * b + t + 1)
                            stepped(nc.vector.tensor_scalar(total[:, t:t + 1], expd[:, t, 1:2], 1.0, None, ALU.add))
                            stepped(nc.vector.reciprocal(r_total[:, t:t + 1], total[:, t:t + 1]))
                            stepped(nc.vector.tensor_scalar(p2[:, t:t + 1], expd[:, t, 1:2], r_total[:, t:t + 1],
                                                            2.0, ALU.mult, ALU.mult))
                            stepped(nc.vector.tensor_scalar(weight[:, t, :], iota[:, :], top_atf[:, t, 0:1],
                                                            r_total[:, t:t + 1], ALU.is_equal, ALU.mult))
                            stepped(nc.vector.tensor_scalar(weight2[:, t, :], iota[:, :], top_atf[:, t, 1:2],
                                                            p2[:, t:t + 1], ALU.is_equal, ALU.mult))
                            stepped(nc.vector.scalar_tensor_tensor(weight[:, t, :], weight[:, t, :], 2.0,
                                                                   weight2[:, t, :], ALU.mult, ALU.add))
                        apply_weights(dve, t)
                assert count[0] <= per
                while count[0] < per:
                    stepped(nc.vector.memset(top_atf[:, 0, 7:8], 0.0))
                if bias:
                    dve.wait_ge(bias_added, TPS * (b + 1))
                for t in range(TPS):
                    summed.wait_full(dve, b, t)
                    nc.vector.tensor_tensor(X[:, TPS * b + t, :], X[:, TPS * b + t, :], summed.banks[t][:, :],
                                            ALU.add).then_inc(summed.emptied[t], 1)

        @block.scalar
        def _(act):
            ln.scalar_all(act)
            with act.Fori(0, B) as b:
                ln.scalar_xT(act, b)
                if mode == "sequence":
                    act.wait_ge(max_ready, b + 1)
                    nc.scalar.activation(expd[:, 0, 0:E], top[:, 0, 0:E], ACT.Exp, bias=total[:, 1:2],
                                         accum_out=total[:, 0:1]).then_inc(expd_ready, 1)
                elif mode == "top2":
                    for t in range(TPS):
                        act.wait_ge(max_ready, TPS * b + t + 1)
                        nc.scalar.activation(expd[:, t, 1:2], expd[:, t, 2:3], ACT.Exp).then_inc(expd_ready, 1)
                for t in range(TPS):
                    n = TPS + t
                    turned.wait_full(act, b, n)
                    nc.scalar.copy(zwT[0:ER, t, :], turned.banks[n % 2][0:ER, 0:P])\
                        .then_inc(turned.emptied[n % 2], 1)

        @block.tensor
        def _(pe):
            pe.wait_ge(weights_loaded, 16 * n_loads)
            for ring in (turned, routed, summed):
                ring.open(pe)
            with pe.Fori(0, B) as b:
                ln.tensor(pe, b)
                for t in range(TPS):
                    ln.wait_xT(pe, b, t)
                    routed.wait_free(pe, b, t)
                    for c in range(C):
                        last = nc.tensor.matmul(routed.banks[t][:, 0:RC], ln.xT[:, c, t * P:(t + 1) * P],
                                                w_ra[:, c, :], start=(c == 0), stop=(c == C - 1))
                    last.then_inc(routed.filled[t], 1)
                for t in range(TPS):
                    summed.wait_free(pe, b, t)
                    for c in range(C):
                        nc.tensor.matmul(summed.banks[t][:, :], ln.xT[:, c, t * P:(t + 1) * P], w[:, c, :],
                                         start=(c == 0), stop=False)
                if mode == "sequence":
                    pe.wait_ge(logits_ready, TPS * (b + 1))
                    for k in range(2):
                        n = TPS + k
                        routed.wait_free(pe, b, n)
                        for t in range(TPS):
                            last = nc.tensor.matmul(routed.banks[n % 2][:, 0:E], mean_rows[:, t, :],
                                                    logits[:, t, 0:E], start=(t == 0), stop=(t == TPS - 1))
                        last.then_inc(routed.filled[n % 2], 1)
                for t in range(TPS):
                    n = TPS + t
                    pe.wait_ge(zw_ready, TPS * b + t + 1)
                    turned.wait_free(pe, b, n)
                    nc.tensor.transpose(turned.banks[n % 2][0:ER, 0:P], zw[:, t, :], ident[:, :])\
                        .then_inc(turned.filled[n % 2], 1)
                for t in range(TPS):
                    n = TPS + t
                    turned.wait_empty(pe, b, n)
                    nc.tensor.matmul(summed.banks[t][:, :], zwT[0:ER, t, :], w_b[:, :], start=False, stop=True)\
                        .then_inc(summed.filled[t], 1)


def gated_ffn(core, name, following):
    nc, dram, X = core.nc, core.dram, core.X
    H, RANK = 1376, 16
    HT = -(-H // P)
    ROWS = [min(P, H - P * j) for j in range(HT)]
    LOW = 2 * RANK
    S_USES = 1 + HT

    with ExitStack() as ctx:
        L = Layer(core, ctx, name)
        turned = Ring(L, "turned", TPS)
        summed = Ring(L, "summed", S_USES)
        results = Ring(L, "results", TPS)
        low_bank = L.bank("low_bank")
        ln = LayerNorm(L, turned)
        xT_all = L.sb("xT_all", [P, B, C, S])
        w_gate = L.sb("w_gate", [P, C, H])
        w_up = L.sb("w_up", [P, C, H])
        w_down = L.sb("w_down", [P, HT, D])
        a_in = L.sb("a_in", [P, C, LOW])
        b_in = L.sb("b_in", [LOW, 2, H])
        a_down = L.sb("a_down", [P, HT, RANK])
        b_down = L.sb("b_down", [RANK, D])
        low_in = L.sb("low_in", [LOW, S])
        low_down = L.sb("low_down", [RANK, S])
        silu = L.sb("silu", [P, 2, S])
        hidden = L.sb("hidden", [P, HT, S])

        zeroed = L.sem("zeroed")
        in_loaded = L.sem("in_loaded")
        down_loaded = L.sem("down_loaded")
        silu_ready = L.sem("silu_ready")
        low_filled = L.sem("low_filled")
        low_emptied = L.sem("low_emptied")
        block = ctx.enter_context(nc.Block())

        @block.sync
        def _(sp):
            sp.wait_ge(zeroed, 1)
            for a, at in (("gate_a", 0), ("up_a", RANK)):
                sp.dma_start(a_in[:, :, at:at + RANK], dram[f"{name}_{a}"].rearrange("(c p) n -> p c n", p=P),
                             allow_slow_non_contiguous=True).then_inc(in_loaded, 16)
            for k, b in enumerate(("gate_b", "up_b")):
                sp.dma_start(b_in[k * RANK:(k + 1) * RANK, k, :], dram[f"{name}_{b}"]).then_inc(in_loaded, 16)
            for w, k in ((w_gate, "gate_w"), (w_up, "up_w")):
                sp.dma_start(w[:, :, :], dram[f"{name}_{k}"].rearrange("(c p) n -> p c n", p=P)).then_inc(in_loaded, 16)
            full = P * (HT - 1)
            for w, k in ((w_down, "down_w"), (a_down, "down_a")):
                src = dram[f"{name}_{k}"]
                sp.dma_start(w[:, 0:HT - 1, :], src[0:full, :].rearrange("(j p) n -> p j n", p=P),
                             allow_slow_non_contiguous=True).then_inc(down_loaded, 16)
                sp.dma_start(w[0:H - full, HT - 1, :], src[full:H, :]).then_inc(down_loaded, 16)
            sp.dma_start(b_down[:, :], dram[f"{name}_down_b"]).then_inc(down_loaded, 16)
            following.load(sp)

        @block.gpsimd
        def _(pool):
            nc.gpsimd.memset(b_in[:, :, :], 0.0).then_inc(zeroed, 1)

        @block.vector
        def _(dve):
            ln.vector_all(dve)
            with dve.Fori(0, B) as b:
                ln.normalise(dve, b, alone=True)
            with dve.Fori(0, B) as b:
                for j in range(HT):
                    use, rows = 1 + j, slice(0, ROWS[j])
                    dve.wait_ge(silu_ready, HT * b + j + 1)
                    nc.vector.tensor_tensor(hidden[rows, j, :], silu[rows, j % 2, :],
                                            summed.banks[use % 2][rows, S:2 * S], ALU.mult)\
                        .then_inc(summed.emptied[use % 2], 1)
                for t in range(TPS):
                    results.wait_full(dve, b, t)
                    nc.vector.tensor_tensor(X[:, TPS * b + t, :], X[:, TPS * b + t, :], results.banks[t][:, :],
                                            ALU.add).then_inc(results.emptied[t], 1)

        @block.scalar
        def _(act):
            ln.scalar_all(act)
            with act.Fori(0, B) as b:
                ln.scalar_xT(act, b, xT_all[:, b, :, :])
            with act.Fori(0, B) as b:
                summed.wait_full(act, b, 0)
                nc.scalar.copy(low_in[:, :], summed.banks[0][0:LOW, 0:S]).then_inc(summed.emptied[0], 1)
                for j in range(HT):
                    use, rows = 1 + j, slice(0, ROWS[j])
                    summed.wait_full(act, b, use)
                    if j >= 2:
                        summed.wait_empty(act, b, use - 2)
                    nc.scalar.activation(silu[rows, j % 2, :], summed.banks[use % 2][rows, 0:S], ACT.Silu)\
                        .then_inc(silu_ready, 1)
                act.wait_ge(low_filled, b + 1)
                nc.scalar.copy(low_down[:, :], low_bank[0:RANK, 0:S]).then_inc(low_emptied, 1)

        @block.tensor
        def _(pe):
            for ring in (turned, summed, results):
                ring.open(pe)
            with pe.Fori(0, B) as b:
                ln.tensor(pe, b)
            pe.wait_ge(in_loaded, 16 * (2 + 2 + 2))
            with pe.Fori(0, B) as b:
                for t in range(TPS):
                    ln.wait_xT(pe, b, t)
                summed.wait_free(pe, b, 0)
                for c in range(C):
                    last = nc.tensor.matmul(summed.banks[0][0:LOW, 0:S], a_in[:, c, :], xT_all[:, b, c, :],
                                            start=(c == 0), stop=(c == C - 1))
                last.then_inc(summed.filled[0], 1)
                for j in range(HT):
                    use, rows = 1 + j, slice(0, ROWS[j])
                    cols = slice(P * j, P * j + ROWS[j])
                    bank = summed.banks[use % 2]
                    summed.wait_free(pe, b, use)
                    for k, (w, half) in enumerate(((w_gate, 0), (w_up, S))):
                        for c in range(C):
                            nc.tensor.matmul(bank[rows, half:half + S], w[:, c, cols], xT_all[:, b, c, :],
                                             start=(c == 0), stop=False)
                        if j == 0 and half == 0:
                            summed.wait_empty(pe, b, 0)
                        last = nc.tensor.matmul(bank[rows, half:half + S], b_in[:, k, cols],
                                                low_in[:, :], start=False, stop=True)
                    last.then_inc(summed.filled[use % 2], 1)
                pe.wait_ge(down_loaded, 16 * 5)
                for j in range(HT):
                    if j in (HT - 2, HT - 1):
                        summed.wait_empty(pe, b, 1 + j)
                    elif j == 0:
                        summed.wait_empty(pe, b, 1 + HT - 3)
                        summed.wait_empty(pe, b, 1 + HT - 4)
                    last = nc.tensor.matmul(low_bank[0:RANK, 0:S], a_down[0:ROWS[j], j, :], hidden[0:ROWS[j], j, :],
                                            start=(j == 0), stop=(j == HT - 1))
                last.then_inc(low_filled, 1)
                for t in range(TPS):
                    results.wait_free(pe, b, t)
                    for j in range(HT):
                        nc.tensor.matmul(results.banks[t][:, :], hidden[0:ROWS[j], j, t * P:(t + 1) * P],
                                         w_down[0:ROWS[j], j, :], start=(j == 0), stop=False)
                    if t == 0:
                        pe.wait_ge(low_emptied, b + 1)
                    nc.tensor.matmul(results.banks[t][:, :], low_down[:, t * P:(t + 1) * P], b_down[:, :],
                                     start=False, stop=True).then_inc(results.filled[t], 1)


def build(nc, dram):
    with ExitStack() as ctx:
        core = Core(nc, ctx, dram)
        with ExitStack() as ffn:
            w_ffn = RoutedWeights(core, ffn, "L0_ffn", 8, 16, "sequence")
            with ExitStack() as attn:
                w_attn = NarrowWeights(core, attn, "L0_attn", rope=True)
                load_constants(core, w_attn)
                narrow_attention(core, w_attn, w_ffn)
            routed_ffn(core, w_ffn)
        wide_attention(core, "L1_attn", linear=True)
        with ExitStack() as ffn:
            w_ffn = RoutedWeights(core, ffn, "L2_ffn", 4, 8, "top1")
            with ExitStack() as attn:
                w_attn = NarrowWeights(core, attn, "L2_attn", rope=False)
                gated_ffn(core, "L1_ffn", w_attn)
                narrow_attention(core, w_attn, w_ffn)
            routed_ffn(core, w_ffn)
        with ExitStack() as ffn:
            w_ffn = RoutedWeights(core, ffn, "L3_ffn", 8, 16, "top2")
            wide_attention(core, "L3_attn", linear=False, following=w_ffn)
            routed_ffn(core, w_ffn)
        store_result(core)


def narrow_tables():
    HD = 16
    inv = (1.0 / 10000.0 ** (np.arange(0, HD, 2, dtype=np.float32) / HD)).astype(np.float32)
    ang = np.arange(S, dtype=np.float32)[:, None] * inv[None, :]
    cos, sin = np.cos(ang).astype(np.float32), np.sin(ang).astype(np.float32)
    return [np.ascontiguousarray(t.reshape(TPS, P, HD).transpose(1, 0, 2))
            for t in (np.repeat(cos, 2, axis=1), np.stack([-sin, sin], axis=-1).reshape(S, HD))]


def wide_tables():
    HD = 128
    inv = (1.0 / 10000.0 ** (np.arange(0, HD, 2, dtype=np.float32) / HD)).astype(np.float32)
    ang = np.arange(S, dtype=np.float32)[:, None] * inv[None, :]
    cos, sin = np.cos(ang).astype(np.float32), np.sin(ang).astype(np.float32)
    return [np.ascontiguousarray(t.reshape(TPS, P, HD).transpose(1, 0, 2))
            for t in (np.concatenate([cos, cos], axis=1), np.concatenate([-sin, sin], axis=1))]


def shape_constants():
    k = {"ident": np.eye(P, dtype=np.float32), "eps": np.full((P, 1), EPS, np.float32),
         "one": np.ones((P, 1), np.float32)}
    q, c = np.arange(P)[:, None], np.arange(P)[None, :]
    tri = np.where(c <= q, 0.0, BIG).astype(np.float32)
    k["mask"] = np.concatenate([tri, np.zeros((P, P), np.float32), tri], axis=1)
    k["wide_cos"], k["wide_sin"] = wide_tables()
    qt, kt = np.arange(S)[:, None], np.arange(S)[None, :]
    window = np.where((kt <= qt) & (qt - kt <= WINDOW), 0.0, BIG).astype(np.float32)
    k["window_mask"] = np.concatenate([window[:P, :P], window[P:, :]], axis=1)
    key, blk, query = np.arange(P)[:, None, None, None], np.arange(4)[:, None, None], np.arange(32)
    half = np.broadcast_to(np.where(key <= 32 * blk + query, 0.5, 0.0), (P, 4, GROUP, 32))
    k["half_mask"] = half.reshape(P, 4, GROUP * 32).astype(np.float32)
    tok = np.arange(S)
    rows = ((tok >= MEAN_FROM) & (tok < MEAN_TO)).astype(np.float32) / np.float32(MEAN_TO - MEAN_FROM)
    k["mean_rows"] = np.repeat(rows.reshape(TPS, P).T[:, :, None], P, axis=2).astype(np.float32)
    k["L0_attn_cos"], k["L0_attn_sin"] = narrow_tables()
    start = 2.0 ** (-2.0 ** (-(np.log2(HEADS) - 3)))
    slopes = np.array([start ** (i + 1) for i in range(HEADS)], dtype=np.float32)
    pos = np.arange(S, dtype=np.float32).reshape(TPS, P).T
    qp = np.zeros((P, TPS, HEADS, 32), np.float32)
    qp[:, :, :, 16] = -slopes
    qp[:, :, :, 17] = slopes * pos[:, :, None]
    kp = np.zeros((P, TPS, 1, 4, 32), np.float32)
    kp[:, :, :, :, 16] = pos[:, :, None, None]
    kp[:, :, :, :, 17] = 1.0
    k["L2_attn_q_pad"], k["L2_attn_k_pad"] = qp, kp
    return k


def by_group(*ws):
    return np.concatenate([w.reshape(D, KV_HEADS, -1).transpose(1, 0, 2) for w in ws], axis=2)


def layouts(i):
    a = {k: np.asarray(v) for k, v in i.items()}
    return {
        "x": a["L0_attn_x"],
        "L0_attn_w_qkv": a["L0_attn_w_qkv"].T, "L0_attn_b_qkv": a["L0_attn_b_qkv"],
        "L0_attn_w_o": a["L0_attn_w_o"].T, "L0_attn_b_o": a["L0_attn_b_o"],
        "L0_ffn_w": a["L0_ffn_W"].T, "L0_ffn_b": a["L0_ffn_b"], "L0_ffn_router": a["L0_ffn_router_W"].T,
        "L0_ffn_router_b": a["L0_ffn_router_b"], "L0_ffn_A": a["L0_ffn_A"].reshape(-1, D).T,
        "L0_ffn_B": a["L0_ffn_B"].transpose(0, 2, 1).reshape(-1, D),
        "L2_attn_w_qkv": np.concatenate([a["L2_attn_Wq"], a["L2_attn_Wkv"]], axis=1),
        "L2_attn_w_o": a["L2_attn_Wo"],
        "L2_ffn_w": a["L2_ffn_W_up"].T, "L2_ffn_router": a["L2_ffn_gate_w"].T,
        "L2_ffn_router_b": a["L2_ffn_expert_bias"], "L2_ffn_A": a["L2_ffn_lora_A"].reshape(-1, D).T,
        "L2_ffn_B": a["L2_ffn_lora_B"].transpose(0, 2, 1).reshape(-1, D),
        "L1_attn_w_in": by_group(a["L1_attn_Wq"], a["L1_attn_Wk"], a["L1_attn_Wv"]),
        "L1_attn_w_o": a["L1_attn_Wo"].reshape(KV_HEADS, -1, D),
        **{f"L1_ffn_{k}": a[f"L1_ffn_{k}"].T for k in ("gate_w", "up_w", "down_w", "gate_a", "gate_b", "up_a",
                                                       "up_b", "down_a", "down_b")},
        "L3_attn_w_in": by_group(a["L3_attn_Wq"], a["L3_attn_Wk"], a["L3_attn_Wv"]),
        "L3_attn_w_o": a["L3_attn_Wo"].reshape(KV_HEADS, -1, D),
        "L3_ffn_w": a["L3_ffn_W_base"].T, "L3_ffn_b": a["L3_ffn_b_base"],
        "L3_ffn_router": a["L3_ffn_W_router"].T, "L3_ffn_A": a["L3_ffn_A"].reshape(-1, D).T,
        "L3_ffn_B": a["L3_ffn_B"].transpose(0, 2, 1).reshape(-1, D),
    }


def kernel(**inputs):
    import concourse.bacc as bacc
    from concourse.bass_utils import run_bass_kernel_spmd

    nc = bacc.Bacc("TRN2", target_bir_lowering=False, num_devices=1)
    arrays, dram = {}, {}
    for name, a in {**layouts(inputs), **shape_constants()}.items():
        arrays[f"in_{name}"] = np.ascontiguousarray(a)
        dram[name] = nc.dram_tensor(f"in_{name}", a.shape, mybir.dt.from_np(a.dtype), kind="ExternalInput").ap()
    dram["out"] = nc.dram_tensor("out_x", (B, S, D), F32, kind="ExternalOutput").ap()
    build(nc, dram)
    r = run_bass_kernel_spmd(nc, [arrays], core_ids=[0])
    return r.results[0]["out_x"]
```
